# Optimizing a Trainium2 kernel written in Bass

```python
import numpy as np
import jax
import jax.numpy as jnp

def _softmax(x, axis=-1):
    return jax.nn.softmax(x, axis=axis)

def _gelu(x):
    return jax.nn.gelu(x, approximate=True)

def _silu(x):
    return jax.nn.silu(x)

def _sigmoid(x):
    return jax.nn.sigmoid(x)

def _layernorm(x, axis=-1, eps=1e-05):
    m = jnp.mean(x, axis=axis, keepdims=True)
    v = jnp.var(x, axis=axis, keepdims=True)
    return (x - m) / jnp.sqrt(v + eps)

def _scatter_add(tgt, idx, src, axis=0):
    return tgt.at[idx].add(src)

def _segment_sum(src, seg, n):
    return jax.ops.segment_sum(src, seg, n)
kernel_name = 'mk_prb_d2_jaxref_r4_72d42e'

def setup_inputs(seed: int=0):
    np.random.seed(seed)
    _w = jnp.asarray

    def _L0_attn_setup():
        import jax, jax.numpy as jnp
        import numpy as np
        key = jax.random.key(seed)
        ks = jax.random.split(key, 7)
        B, P, D = (4, 512, 256)
        s = 1.0 / np.sqrt(D)
        return {'x': jax.random.normal(ks[0], (B, P, D), dtype=jnp.float32), 'Wq': jax.random.normal(ks[1], (D, D), dtype=jnp.float32) * s, 'bq': jnp.zeros((D,), dtype=jnp.float32), 'Wk': jax.random.normal(ks[2], (D, D), dtype=jnp.float32) * s, 'bk': jnp.zeros((D,), dtype=jnp.float32), 'Wv': jax.random.normal(ks[3], (D, D), dtype=jnp.float32) * s, 'bv': jnp.zeros((D,), dtype=jnp.float32)}
    _L0_attn_in = _L0_attn_setup()

    def _L0_ffn_setup():
        import jax, jax.numpy as jnp
        import numpy as np
        B, T, D, H = (4, 512, 256, 512)
        E, S, K = (8, 2, 2)

        def _swiglu_stacked(x, w1, b1, w2, b2, w3, b3):
            p1 = jnp.einsum('btd,ndh->nbth', x, w1) + b1[:, None, None, :]
            p2 = jnp.einsum('btd,ndh->nbth', x, w2) + b2[:, None, None, :]
            glu = jax.nn.silu(p1) * p2
            return jnp.einsum('nbth,nhd->nbtd', glu, w3) + b3[:, None, None, :]
        key = jax.random.key(seed)
        ks = jax.random.split(key, 10)
        s = 0.02
        return {'x': jax.random.normal(ks[0], (B, T, D), jnp.float32), 'gate_w': jax.random.normal(ks[1], (D, E), jnp.float32) * s, 'gate_b': jnp.zeros((E,), jnp.float32), 'rw1': jax.random.normal(ks[2], (E, D, H), jnp.float32) * s, 'rb1': jnp.zeros((E, H), jnp.float32), 'rw2': jax.random.normal(ks[3], (E, D, H), jnp.float32) * s, 'rb2': jnp.zeros((E, H), jnp.float32), 'rw3': jax.random.normal(ks[4], (E, H, D), jnp.float32) * s, 'rb3': jnp.zeros((E, D), jnp.float32), 'sw1': jax.random.normal(ks[5], (S, D, H), jnp.float32) * s, 'sb1': jnp.zeros((S, H), jnp.float32), 'sw2': jax.random.normal(ks[6], (S, D, H), jnp.float32) * s, 'sb2': jnp.zeros((S, H), jnp.float32), 'sw3': jax.random.normal(ks[7], (S, H, D), jnp.float32) * s, 'sb3': jnp.zeros((S, D), jnp.float32)}
    _L0_ffn_in = _L0_ffn_setup()

    def _L1_attn_setup():
        import jax, jax.numpy as jnp
        import numpy as np
        import math
        B, S, D = (8, 512, 256)

        def _trunc_normal(key, shape, fan_in, fan_out):
            std = math.sqrt(2.0 / (fan_in + fan_out))
            return jax.random.truncated_normal(key, -3.0, 3.0, shape, jnp.float32) * std
        key = jax.random.key(seed)
        kx, kq, kk, kv, ko = jax.random.split(key, 5)
        return {'in_features': jax.random.normal(kx, (B, S, D), jnp.float32), 'Wq': _trunc_normal(kq, (D, D), D, D), 'Wk': _trunc_normal(kk, (D, D), D, D), 'Wv': _trunc_normal(kv, (D, D), D, D), 'Wo': _trunc_normal(ko, (D, D), D, D)}
    _L1_attn_in = _L1_attn_setup()

    def _L1_ffn_setup():
        import jax, jax.numpy as jnp
        import numpy as np
        B, S, D, H, F = (4, 1024, 256, 16, 1024)
        CAP = 0.125
        ROPE_BASE = 10000.0

        def rmsnorm(x, g):
            return x * jax.lax.rsqrt(jnp.mean(x * x, -1, keepdims=True) + 1e-06) * g

        def rope(t, pos):
            hd = t.shape[-1]
            inv = 1.0 / ROPE_BASE ** (jnp.arange(0, hd, 2, dtype=jnp.float32) / hd)
            f = pos[:, None, :, None].astype(jnp.float32) * inv
            emb = jnp.concatenate([f, f], axis=-1)
            cos, sin = (jnp.cos(emb), jnp.sin(emb))
            rot = jnp.concatenate([-t[..., hd // 2:], t[..., :hd // 2]], axis=-1)
            return t * cos + rot * sin
        key = jax.random.key(seed)
        ks = jax.random.split(key, 9)
        scale = 0.02
        x = jax.random.normal(ks[0], (B, S, D), jnp.float32)
        causal = jnp.where(jnp.tril(jnp.ones((S, S), bool)), 0.0, -1000000000.0).astype(jnp.float32)
        attention_mask = jnp.broadcast_to(causal[None, None], (B, 1, S, S))
        position_ids = jnp.broadcast_to(jnp.arange(S, dtype=jnp.int32), (B, S))
        return {'x': x, 'attention_mask': attention_mask, 'position_ids': position_ids, 'router_w': jax.random.normal(ks[1], (D, 1), jnp.float32) * scale, 'router_b': jnp.zeros((1,), jnp.float32), 'wq': jax.random.normal(ks[2], (D, D), jnp.float32) * scale, 'wk': jax.random.normal(ks[3], (D, D), jnp.float32) * scale, 'wv': jax.random.normal(ks[4], (D, D), jnp.float32) * scale, 'wo': jax.random.normal(ks[5], (D, D), jnp.float32) * scale, 'w1': jax.random.normal(ks[6], (D, F), jnp.float32) * scale, 'w2': jax.random.normal(ks[7], (F, D), jnp.float32) * scale, 'ln1': jnp.ones((D,), jnp.float32), 'ln2': jnp.ones((D,), jnp.float32)}
    _L1_ffn_in = _L1_ffn_setup()
    _d = {'L0_attn_x': _L0_attn_in['x'], 'L0_attn_Wq': _L0_attn_in['Wq'], 'L0_attn_bq': _L0_attn_in['bq'], 'L0_attn_Wk': _L0_attn_in['Wk'], 'L0_attn_bk': _L0_attn_in['bk'], 'L0_attn_Wv': _L0_attn_in['Wv'], 'L0_attn_bv': _L0_attn_in['bv'], 'L0_ffn_gate_w': _L0_ffn_in['gate_w'], 'L0_ffn_gate_b': _L0_ffn_in['gate_b'], 'L0_ffn_rw1': _L0_ffn_in['rw1'], 'L0_ffn_rb1': _L0_ffn_in['rb1'], 'L0_ffn_rw2': _L0_ffn_in['rw2'], 'L0_ffn_rb2': _L0_ffn_in['rb2'], 'L0_ffn_rw3': _L0_ffn_in['rw3'], 'L0_ffn_rb3': _L0_ffn_in['rb3'], 'L0_ffn_sw1': _L0_ffn_in['sw1'], 'L0_ffn_sb1': _L0_ffn_in['sb1'], 'L0_ffn_sw2': _L0_ffn_in['sw2'], 'L0_ffn_sb2': _L0_ffn_in['sb2'], 'L0_ffn_sw3': _L0_ffn_in['sw3'], 'L0_ffn_sb3': _L0_ffn_in['sb3'], 'L1_attn_Wq': _L1_attn_in['Wq'], 'L1_attn_Wk': _L1_attn_in['Wk'], 'L1_attn_Wv': _L1_attn_in['Wv'], 'L1_attn_Wo': _L1_attn_in['Wo'], 'L1_ffn_attention_mask': _L1_ffn_in['attention_mask'], 'L1_ffn_position_ids': _L1_ffn_in['position_ids'], 'L1_ffn_router_w': _L1_ffn_in['router_w'], 'L1_ffn_router_b': _L1_ffn_in['router_b'], 'L1_ffn_wq': _L1_ffn_in['wq'], 'L1_ffn_wk': _L1_ffn_in['wk'], 'L1_ffn_wv': _L1_ffn_in['wv'], 'L1_ffn_wo': _L1_ffn_in['wo'], 'L1_ffn_w1': _L1_ffn_in['w1'], 'L1_ffn_w2': _L1_ffn_in['w2'], 'L1_ffn_ln1': _L1_ffn_in['ln1'], 'L1_ffn_ln2': _L1_ffn_in['ln2']}
    _x0 = _d['L0_attn_x']
    _d['L0_attn_x'] = jax.random.normal(jax.random.fold_in(jax.random.key(seed), 1), (2, 2048, 256), dtype=_x0.dtype)
    del _x0
    return _d

def reference(L0_attn_x, L0_attn_Wq, L0_attn_bq, L0_attn_Wk, L0_attn_bk, L0_attn_Wv, L0_attn_bv, L0_ffn_gate_w, L0_ffn_gate_b, L0_ffn_rw1, L0_ffn_rb1, L0_ffn_rw2, L0_ffn_rb2, L0_ffn_rw3, L0_ffn_rb3, L0_ffn_sw1, L0_ffn_sb1, L0_ffn_sw2, L0_ffn_sb2, L0_ffn_sw3, L0_ffn_sb3, L1_attn_Wq, L1_attn_Wk, L1_attn_Wv, L1_attn_Wo, L1_ffn_attention_mask, L1_ffn_position_ids, L1_ffn_router_w, L1_ffn_router_b, L1_ffn_wq, L1_ffn_wk, L1_ffn_wv, L1_ffn_wo, L1_ffn_w1, L1_ffn_w2, L1_ffn_ln1, L1_ffn_ln2):

    def _L0_attn_ref(x, Wq, bq, Wk, bk, Wv, bv):
        import jax, jax.numpy as jnp
        import numpy as np
        b, p, d = x.shape
        q = jnp.einsum('bpd,ed->bpe', x, Wq) + bq
        k = jnp.einsum('bpd,ed->bpe', x, Wk) + bk
        v = jnp.einsum('bpd,ed->bpe', x, Wv) + bv
        attn = jnp.einsum('bqd,bkd->bqk', q, k)
        causal = jnp.triu(jnp.ones((p, p), dtype=bool), k=1)
        attn = jnp.where(causal, -jnp.inf, attn)
        attn = attn / jnp.sqrt(jnp.asarray(d, dtype=attn.dtype))
        scores = jax.nn.softmax(attn, axis=-1)
        return jnp.einsum('bqk,bkd->bqd', scores, v)

    def _L0_ffn_ref(x, gate_w, gate_b, rw1, rb1, rw2, rb2, rw3, rb3, sw1, sb1, sw2, sb2, sw3, sb3):
        import jax, jax.numpy as jnp
        import numpy as np
        B, T, D, H = (4, 512, 256, 512)
        E, S, K = (8, 2, 2)

        def _swiglu_stacked(x, w1, b1, w2, b2, w3, b3):
            p1 = jnp.einsum('btd,ndh->nbth', x, w1) + b1[:, None, None, :]
            p2 = jnp.einsum('btd,ndh->nbth', x, w2) + b2[:, None, None, :]
            glu = jax.nn.silu(p1) * p2
            return jnp.einsum('nbth,nhd->nbtd', glu, w3) + b3[:, None, None, :]
        scores = jax.nn.softmax(x @ gate_w + gate_b, axis=-1)
        weights, indices = jax.lax.top_k(scores, K)
        routed_all = _swiglu_stacked(x, rw1, rb1, rw2, rb2, rw3, rb3)
        out_bted = jnp.transpose(routed_all, (1, 2, 0, 3))
        gathered = jnp.take_along_axis(out_bted, indices[..., None], axis=2)
        routed = jnp.sum(weights[..., None] * gathered, axis=2)
        shared = _swiglu_stacked(x, sw1, sb1, sw2, sb2, sw3, sb3).mean(axis=0)
        return shared + routed

    def _L1_attn_ref(in_features, Wq, Wk, Wv, Wo):
        import jax, jax.numpy as jnp
        import numpy as np
        import math
        B, S, D = (8, 512, 256)

        def _trunc_normal(key, shape, fan_in, fan_out):
            std = math.sqrt(2.0 / (fan_in + fan_out))
            return jax.random.truncated_normal(key, -3.0, 3.0, shape, jnp.float32) * std
        d_k = Wq.shape[0]
        scale = 1.0 / math.sqrt(d_k)
        x = in_features
        Q = x @ Wq.T
        K = x @ Wk.T
        V = x @ Wv.T
        scores = jnp.einsum('bqd,bkd->bqk', Q, K) * scale
        seq_len = x.shape[-2]
        causal = jnp.tril(jnp.ones((seq_len, seq_len), dtype=bool))
        scores = jnp.where(causal, scores, -jnp.inf)
        attn = jax.nn.softmax(scores, axis=-1)
        out = jnp.einsum('bqk,bkd->bqd', attn, V)
        return out @ Wo.T

    def _L1_ffn_ref(x, attention_mask, position_ids, router_w, router_b, wq, wk, wv, wo, w1, w2, ln1, ln2):
        import jax, jax.numpy as jnp
        import numpy as np
        B, S, D, H, F = (4, 1024, 256, 16, 1024)
        CAP = 0.125
        ROPE_BASE = 10000.0

        def rmsnorm(x, g):
            return x * jax.lax.rsqrt(jnp.mean(x * x, -1, keepdims=True) + 1e-06) * g

        def rope(t, pos):
            hd = t.shape[-1]
            inv = 1.0 / ROPE_BASE ** (jnp.arange(0, hd, 2, dtype=jnp.float32) / hd)
            f = pos[:, None, :, None].astype(jnp.float32) * inv
            emb = jnp.concatenate([f, f], axis=-1)
            cos, sin = (jnp.cos(emb), jnp.sin(emb))
            rot = jnp.concatenate([-t[..., hd // 2:], t[..., :hd // 2]], axis=-1)
            return t * cos + rot * sin
        b, s, d = x.shape
        hd = d // H
        weights = (x @ router_w)[..., 0] + router_b[0]
        k = int(CAP * s)
        topv, topi = jax.lax.top_k(weights, k)
        thr = topv[:, -1]
        sel_mask = (weights > thr[:, None]).astype(x.dtype)
        kc = k - 1
        sel_idx = jnp.sort(topi[:, :kc], axis=1)
        bidx = jnp.arange(b)[:, None]
        x_sel = x[bidx, sel_idx]
        pos_sel = position_ids[bidx, sel_idx]
        w_sel = weights[bidx, sel_idx]
        m = attention_mask[:, 0]
        m_sel = m[bidx[:, :, None], sel_idx[:, :, None], sel_idx[:, None, :]]
        hn = rmsnorm(x_sel, ln1)

        def heads(t):
            return t.reshape(b, kc, H, hd).transpose(0, 2, 1, 3)
        q = rope(heads(hn @ wq), pos_sel)
        kk = rope(heads(hn @ wk), pos_sel)
        v = heads(hn @ wv)
        sc = jnp.einsum('bhqd,bhkd->bhqk', q, kk) / np.sqrt(hd).astype(np.float32)
        sc = sc + m_sel[:, None]
        a = jax.nn.softmax(sc, axis=-1)
        o = jnp.einsum('bhqk,bhkd->bhqd', a, v).transpose(0, 2, 1, 3).reshape(b, kc, d) @ wo
        x1 = x_sel + o
        x2 = x1 + jax.nn.gelu(rmsnorm(x1, ln2) @ w1) @ w2
        proc = x2 * w_sel[..., None]
        out = jnp.zeros_like(x).at[bidx, sel_idx].set(proc)
        return out + x * (1.0 - sel_mask)[..., None]
    x = L0_attn_x
    xn = _layernorm(x, axis=-1)
    x = x + _L0_attn_ref(xn, L0_attn_Wq, L0_attn_bq, L0_attn_Wk, L0_attn_bk, L0_attn_Wv, L0_attn_bv) + _L0_ffn_ref(xn, L0_ffn_gate_w, L0_ffn_gate_b, L0_ffn_rw1, L0_ffn_rb1, L0_ffn_rw2, L0_ffn_rb2, L0_ffn_rw3, L0_ffn_rb3, L0_ffn_sw1, L0_ffn_sb1, L0_ffn_sw2, L0_ffn_sb2, L0_ffn_sw3, L0_ffn_sb3)
    xn = _layernorm(x, axis=-1)
    x = x + _L1_attn_ref(xn, L1_attn_Wq, L1_attn_Wk, L1_attn_Wv, L1_attn_Wo) + _L1_ffn_ref(xn, L1_ffn_attention_mask, L1_ffn_position_ids, L1_ffn_router_w, L1_ffn_router_b, L1_ffn_wq, L1_ffn_wk, L1_ffn_wv, L1_ffn_wo, L1_ffn_w1, L1_ffn_w2, L1_ffn_ln1, L1_ffn_ln2)
    return x

_drawn_inputs = setup_inputs


def setup_inputs(seed=0):
    import zlib

    import numpy as np

    out = dict(_drawn_inputs(seed))
    spreads = {'L0_attn_bq': (0.0, 0.613),
     'L0_attn_bk': (0.0, 0.8),
     'L0_attn_bv': (0.0, 0.1),
     'L0_ffn_gate_b': (0.0, 0.422),
     'L0_ffn_rb1': (0.0, 0.8),
     'L0_ffn_rb2': (0.0, 0.8),
     'L0_ffn_rb3': (0.0, 0.1),
     'L0_ffn_sb1': (0.0, 0.8),
     'L0_ffn_sb2': (0.0, 0.8),
     'L0_ffn_sb3': (0.0, 0.1),
     'L1_ffn_ln1': (1.0, 0.6),
     'L1_ffn_ln2': (1.0, 0.6)}
    factors = {'L0_ffn_rw1': 5.401,
     'L0_ffn_rw2': 6.082,
     'L0_ffn_rw3': 5.944,
     'L1_ffn_wq': 8.0,
     'L1_ffn_wk': 8.0,
     'L1_ffn_wv': 8.0,
     'L1_ffn_wo': 8.0,
     'L1_ffn_w1': 4.683,
     'L1_ffn_w2': 4.616}
    for name, (base, spread) in spreads.items():
        noise = np.random.default_rng([zlib.crc32(name.encode()), seed]).standard_normal(out[name].shape)
        drawn = base * np.exp(spread * noise) if base else spread * noise
        out[name] = jnp.asarray(drawn.astype(out[name].dtype))
    for name, factor in factors.items():
        out[name] = (out[name] * factor).astype(out[name].dtype)
    return out
```

```python
import concourse.bass as bass
from concourse import mybir
from contextlib import ExitStack

P = 128
FP32 = mybir.dt.float32
FR = mybir.dt.float32r
I32 = mybir.dt.int32
ACT = mybir.ActivationFunctionType
ALU = mybir.AluOpType
AX = mybir.AxisListType
MASKED = -1e30


class Chip:

    def __init__(self, nc, B, S, D):
        self.nc, self.B, self.S, self.D = nc, B, S, D
        self.NT = S // P
        self.KD = D // P
        self.NG = self.NT // 4

    def sems(self, stack, *names):
        return [stack.enter_context(self.nc.semaphore(n)) for n in names]

    def pool_sems(self, *names):
        return [self.nc.alloc_semaphore(name=n) for n in names]


def three_pass(nc, out, lhs, rhs, start, stop):
    (lh, ll), (rh, rl) = lhs, rhs
    nc.tensor.matmul(out, ll, rh, start=start, stop=False)
    nc.tensor.matmul(out, lh, rl, start=False, stop=False)
    return nc.tensor.matmul(out, lh, rh, start=False, stop=stop)


def constants(chip, stack):
    nc = chip.nc
    ident = stack.enter_context(nc.sbuf_tensor("ident", [P, P], FP32))
    ident_r = stack.enter_context(nc.sbuf_tensor("ident_r", [P, P], FR))
    causal_r = stack.enter_context(nc.sbuf_tensor("causal_r", [P, P], FR))
    with ExitStack() as st:
        causal = st.enter_context(nc.sbuf_tensor("causal", [P, P], FP32))
        filled, selected, copied = chip.sems(st, "const_filled", "const_selected", "const_copied")
        with nc.Block() as block:

            @block.gpsimd
            def _(pool):
                nc.gpsimd.memset(ident[:], 0.0).then_inc(filled, 1)
                nc.gpsimd.memset(causal[:], 0.0).then_inc(filled, 1)
                pool.wait_ge(filled, 2)
                nc.gpsimd.affine_select(out=ident[:], in_=ident[:], compare_op=ALU.not_equal, fill=1.0,
                                        base=0, pattern=[[-1, P]], channel_multiplier=1).then_inc(selected, 1)
                nc.gpsimd.affine_select(out=causal[:], in_=causal[:], compare_op=ALU.is_ge, fill=MASKED,
                                        base=0, pattern=[[-1, P]], channel_multiplier=1).then_inc(selected, 1)

            @block.vector
            def _(dve):
                dve.wait_ge(selected, 2)
                nc.vector.tensor_copy(ident_r[:], ident[:]).then_inc(copied, 1)
                nc.vector.tensor_copy(causal_r[:], causal[:]).then_inc(copied, 1)
                dve.wait_ge(copied, 2)

        nc.sync.sem_clear(filled), nc.sync.sem_clear(selected), nc.sync.sem_clear(copied)
    chip.ident, chip.ident_r, chip.causal_r = ident, ident_r, causal_r
    nc.all_engine_barrier()


def split_weights(chip, stack, named, scales={}, tag=""):
    nc = chip.nc
    out = {}
    with ExitStack() as keep:
        for name, w in named:
            k, n = w.shape
            out[name] = tuple(stack.enter_context(nc.sbuf_tensor(f"{tag}{name}_{part}", [P, k // P, n], FR))
                              for part in ("hi", "lo"))
        raws = [keep.enter_context(nc.sbuf_tensor(f"{tag}{name}_raw", [P, w.shape[0] // P, w.shape[1]], FP32))
                for name, w in named]
        loaded = chip.sems(keep, *[f"{tag}{name}_loaded" for name, _ in named])
        (hi_done, lo_done) = chip.sems(keep, tag + "w_hi_done", tag + "w_lo_done")
        with nc.Block() as block:

            @block.sync
            def _(sp):
                for (name, w), raw, sem in zip(named, raws, loaded):
                    sp.dma_start(raw[:], w.rearrange("(k p) n -> p k n", p=P)).then_inc(sem, 16)

            @block.scalar
            def _(act):
                for (name, w), raw, sem in zip(named, raws, loaded):
                    act.wait_ge(sem, 16)
                    nc.scalar.activation(out[name][0][:], raw[:], ACT.Copy, scale=scales.get(name, 1.0)
                                         ).then_inc(hi_done, 1)

            @block.vector
            def _(dve):
                for n, ((name, w), raw) in enumerate(zip(named, raws)):
                    dve.wait_ge(hi_done, n + 1)
                    flat = lambda a: a.rearrange("p k n -> p (k n)")
                    nc.vector.scalar_tensor_tensor(flat(out[name][1][:]), flat(raw[:]), scales.get(name, 1.0),
                                                   flat(out[name][0][:]).bitcast(FP32), ALU.mult,
                                                   ALU.subtract).then_inc(lo_done, 1)
                dve.wait_ge(lo_done, len(named))

        for s in [*loaded, hi_done, lo_done]:
            nc.sync.sem_clear(s)
    nc.all_engine_barrier()
    return out


def norm_stage(chip, b, tag, src, xn_dram, T, V, w, extra, scores):
    nc, NT, KD, NG, D = chip.nc, chip.NT, chip.KD, chip.NG, chip.D
    E = scores.shape[2]
    AHEAD = 2
    with ExitStack() as st:
        sb = lambda n, s, d=FP32: st.enter_context(nc.sbuf_tensor(f"{tag}_{n}", s, d))
        pb = lambda n, s: st.enter_context(nc.psum_tensor(f"{tag}_{n}", s, FP32))
        X, XN = sb("x", [P, NT, D]), sb("xn", [P, NT, D])
        stats, mv = sb("stats", [P, NT, 6]), sb("mv", [P, NT, 2])
        ve, std, rstd, tmp = (sb(n, [P, NT]) for n in ("ve", "std", "rstd", "tmp"))
        Tps, Vps = pb("Tps", [P, 2, 512]), pb("Vps", [P, 2, 512])
        Gps = pb("Gps", [P, NT, E])
        loaded = chip.sems(st, *[f"{tag}_x_loaded{g}" for g in range(NG)])
        (var_ready, std_ready, xn_ready, t_done, t_hi, t_lo, v_done, v_hi, v_lo, stored, chain) = every = chip.sems(
            st, *[f"{tag}_{n}" for n in ("var_ready", "std_ready", "xn_ready", "t_done", "t_hi", "t_lo", "v_done",
                                         "v_hi", "v_lo", "xn_stored", "dve_chain")])
        x_view = src.rearrange("(t p) d -> p t d", p=P)
        xn_view = xn_dram.rearrange("(t p) d -> p t d", p=P)

        with nc.Block() as block:

            @block.sync
            def _(sp):
                for g in range(NG):
                    sp.dma_start(X[:, 4 * g:4 * g + 4, :], x_view[:, bass.ds(b * NT + 4 * g, 4), :]
                                 ).then_inc(loaded[g], 16)
                for g in range(NG):
                    sp.wait_ge(xn_ready, 4 * (g + 1))
                    sp.dma_start(xn_view[:, bass.ds(b * NT + 4 * g, 4), :], XN[:, 4 * g:4 * g + 4, :]
                                 ).then_inc(stored, 16)
                sp.wait_ge(stored, 16 * NG)

            @block.vector
            def _(dve):
                links = [0]

                def link(ins):
                    links[0] += 1
                    ins.then_inc(chain, 1)
                    dve.wait_ge(chain, links[0])

                def values_lo(g):
                    for h in range(2):
                        n = 2 * g + h
                        pair = slice(2 * n, 2 * n + 2)
                        dve.wait_ge(v_hi, n + 1)
                        nc.vector.tensor_tensor(
                            V[1][:, pair, :].rearrange("p t d -> p (t d)"), Vps[:, n % 2, :],
                            V[0][:, pair, :].rearrange("p t d -> p (t d)").bitcast(FP32),
                            ALU.subtract).then_inc(v_lo, 1)

                def normalise(g):
                    four = slice(4 * g, 4 * g + 4)
                    dve.wait_ge(loaded[g], 16)
                    for t in range(4 * g, 4 * g + 4):
                        ins = nc.vector.bn_stats(stats[:, t, :], X[:, t, :])
                    link(ins)
                    for t in range(4 * g, 4 * g + 4):
                        ins = nc.vector.bn_aggr(mv[:, t, :], stats[:, t, :])
                    link(ins)
                    nc.vector.tensor_scalar_add(ve[:, four], mv[:, four, 1], 1e-5).then_inc(var_ready, 1)
                    dve.wait_ge(std_ready, g + 1)
                    link(nc.vector.reciprocal(rstd[:, four], std[:, four]))
                    link(nc.vector.tensor_tensor(tmp[:, four], rstd[:, four], rstd[:, four], ALU.mult))
                    link(nc.vector.tensor_tensor(tmp[:, four], tmp[:, four], ve[:, four], ALU.mult))
                    link(nc.vector.tensor_scalar(tmp[:, four], tmp[:, four], -0.5, 1.5, ALU.mult, ALU.add))
                    link(nc.vector.tensor_tensor(rstd[:, four], rstd[:, four], tmp[:, four], ALU.mult))
                    for t in range(4 * g, 4 * g + 4):
                        nc.vector.tensor_scalar(XN[:, t, :], X[:, t, :], mv[:, t, 0:1], rstd[:, t:t + 1],
                                                ALU.subtract, ALU.mult).then_inc(xn_ready, 1)

                for g in range(AHEAD):
                    normalise(g)
                for g in range(NG):
                    if g + AHEAD < NG:
                        normalise(g + AHEAD)
                    for k in range(KD):
                        n = KD * g + k
                        dve.wait_ge(t_hi, n + 1)
                        tok = slice(512 * g, 512 * g + 512)
                        nc.vector.tensor_tensor(T[1][:, k, tok], Tps[:, n % 2, :], T[0][:, k, tok].bitcast(FP32),
                                                ALU.subtract).then_inc(t_lo, 1)
                    if g:
                        values_lo(g - 1)
                values_lo(NG - 1)
                nc.vector.tensor_copy(scores[:, bass.ds(b * NT, NT), :], Gps[:]).then_inc(chain, 1)

            @block.scalar
            def _(act):
                def values_hi(g):
                    for h in range(2):
                        n = 2 * g + h
                        act.wait_ge(v_done, n + 1)
                        nc.scalar.activation(V[0][:, 2 * n:2 * n + 2, :].rearrange("p t d -> p (t d)"),
                                             Vps[:, n % 2, :], ACT.Copy).then_inc(v_hi, 1)

                def root(g):
                    four = slice(4 * g, 4 * g + 4)
                    act.wait_ge(var_ready, g + 1)
                    nc.scalar.activation(std[:, four], ve[:, four], ACT.Sqrt).then_inc(std_ready, 1)

                for g in range(AHEAD):
                    root(g)
                for g in range(NG):
                    if g + AHEAD < NG:
                        root(g + AHEAD)
                    for k in range(KD):
                        n = KD * g + k
                        act.wait_ge(t_done, n + 1)
                        nc.scalar.activation(T[0][:, k, 512 * g:512 * g + 512], Tps[:, n % 2, :],
                                             ACT.Copy).then_inc(t_hi, 1)
                    if g:
                        values_hi(g - 1)
                values_hi(NG - 1)

            @block.tensor
            def _(pe):
                def values(g):
                    pe.wait_ge(t_lo, KD * (g + 1))
                    for h in range(2):
                        n = 2 * g + h
                        if n >= 2:
                            pe.wait_ge(v_lo, n - 1)
                        for j in range(2):
                            t = 2 * n + j
                            x = [[part[:, k, P * t:P * t + P] for part in T] for k in range(KD)]
                            for k in range(KD):
                                three_pass(nc, Gps[:, t, :], x[k], [part[:, k, :] for part in extra],
                                           k == 0, k == KD - 1)
                            for k in range(KD):
                                last = three_pass(nc, Vps[:, n % 2, D * j:D * j + D], x[k],
                                                  [part[:, k, :] for part in w["wv"]], k == 0, k == KD - 1)
                        last.then_inc(v_done, 1)

                for g in range(NG):
                    pe.wait_ge(xn_ready, 4 * (g + 1))
                    for k in range(KD):
                        n = KD * g + k
                        if n >= 2:
                            pe.wait_ge(t_lo, n - 1)
                        for j in range(4):
                            last = nc.tensor.transpose(Tps[:, n % 2, P * j:P * j + P],
                                                       XN[:, 4 * g + j, P * k:P * k + P], chip.ident[:])
                        last.then_inc(t_done, 1)
                    if g:
                        values(g - 1)
                values(NG - 1)

        for s in [*loaded, *every]:
            nc.sync.sem_clear(s)
    nc.all_engine_barrier()


def attention_stage(chip, b, tag, T, V, w, biases, bases, value_bias, dst):
    nc, NT, KD, NG, D = chip.nc, chip.NT, chip.KD, chip.NG, chip.D
    has_o = "wo" in w
    SLOTS = 4
    TBANKS = 3
    FRONTS = 3
    SBUFS = 3
    AHEAD = 2
    LAG = 2

    steps, of_tile = [], []
    for i in range(NT):
        groups = [("p", i, k0, min(4, i + 1 - k0)) for k0 in range(0, i + 1, 4)]
        if has_o and i >= 2:
            groups.append(("o", i - 2, 0, KD))
        if has_o and i == NT - 1:
            groups += [("o", i - 1, 0, KD)]
        of_tile.append(range(len(steps), len(steps) + len(groups)))
        steps += groups
    body_steps = len(steps)
    if has_o:
        steps.append(("o", NT - 1, 0, KD))
    last_p = {i: max(n for n, s in enumerate(steps) if s[0] == "p" and s[1] == i) for i in range(NT)}
    o_step = {s[1]: n for n, s in enumerate(steps) if s[0] == "o"}
    chunks = lambda i: i // 4 + 1
    chunks_before = lambda i: sum(chunks(j) for j in range(i))
    acc_use = {}
    for kind, i, k0, _ in steps:
        if k0 == 0:
            acc_use[(kind, i)] = len(acc_use)

    project = lambda c: [(kind, c, m) for kind in "kq" for m in range(KD)]
    score = lambda i: [("s", i, j) for j in range(chunks(i))]
    first_units = project(0) + [u for i in range(AHEAD) for u in score(i)]
    front_at = {n: [] for n in range(len(steps))}
    for i in range(NT):
        units = score(i + AHEAD) if i + AHEAD < NT else []
        c = (i + AHEAD + 1) // 4
        if (i + AHEAD + 1) % 4 == 0 and c < NG:
            units = units + project(c)
        for q, u in enumerate(units):
            front_at[of_tile[i][q * len(of_tile[i]) // len(units)]].append(u)
    every_unit = first_units + [u for n in range(len(steps)) for u in front_at[n]]
    unit_no = {u: n for n, u in enumerate(every_unit)}
    proj_no = {u: n for n, u in enumerate(u for u in every_unit if u[0] != "s")}
    exp_at = {of_tile[i - 1][0]: i for i in range(1, NT)}

    with ExitStack() as st:
        sb = lambda n, s, d=FP32: st.enter_context(nc.sbuf_tensor(f"{tag}_{n}", s, d))
        pb = lambda n, s: st.enter_context(nc.psum_tensor(f"{tag}_{n}", s, FP32))
        kT = [sb(f"kT{p}", [P, KD, chip.S], FR) for p in "hl"]
        qT = [sb(f"qT{p}", [P, 2, KD, 512], FR) for p in "hl"]
        probs = sb("probs", [P, SBUFS, chip.S])
        pT = [sb(f"pT{p}", [P, SLOTS, 512], FR) for p in "hl"]
        base = sb("base", [P, 2, 4, D])
        base2 = sb("base2", [P, 2, 4, D]) if len(bases) > 1 else None
        if has_o:
            heads = sb("o_norm", [P, 2, D])
        part_min, neg_max = sb("part_min", [P, NT, 4]), sb("neg_max", [P, NT])
        sums, rsum = sb("sums", [P, NT]), sb("rsum", [P, NT])
        front, Tps, acc = pb("front", [P, FRONTS, 512]), pb("Tps", [P, TBANKS, 512]), pb("acc", [P, 2, 512])
        base_loaded = chip.sems(st, f"{tag}_base_loaded0", f"{tag}_base_loaded1")
        (proj_done, proj_hi, front_free, acc_free, s_done, max_done, exp_done, t_done, t_hi, t_lo, pv_done, rs_ready,
         base_ready, y_stored) = every = chip.sems(
            st, *[f"{tag}_{n}" for n in (
                "proj_done", "proj_hi", "front_free", "acc_free", "scores_done", "max_done", "exp_done", "t_done",
                "t_hi", "t_lo", "pv_done", "rsum_ready", "base_ready", "y_stored")])
        stored_as = "o" if has_o else "p"
        view = lambda a: a.rearrange("(t p) d -> p t d", p=P)
        bank_of = lambda u: front[:, unit_no[u] % FRONTS, :]

        def projected(u, part):
            kind, c, m = u
            return qT[part][:, c % 2, m, :] if kind == "q" else kT[part][:, m, 512 * c:512 * c + 512]

        with nc.Block() as block:

            @block.sync
            def _(sp):
                for c in range(NG):
                    if c >= 2:
                        sp.wait_ge(y_stored, 16 * (c - 1))
                    tiles = bass.ds(b * NT + 4 * c, 4)
                    sp.dma_start(base[:, c % 2, :, :], view(bases[0])[:, tiles, :]).then_inc(base_loaded[c % 2], 16)
                    if base2 is not None:
                        sp.dma_start(base2[:, c % 2, :, :], view(bases[1])[:, tiles, :]
                                     ).then_inc(base_loaded[c % 2], 16)
                    if c:
                        sp.wait_ge(acc_free, acc_use[(stored_as, 4 * c - 1)] + 1)
                        sp.dma_start(view(dst)[:, bass.ds(b * NT + 4 * (c - 1), 4), :], base[:, (c - 1) % 2, :, :]
                                     ).then_inc(y_stored, 16)
                sp.wait_ge(acc_free, acc_use[(stored_as, NT - 1)] + 1)
                sp.dma_start(view(dst)[:, bass.ds(b * NT + 4 * (NG - 1), 4), :], base[:, (NG - 1) % 2, :, :]
                             ).then_inc(y_stored, 16)
                sp.wait_ge(y_stored, 16 * NG)

            @block.gpsimd
            def _(pool):
                for c in range(NG):
                    pool.wait_ge(base_loaded[c % 2], 16 * len(bases) * (c // 2 + 1))
                    slot = base[:, c % 2, :, :]
                    if base2 is not None:
                        other = base2[:, c % 2, :, :]
                    else:
                        other = value_bias[:].rearrange("p (a d) -> p a d", a=1).to_broadcast([P, 4, D])
                    nc.gpsimd.tensor_tensor(slot, slot, other, ALU.add).then_inc(base_ready, 1)

            @block.scalar
            def _(act):
                def project_hi(u):
                    kind, c, m = u
                    act.wait_ge(proj_done, proj_no[u] + 1)
                    if kind == "q" and c >= 2 and m == 0:
                        act.wait_ge(s_done, chunks_before(4 * (c - 1)))
                    if biases:
                        ins = nc.scalar.activation(projected(u, 0), bank_of(u), ACT.Identity,
                                                   bias=biases[kind][:, m:m + 1])
                    else:
                        ins = nc.scalar.activation(projected(u, 0), bank_of(u), ACT.Copy)
                    ins.then_inc(proj_hi, 1)

                def exponentials(i):
                    act.wait_ge(max_done, i + 1)
                    both = probs[:, i % SBUFS, 0:P * (i + 1)]
                    nc.scalar.activation(both, both, ACT.Exp, scale=-1.0, bias=neg_max[:, i:i + 1],
                                         accum_out=sums[:, i:i + 1]).then_inc(exp_done, 1)

                def transposed_hi(n):
                    act.wait_ge(t_done, n + 1)
                    if n >= SLOTS:
                        act.wait_ge(pv_done, n - SLOTS + 1)
                    width = P * steps[n][3]
                    nc.scalar.activation(pT[0][:, n % SLOTS, 0:width], Tps[:, n % TBANKS, 0:width],
                                         ACT.Copy).then_inc(t_hi, 1)

                for u in project(0):
                    project_hi(u)
                exponentials(0)
                for n in range(len(steps)):
                    transposed_hi(n)
                    if n in exp_at:
                        exponentials(exp_at[n])
                    for u in front_at[n]:
                        if u[0] != "s":
                            project_hi(u)

            @block.vector
            def _(dve):
                def front_read(u):
                    if u[0] != "s":
                        dve.wait_ge(proj_hi, proj_no[u] + 1)
                        hi = projected(u, 0).bitcast(FP32)
                        if biases:
                            ins = nc.vector.scalar_tensor_tensor(projected(u, 1), bank_of(u),
                                                                 biases[u[0]][:, u[2]:u[2] + 1], hi, ALU.add,
                                                                 ALU.subtract)
                        else:
                            ins = nc.vector.tensor_tensor(projected(u, 1), bank_of(u), hi, ALU.subtract)
                        ins.then_inc(front_free, 1)
                        return
                    _, i, j = u
                    dve.wait_ge(s_done, chunks_before(i) + j + 1)
                    if i >= SBUFS and j == 0:
                        dve.wait_ge(t_done, last_p[i - SBUFS] + 1)
                    width = min(512, P * (i + 1) - 512 * j)
                    one = chunks(i) == 1
                    nc.vector.tensor_scalar(probs[:, i % SBUFS, 512 * j:512 * j + width], bank_of(u)[:, 0:width],
                                            -1.0, None, ALU.mult, ALU.min,
                                            accum_out=neg_max[:, i:i + 1] if one else part_min[:, i, j:j + 1]
                                            ).then_inc(front_free, 1)
                    if j == chunks(i) - 1:
                        dve.wait_ge(front_free, unit_no[u] + 1)
                        if one:
                            dve.sem_inc(max_done, 1)
                        else:
                            nc.vector.tensor_reduce(neg_max[:, i:i + 1], part_min[:, i, 0:chunks(i)], AX.X, ALU.min
                                                    ).then_inc(max_done, 1)

                def transposed_lo(n):
                    dve.wait_ge(t_hi, n + 1)
                    width = P * steps[n][3]
                    nc.vector.tensor_tensor(pT[1][:, n % SLOTS, 0:width], Tps[:, n % TBANKS, 0:width],
                                            pT[0][:, n % SLOTS, 0:width].bitcast(FP32),
                                            ALU.subtract).then_inc(t_lo, 1)

                def finish(n):
                    kind, i = steps[n][:2]
                    if kind == "p" and n != last_p[i]:
                        return
                    bank = acc[:, acc_use[(kind, i)] % 2, 0:D]
                    slot = base[:, (i // 4) % 2, i % 4, :]
                    if kind == "p":
                        dve.wait_ge(exp_done, i + 1)
                        nc.vector.reciprocal(rsum[:, i:i + 1], sums[:, i:i + 1]).then_inc(rs_ready, 1)
                        dve.wait_ge(rs_ready, i + 1)
                    dve.wait_ge(pv_done, n + 1)
                    if kind == "p" and has_o:
                        if i >= 2:
                            dve.wait_ge(t_done, o_step[i - 2] + 1)
                        nc.vector.tensor_scalar(heads[:, i % 2, :], bank, rsum[:, i:i + 1], None,
                                                ALU.mult).then_inc(acc_free, 1)
                        return
                    dve.wait_ge(base_ready, i // 4 + 1)
                    if kind == "p":
                        ins = nc.vector.scalar_tensor_tensor(slot, bank, rsum[:, i:i + 1], slot, ALU.mult, ALU.add)
                    else:
                        ins = nc.vector.tensor_tensor(slot, bank, slot, ALU.add)
                    ins.then_inc(acc_free, 1)

                for u in first_units:
                    front_read(u)
                for n in range(len(steps)):
                    if n > LAG:
                        finish(n - LAG - 1)
                    transposed_lo(n)
                    for u in front_at[n]:
                        front_read(u)
                for n in range(len(steps) - LAG - 1, len(steps)):
                    finish(n)

            @block.tensor
            def _(pe):
                def front_unit(u):
                    kind, c, m = u
                    if unit_no[u] >= FRONTS:
                        pe.wait_ge(front_free, unit_no[u] - FRONTS + 1)
                    if kind != "s":
                        for k in range(KD):
                            last = three_pass(nc, bank_of(u), [p[:, k, P * m:P * m + P] for p in w["w" + kind]],
                                              [p[:, k, 512 * c:512 * c + 512] for p in T], k == 0, k == KD - 1)
                        last.then_inc(proj_done, 1)
                        return
                    _, i, j = u
                    if i % 4 == 0 and j == 0:
                        pe.wait_ge(front_free, unit_no[("q", i // 4, KD - 1)] + 1)
                    rows = slice(P * (i % 4), P * (i % 4) + P)
                    cols = slice(512 * j, min(512 * j + 512, P * (i + 1)))
                    width = cols.stop - cols.start
                    diagonal = j == chunks(i) - 1
                    for k in range(KD):
                        last = three_pass(nc, bank_of(u)[:, 0:width], [p[:, (i // 4) % 2, k, rows] for p in qT],
                                          [p[:, k, cols] for p in kT], k == 0, k == KD - 1 and not diagonal)
                    if diagonal:
                        last = nc.tensor.matmul(bank_of(u)[:, width - P:width], chip.ident_r[:], chip.causal_r[:],
                                                start=False, stop=True)
                    last.then_inc(s_done, 1)

                def transposes(n):
                    kind, i, k0, count = steps[n]
                    if n >= TBANKS:
                        pe.wait_ge(t_lo, n - TBANKS + 1)
                    if kind == "p":
                        pe.wait_ge(exp_done, i + 1)
                        src = probs[:, i % SBUFS, :]
                    else:
                        pe.wait_ge(acc_free, acc_use[("p", i)] + 1)
                        src = heads[:, i % 2, :]
                    for j in range(count):
                        last = nc.tensor.transpose(Tps[:, n % TBANKS, P * j:P * j + P],
                                                   src[:, P * (k0 + j):P * (k0 + j) + P], chip.ident[:])
                    last.then_inc(t_done, 1)

                def products(n):
                    kind, i, k0, count = steps[n]
                    pe.wait_ge(t_lo, n + 1)
                    u = acc_use[(kind, i)]
                    if k0 == 0 and u >= 2:
                        pe.wait_ge(acc_free, u - 1)
                    ends = kind == "o" or n == last_p[i]
                    for j in range(count):
                        rhs = [p[:, k0 + j, :] for p in (V if kind == "p" else w["wo"])]
                        last = three_pass(nc, acc[:, u % 2, 0:D], [p[:, n % SLOTS, P * j:P * j + P] for p in pT],
                                          rhs, k0 + j == 0, ends and j == count - 1)
                    last.then_inc(pv_done, 1)

                for u in first_units:
                    front_unit(u)
                for n in range(body_steps):
                    transposes(n)
                    if n >= LAG:
                        products(n - LAG)
                    for u in front_at[n]:
                        front_unit(u)
                if has_o:
                    products(body_steps - 2)
                    products(body_steps - 1)
                    transposes(body_steps)
                    products(body_steps)
                else:
                    products(body_steps - 2)
                    products(body_steps - 1)

        for s in [*base_loaded, *every]:
            nc.sync.sem_clear(s)
    nc.all_engine_barrier()


def gating_stage(chip, logits, gate_b, gates, slots, tile_expert, tile_rows, E, TILES):
    nc = chip.nc
    NA = logits.shape[1]
    with ExitStack() as st:
        sb = lambda n, s, d=FP32: st.enter_context(nc.sbuf_tensor(f"g_{n}", s, d))
        ones, before, rev = sb("ones", [P, P]), sb("before", [P, P]), sb("rev", [P, E])
        tile_no, row_no = sb("tile_no", [P, TILES]), sb("row_no", [64, 1])
        L, L2, ex, eq = (sb(n, [P, NA, E]) for n in ("L", "L2", "ex", "eq"))
        oh = [sb(f"oh{k}", [P, NA, E]) for k in range(2)]
        m = [sb(f"m{k}", [P, NA]) for k in range(2)]
        mx, total = sb("mx", [P, NA]), sb("total", [P, NA])
        picked, where = sb("picked", [P, NA, E]), sb("where", [P, NA, E])
        gsum = sb("gsum", [P, NA])
        counts, running = sb("counts", [P, NA, E]), sb("running", [P, NA, E])
        tiles_i, tiles_f, end_tile, start_row = (sb("tiles_i", [P, E], I32), sb("tiles_f", [P, E]),
                                                 sb("end_tile", [P, E]), sb("start_row", [P, E]))
        expert_f = sb("expert_f", [P, TILES])
        slot_f = sb("slot_f", [P, NA])
        onesE = sb("onesE", [P, max(NA, E)])
        within = st.enter_context(nc.psum_tensor("g_within", [P, NA, E], FP32))
        in_tile = st.enter_context(nc.psum_tensor("g_in_tile", [P, NA, E], FP32))
        chain, made, exp_ready, picked_ready, counted = every = chip.sems(
            st, "g_chain", "g_made", "g_exp_ready", "g_picked_ready", "g_counted")
        wide = lambda a: a.rearrange("p (t o) -> p t o", o=1).to_broadcast([P, NA, E])
        tall = lambda a: a.rearrange("p (o e) -> p o e", o=1).to_broadcast([P, NA, E])

        with nc.Block() as block:

            @block.gpsimd
            def _(pool):
                nc.gpsimd.memset(ones[:], 1.0).then_inc(made, 1)
                nc.gpsimd.memset(before[:], 1.0).then_inc(made, 1)
                nc.gpsimd.memset(onesE[:], 1.0).then_inc(made, 1)
                nc.gpsimd.iota(rev[:], pattern=[[-1, E]], base=E, channel_multiplier=0,
                               allow_small_or_imprecise_dtypes=True).then_inc(made, 1)
                nc.gpsimd.iota(tile_no[:], pattern=[[1, TILES]], base=0, channel_multiplier=0,
                               allow_small_or_imprecise_dtypes=True).then_inc(made, 1)
                nc.gpsimd.iota(row_no[:], pattern=[[0, 1]], base=0, channel_multiplier=1,
                               allow_small_or_imprecise_dtypes=True).then_inc(made, 1)
                pool.wait_ge(made, 6)
                nc.gpsimd.affine_select(out=before[:], in_=before[:], compare_op=ALU.is_gt, fill=0.0, base=0,
                                        pattern=[[1, P]], channel_multiplier=-1).then_inc(made, 1)

            @block.vector
            def _(dve):
                links = [0]

                def link(ins):
                    links[0] += 1
                    ins.then_inc(chain, 1)
                    dve.wait_ge(chain, links[0])

                tt, V = nc.vector.tensor_tensor, nc.vector
                dve.wait_ge(made, 7)
                link(tt(L[:], logits[:], tall(gate_b[:]), ALU.add))
                link(V.tensor_reduce(m[0][:], L[:], AX.X, ALU.max))
                tt(ex[:], L[:], wide(m[0][:]), ALU.subtract).then_inc(exp_ready, 1)
                src = L
                for k in range(2):
                    link(tt(eq[:], src[:], wide(m[k][:]), ALU.is_equal))
                    link(tt(eq[:], eq[:], tall(rev[:]), ALU.mult))
                    link(V.tensor_reduce(mx[:], eq[:], AX.X, ALU.max))
                    link(tt(oh[k][:], eq[:], wide(mx[:]), ALU.is_equal))
                    if k == 0:
                        flat = lambda a: a.rearrange("p t e -> p (t e)")
                        link(V.scalar_tensor_tensor(flat(L2[:]), flat(oh[0][:]), MASKED, flat(L[:]), ALU.mult, ALU.add))
                        link(V.tensor_reduce(m[1][:], L2[:], AX.X, ALU.max))
                        src = L2
                tt(picked[:], oh[0][:], oh[1][:], ALU.add).then_inc(picked_ready, 1)
                dve.wait_ge(exp_ready, 2)
                link(V.tensor_reduce(total[:], ex[:], AX.X, ALU.add))
                link(V.reciprocal(total[:], total[:]))
                for k in range(2):
                    link(tt(eq[:], ex[:], oh[k][:], ALU.mult))
                    link(V.tensor_reduce(gsum[:], eq[:], AX.X, ALU.add))
                    link(tt(gates[:, :, k], gsum[:], total[:], ALU.mult))
                dve.wait_ge(counted, 1)
                link(V.tensor_copy(counts[:], in_tile[:]))
                for e in range(E):
                    ins = V.tensor_tensor_scan(running[:, :, e], onesE[:, 0:NA], counts[:, :, e], 0.0,
                                               ALU.mult, ALU.add)
                link(ins)
                link(V.tensor_scalar_add(tiles_i[:], running[:, NA - 1, :], float(P - 1)))
                link(V.tensor_single_scalar(tiles_i[:], tiles_i[:], 7, ALU.logical_shift_right))
                link(V.tensor_copy(tiles_f[:], tiles_i[:]))
                link(V.tensor_tensor_scan(end_tile[:], onesE[:, 0:E], tiles_f[:], 0.0, ALU.mult, ALU.add))
                link(tt(start_row[:], end_tile[:], tiles_f[:], ALU.subtract))
                link(V.tensor_single_scalar(start_row[:], start_row[:], float(P), ALU.mult))
                link(tt(running[:], running[:], counts[:], ALU.subtract))
                link(tt(where[:], running[:], within[:], ALU.add))
                link(tt(where[:], where[:], tall(start_row[:]), ALU.add))
                for k in range(2):
                    link(tt(eq[:], where[:], oh[k][:], ALU.mult))
                    link(V.tensor_reduce(slot_f[:], eq[:], AX.X, ALU.add))
                    link(V.tensor_copy(slots[:, :, k], slot_f[:]))
                link(V.tensor_scalar(expert_f[:], tile_no[:], end_tile[:, 0:1], None, ALU.is_ge))
                for e in range(1, E - 1):
                    link(V.scalar_tensor_tensor(expert_f[:], tile_no[:], end_tile[:, e:e + 1], expert_f[:],
                                                ALU.is_ge, ALU.add))
                V.tensor_scalar(tile_rows[0:32, :], expert_f[0:32, :], row_no[0:32, :], None, ALU.is_equal)
                V.tensor_scalar(tile_rows[32:64, :], expert_f[32:64, :], 32.0, row_no[32:64, :], ALU.add, ALU.is_equal)
                link(V.tensor_copy(tile_expert[:], expert_f[0:1, :]))

            @block.scalar
            def _(act):
                act.wait_ge(exp_ready, 1)
                nc.scalar.activation(ex[:], ex[:], ACT.Exp).then_inc(exp_ready, 1)

            @block.tensor
            def _(pe):
                pe.wait_ge(picked_ready, 1)
                nc.tensor.matmul(within[:], before[:], picked[:], start=True, stop=True)
                nc.tensor.matmul(in_tile[:], ones[:], picked[:], start=True, stop=True).then_inc(counted, 1)

        for s in every:
            nc.sync.sem_clear(s)
    nc.all_engine_barrier()


def dispatch_stage(chip, xn_dram, slots, sorted_dram):
    nc = chip.nc
    NA = slots.shape[1]
    RING = 4
    with ExitStack() as st:
        rows = st.enter_context(nc.sbuf_tensor("d_rows", [P, RING, chip.D], FP32))
        loaded = chip.sems(st, *[f"d_loaded{r}" for r in range(RING)])
        sent = chip.pool_sems(*[f"d_sent{r}" for r in range(RING)])
        with nc.Block() as block:

            @block.sync
            def _(sp):
                for t in range(NA):
                    if t >= RING:
                        sp.wait_ge(sent[t % RING], 32 * (t // RING))
                    sp.dma_start(rows[:, t % RING, :], xn_dram[P * t:P * t + P, :]).then_inc(loaded[t % RING], 16)

            @block.gpsimd
            def _(pool):
                for t in range(NA):
                    pool.wait_ge(loaded[t % RING], 16 * (t // RING + 1))
                    for k in range(2):
                        nc.gpsimd.indirect_dma_start(
                            out=sorted_dram[:, :], out_offset=bass.IndirectOffsetOnAxis(ap=slots[:, t, k:k + 1], axis=0),
                            in_=rows[:, t % RING, :], in_offset=None).then_inc(sent[t % RING], 16)
                for r in range(RING):
                    pool.wait_ge(sent[r], 32 * (NA // RING))

        for s in [*loaded, *sent]:
            nc.sync.sem_clear(s)
    nc.all_engine_barrier()


def combine_stage(chip, base_dram, routed_dram, slots, gates, dst):
    nc, D = chip.nc, chip.D
    NA = slots.shape[1]
    RING = 4
    with ExitStack() as st:
        base = st.enter_context(nc.sbuf_tensor("c_base", [P, RING, D], FP32))
        rows = st.enter_context(nc.sbuf_tensor("c_rows", [P, RING, 2, D], FP32))
        loaded = chip.sems(st, *[f"c_loaded{r}" for r in range(RING)])
        gathered = chip.pool_sems(*[f"c_gathered{r}" for r in range(RING)])
        stored = chip.sems(st, *[f"c_stored{r}" for r in range(RING)])
        (added,) = chip.sems(st, "c_added")
        with nc.Block() as block:

            @block.sync
            def _(sp):
                for t in range(NA):
                    r = t % RING
                    if t >= RING:
                        sp.wait_ge(stored[r], 16 * (t // RING))
                    sp.dma_start(base[:, r, :], base_dram[P * t:P * t + P, :]).then_inc(loaded[r], 16)

            @block.gpsimd
            def _(pool):
                for t in range(NA):
                    r = t % RING
                    if t >= RING:
                        pool.wait_ge(added, 2 * (t - RING + 1))
                    for k in range(2):
                        nc.gpsimd.indirect_dma_start(
                            out=rows[:, r, k, :], out_offset=None, in_=routed_dram[:, :],
                            in_offset=bass.IndirectOffsetOnAxis(ap=slots[:, t, k:k + 1], axis=0)
                        ).then_inc(gathered[r], 16)

            @block.vector
            def _(dve):
                for t in range(NA):
                    r = t % RING
                    dve.wait_ge(loaded[r], 16 * (t // RING + 1))
                    dve.wait_ge(gathered[r], 32 * (t // RING + 1))
                    for k in range(2):
                        nc.vector.scalar_tensor_tensor(base[:, r, :], rows[:, r, k, :], gates[:, t, k:k + 1],
                                                       base[:, r, :], ALU.mult, ALU.add).then_inc(added, 1)
                        dve.wait_ge(added, 2 * t + k + 1)

            @block.scalar
            def _(act):
                for t in range(NA):
                    r = t % RING
                    act.wait_ge(added, 2 * (t + 1))
                    act.dma_start(dst[P * t:P * t + P, :], base[:, r, :]).then_inc(stored[r], 16)
                for r in range(RING):
                    act.wait_ge(stored[r], 16 * (NA // RING))

        for s in [*loaded, *gathered, *stored, added]:
            nc.sync.sem_clear(s)
    nc.all_engine_barrier()


def shared_stage(chip, xn_dram, base_dram, w1, b1, w2, b2, w3, b3, dst):
    nc, D, KD = chip.nc, chip.D, chip.KD
    n_sh, _, H = w1.shape
    HM = H // P
    U = n_sh * HM
    NC = xn_dram.shape[0] // 512
    view = lambda a: a.rearrange("(t p) d -> p t d", p=P)
    with ExitStack() as st:
        sb = lambda n, s, d=FP32: st.enter_context(nc.sbuf_tensor(f"s_{n}", s, d))
        pb = lambda n, s: st.enter_context(nc.psum_tensor(f"s_{n}", s, FP32))
        W1 = [sb(f"w1{p}", [P, n_sh, KD, H], FR) for p in "hl"]
        W2 = [sb(f"w2{p}", [P, n_sh, KD, H], FR) for p in "hl"]
        W3 = [sb(f"w3{p}", [P, n_sh, HM, D], FR) for p in "hl"]
        raw = sb("raw", [P, 3, KD * H])
        B1, B2, B3 = sb("b1", [P, n_sh, HM]), sb("b2", [P, n_sh, HM]), sb("b3", [P, n_sh, D])
        rows, base = sb("rows", [P, 2, 4, D]), sb("base", [P, 2, 4, D])
        T = [sb(f"T{p}", [P, 2, KD, 512], FR) for p in "hl"]
        gate, hidden = sb("gate", [P, 2, 512]), sb("hidden", [P, 2, 512])
        hT = [sb(f"hT{p}", [P, U, 512], FR) for p in "hl"]
        Tps, up, acc = pb("Tps", [P, 2, 512]), pb("up", [P, 2, 2, 512]), pb("acc", [P, 2, 512])
        raw_loaded = chip.sems(st, *[f"s_raw_loaded{r}" for r in range(3)])
        rows_loaded = chip.sems(st, "s_rows_loaded0", "s_rows_loaded1")
        base_loaded = chip.sems(st, "s_base_loaded0", "s_base_loaded1")
        stored = chip.sems(st, "s_stored0", "s_stored1")
        (biases, w_hi, w_lo, b3_ready, t_done, t_hi, t_lo, up_done, gate_done, hid_done, hid_hi, hid_lo, acc_done,
         acc_free, base_ready) = every = chip.sems(
            st, *[f"s_{n}" for n in ("biases", "w_hi", "w_lo", "b3_ready", "t_done", "t_hi", "t_lo", "up_done",
                                     "gate_done", "hid_done", "hid_hi", "hid_lo", "acc_done", "acc_free",
                                     "base_ready")])
        loads = []
        for n in range(n_sh):
            for W, w in ((W1, w1), (W2, w2), (W3, w3)):
                loads.append((W, n, w[n].rearrange("(k p) h -> p k h", p=P)))
        parts_of = lambda W, n: [p[:, n, :, :].rearrange("p k h -> p (k h)") for p in W]

        with nc.Block() as block:

            @block.sync
            def _(sp):
                for c in range(2):
                    sp.dma_start(rows[:, c, :, :], view(xn_dram)[:, 4 * c:4 * c + 4, :]).then_inc(rows_loaded[c], 16)
                for q, (W, n, src) in enumerate(loads):
                    if q >= 3:
                        sp.wait_ge(w_lo, q - 2)
                    sp.dma_start(raw[:, q % 3, :].rearrange("p (k h) -> p k h", k=src.shape[1]), src
                                 ).then_inc(raw_loaded[q % 3], 16)
                    if q == 0:
                        sp.dma_start(B1[:], b1).then_inc(biases, 16)
                        sp.dma_start(B2[:], b2).then_inc(biases, 16)
                        sp.dma_start(B3[:], b3.rearrange("(o n) d -> o n d", o=1).to_broadcast([P, n_sh, D])
                                     ).then_inc(biases, 16)
                for c in range(NC):
                    r = c % 2
                    if c >= 2:
                        sp.wait_ge(t_done, KD * (c - 1))
                        sp.dma_start(rows[:, r, :, :], view(xn_dram)[:, 4 * c:4 * c + 4, :]
                                     ).then_inc(rows_loaded[r], 16)
                        sp.wait_ge(stored[r], 16 * (c // 2))
                    sp.dma_start(base[:, r, :, :], view(base_dram)[:, 4 * c:4 * c + 4, :]).then_inc(base_loaded[r], 16)

            @block.gpsimd
            def _(pool):
                pool.wait_ge(biases, 48)
                for n in range(1, n_sh):
                    nc.gpsimd.tensor_tensor(B3[:, 0, :], B3[:, 0, :], B3[:, n, :], ALU.add).then_inc(b3_ready, 1)
                    pool.wait_ge(b3_ready, n)
                nc.gpsimd.tensor_scalar(B3[:, 0, :], B3[:, 0, :], 1.0 / n_sh, 0.0, ALU.mult, ALU.add).then_inc(b3_ready, 1)
                pool.wait_ge(b3_ready, n_sh)
                for c in range(NC):
                    pool.wait_ge(base_loaded[c % 2], 16 * (c // 2 + 1))
                    slot = base[:, c % 2, :, :]
                    nc.gpsimd.tensor_tensor(slot, slot, B3[:, 0:1, :].to_broadcast([P, 4, D]), ALU.add
                                            ).then_inc(base_ready, 1)

            @block.scalar
            def _(act):
                def weights_hi(q):
                    W, n, _ = loads[q]
                    act.wait_ge(raw_loaded[q % 3], 16 * (q // 3 + 1))
                    nc.scalar.activation(parts_of(W, n)[0], raw[:, q % 3, :], ACT.Copy).then_inc(w_hi, 1)

                def tokens_hi(c):
                    for k in range(KD):
                        n = KD * c + k
                        act.wait_ge(t_done, n + 1)
                        if c >= 2 and k == 0:
                            act.wait_ge(up_done, 2 * U * (c - 1))
                        nc.scalar.activation(T[0][:, c % 2, k, :], Tps[:, n % 2, :], ACT.Copy).then_inc(t_hi, 1)

                tokens_hi(0)
                for q in range(3):
                    weights_hi(q)
                act.wait_ge(biases, 48)
                for c in range(NC):
                    for u in range(U):
                        n = c * U + u
                        e, m = divmod(u, HM)
                        act.wait_ge(up_done, 2 * n + 1)
                        if n >= 2:
                            act.wait_ge(hid_done, n - 1)
                        nc.scalar.activation(gate[:, n % 2, :], up[:, n % 2, 0, :], ACT.Silu,
                                             bias=B1[:, e, m:m + 1]).then_inc(gate_done, 1)
                        if c == 0 and u == 0:
                            for q in range(3, len(loads)):
                                weights_hi(q)
                        act.wait_ge(hid_done, n + 1)
                        if c and u == 0:
                            act.wait_ge(acc_done, 4 * c)
                        nc.scalar.activation(hT[0][:, u, :], hidden[:, n % 2, :], ACT.Copy).then_inc(hid_hi, 1)
                        if u == U // 2 and c + 1 < NC:
                            tokens_hi(c + 1)
                    if c:
                        act.wait_ge(acc_free, 4 * c)
                        act.dma_start(view(dst)[:, 4 * c - 4:4 * c, :], base[:, (c - 1) % 2, :, :]
                                      ).then_inc(stored[(c - 1) % 2], 16)
                act.wait_ge(acc_free, 4 * NC)
                act.dma_start(view(dst)[:, 4 * NC - 4:4 * NC, :], base[:, (NC - 1) % 2, :, :]
                              ).then_inc(stored[(NC - 1) % 2], 16)
                for r in range(2):
                    act.wait_ge(stored[r], 16 * (NC // 2))

            @block.vector
            def _(dve):
                def weights_lo(q):
                    W, n, _ = loads[q]
                    hi, lo = parts_of(W, n)
                    dve.wait_ge(w_hi, q + 1)
                    nc.vector.tensor_tensor(lo, raw[:, q % 3, :], hi.bitcast(FP32), ALU.subtract).then_inc(w_lo, 1)

                def tokens_lo(c):
                    for k in range(KD):
                        n = KD * c + k
                        dve.wait_ge(t_hi, n + 1)
                        nc.vector.tensor_tensor(T[1][:, c % 2, k, :], Tps[:, n % 2, :],
                                                T[0][:, c % 2, k, :].bitcast(FP32), ALU.subtract).then_inc(t_lo, 1)

                def results(c):
                    for j in range(4):
                        n = 4 * c + j
                        dve.wait_ge(acc_done, n + 1)
                        if j == 0:
                            dve.wait_ge(base_ready, c + 1)
                        slot = base[:, c % 2, j, :]
                        nc.vector.scalar_tensor_tensor(slot, acc[:, n % 2, 0:D], 1.0 / n_sh, slot, ALU.mult, ALU.add
                                                       ).then_inc(acc_free, 1)

                tokens_lo(0)
                for q in range(3):
                    weights_lo(q)
                dve.wait_ge(biases, 48)
                for c in range(NC):
                    for u in range(U):
                        n = c * U + u
                        e, m = divmod(u, HM)
                        if c == 0 and u == 1:
                            for q in range(3, len(loads)):
                                weights_lo(q)
                        dve.wait_ge(gate_done, n + 1)
                        dve.wait_ge(up_done, 2 * n + 2)
                        if n >= 2:
                            dve.wait_ge(hid_lo, n - 1)
                        nc.vector.scalar_tensor_tensor(hidden[:, n % 2, :], up[:, n % 2, 1, :], B2[:, e, m:m + 1],
                                                       gate[:, n % 2, :], ALU.add, ALU.mult).then_inc(hid_done, 1)
                        dve.wait_ge(hid_hi, n + 1)
                        nc.vector.tensor_tensor(hT[1][:, u, :], hidden[:, n % 2, :], hT[0][:, u, :].bitcast(FP32),
                                                ALU.subtract).then_inc(hid_lo, 1)
                        if u == U // 2 and c + 1 < NC:
                            tokens_lo(c + 1)
                    results(c)

            @block.tensor
            def _(pe):
                def tokens(c):
                    pe.wait_ge(rows_loaded[c % 2], 16 * (c // 2 + 1))
                    for k in range(KD):
                        n = KD * c + k
                        if n >= 2:
                            pe.wait_ge(t_lo, n - 1)
                        for j in range(4):
                            last = nc.tensor.transpose(Tps[:, n % 2, P * j:P * j + P],
                                                       rows[:, c % 2, j, P * k:P * k + P], chip.ident[:])
                        last.then_inc(t_done, 1)

                def down(c):
                    for j in range(4):
                        n = 4 * c + j
                        if n >= 2:
                            pe.wait_ge(acc_free, n - 1)
                        for u in range(U):
                            if j == 0:
                                pe.wait_ge(hid_lo, c * U + u + 1)
                            last = three_pass(nc, acc[:, n % 2, 0:D], [p[:, u, P * j:P * j + P] for p in hT],
                                              [p[:, u // HM, u % HM, :] for p in W3], u == 0, u == U - 1)
                        last.then_inc(acc_done, 1)

                tokens(0)
                for c in range(NC):
                    pe.wait_ge(t_lo, KD * (c + 1))
                    for u in range(U):
                        n = c * U + u
                        e, m = divmod(u, HM)
                        if n >= 2:
                            pe.wait_ge(hid_done, n - 1)
                        for half, W in enumerate((W1, W2)):
                            if c == 0 and m == 0:
                                pe.wait_ge(w_lo, 3 * e + half + 1)
                            for k in range(KD):
                                last = three_pass(nc, up[:, n % 2, half, :], [p[:, e, k, P * m:P * m + P] for p in W],
                                                  [p[:, c % 2, k, :] for p in T], k == 0, k == KD - 1)
                            last.then_inc(up_done, 1)
                        if u == U // 2 and c + 1 < NC:
                            tokens(c + 1)
                    if c == 0:
                        pe.wait_ge(w_lo, len(loads))
                    down(c)

        for s in [*raw_loaded, *rows_loaded, *base_loaded, *stored, *every]:
            nc.sync.sem_clear(s)
    nc.all_engine_barrier()


def routed_stage(chip, sorted_dram, w1, w2, w3, b1, b2, b3, tile_expert, tile_rows, dst):
    nc, D, KD = chip.nc, chip.D, chip.KD
    E, _, H = w1.shape
    HM = H // P
    TILES = tile_expert.shape[1]
    WB = 2 * H + D
    with ExitStack() as st:
        sb = lambda n, s, d=FP32: st.enter_context(nc.sbuf_tensor(f"r_{n}", s, d))
        pb = lambda n, s: st.enter_context(nc.psum_tensor(f"r_{n}", s, FP32))
        W1 = [sb(f"w1{p}", [P, E, KD, H], FR) for p in "hl"]
        W2 = [sb(f"w2{p}", [P, E, KD, H], FR) for p in "hl"]
        W3 = sb("w3", [P, E, HM, D])
        raw = sb("raw", [P, 2, KD * H])
        brows = sb("brows", [64, WB], FR)
        ones = sb("ones", [64, P])
        sel = sb("sel", [64, 2, P], FR)
        rows, out = sb("rows", [P, 2, D]), sb("out", [P, 2, D])
        T = [sb(f"T{p}", [P, 2, KD, P], FR) for p in "hl"]
        gate_hidden, hT = sb("gate_hidden", [P, 4, H]), sb("hT", [P, 2, HM, P])
        gate, hidden = gate_hidden[:, 0:2, :], gate_hidden[:, 2:4, :]
        raw_b = gate_hidden[0:64, :, :].rearrange("p a h -> p (a h)")[:, 0:WB]
        b_hi = raw[0:64, :, :].rearrange("p a h -> p (a h)")[:, 0:WB].bitcast(FR)
        up, Tps, Gps, acc = (pb("up", [P, 2, 2, H]), pb("Tps", [P, KD, P]), pb("Gps", [P, HM, P]),
                             pb("acc", [P, 2, 512]))
        raw_loaded = chip.sems(st, *[f"r_raw_loaded{r}" for r in range(2)])
        rows_loaded = chip.sems(st, "r_rows_loaded0", "r_rows_loaded1")
        stored = chip.sems(st, "r_stored0", "r_stored1")
        (w3_loaded, b_loaded, w_hi, w_lo, b_zero, b_split, sel_ready, t_done, t_hi, t_lo, up_done, gate_done,
         hid_done, g_done, g_copied, acc_done, out_ready) = every = chip.sems(
            st, *[f"r_{n}" for n in ("w3_loaded", "b_loaded", "w_hi", "w_lo", "b_zero", "b_split", "sel_ready",
                                     "t_done", "t_hi", "t_lo", "up_done", "gate_done", "hid_done", "g_done",
                                     "g_copied", "acc_done", "out_ready")])
        loads = [(W, w[e]) for e in range(E) for W, w in ((W1, w1), (W2, w2))]
        flat = lambda a: a.rearrange("p k h -> p (k h)")

        def pairs(engine, body):
            for j in range(2):
                body(j, j, True, False)
            with engine.Fori(1, TILES // 2 - 1) as i:
                for j in range(2):
                    body(2 * i + j, j, False, False)
            for j in range(2):
                body(TILES - 2 + j, j, False, j == 1)

        with nc.Block() as block:

            @block.sync
            def _(sp):
                sp.wait_ge(b_zero, 2)
                for half in range(2):
                    for col, b in ((0, b1), (H, b2), (2 * H, b3)):
                        sp.dma_start(raw_b[32 * half:32 * half + E, col:col + b.shape[1]], b).then_inc(b_loaded, 16)
                sp.wait_ge(b_split, 3)
                for q, (W, w) in enumerate(loads):
                    if q >= 2:
                        sp.wait_ge(w_lo, q - 1)
                    sp.dma_start(raw[:, q % 2, :].rearrange("p (k h) -> p k h", k=KD),
                                 w.rearrange("(k p) h -> p k h", p=P)).then_inc(raw_loaded[q % 2], 16)
                    if q % 2:
                        e = q // 2
                        sp.dma_start(W3[:, e, :, :], w3[e].rearrange("(k p) d -> p k d", p=P)).then_inc(w3_loaded, 16)

                def store(n, j):
                    sp.dma_start(dst[bass.ds(n * P, P), :], out[:, j, :]).then_inc(stored[j], 16)

                def body(n, j, first, last):
                    if not first:
                        sp.wait_ge(t_done, n - 1)
                    sp.dma_start(rows[:, j, :], sorted_dram[bass.ds(n * P, P), :]).then_inc(rows_loaded[j], 16)
                    if not first:
                        sp.wait_ge(out_ready, n - 1)
                        store(n - 2, j)

                pairs(sp, body)
                for n in (TILES - 2, TILES - 1):
                    sp.wait_ge(out_ready, n + 1)
                    store(n, n % 2)
                for j in range(2):
                    sp.wait_ge(stored[j], 16 * (TILES // 2))

            @block.gpsimd
            def _(pool):
                nc.gpsimd.memset(ones[:], 1.0).then_inc(b_zero, 1)
                nc.gpsimd.memset(raw_b, 0.0).then_inc(b_zero, 1)

            @block.scalar
            def _(act):
                act.wait_ge(b_loaded, 96)
                nc.scalar.activation(b_hi, raw_b, ACT.Copy).then_inc(b_split, 1)
                for q, (W, _) in enumerate(loads):
                    act.wait_ge(raw_loaded[q % 2], 16 * (q // 2 + 1))
                    nc.scalar.activation(flat(W[0][:, q // 2, :, :]), raw[:, q % 2, :], ACT.Copy).then_inc(w_hi, 1)

                def tokens_hi(n, j, first):
                    act.wait_ge(t_done, n + 1)
                    if not first:
                        act.wait_ge(up_done, 2 * n - 2)
                    nc.scalar.activation(T[0][:, j, :, :], Tps[:], ACT.Copy).then_inc(t_hi, 1)

                def body(n, j, first, last):
                    if not last:
                        tokens_hi(n + 1, 1 - j, first and j == 0)
                    act.wait_ge(up_done, 2 * n + 1)
                    if not first:
                        act.wait_ge(hid_done, n - 1)
                    nc.scalar.activation(gate[:, j, :], up[:, j, 0, :], ACT.Silu).then_inc(gate_done, 1)
                    if not (first and j == 0):
                        copied(n - 1, 1 - j, first)

                def copied(n, j, first):
                    act.wait_ge(g_done, n + 1)
                    if not first:
                        act.wait_ge(acc_done, n - 1)
                    nc.scalar.activation(hT[:, j, :, :], Gps[:], ACT.Copy).then_inc(g_copied, 1)

                tokens_hi(0, 0, True)
                pairs(act, body)
                copied(TILES - 1, 1, False)

            @block.vector
            def _(dve):
                dve.wait_ge(b_split, 1)
                nc.vector.tensor_copy(brows[0:32, :], b_hi[0:32, :].bitcast(FP32)).then_inc(b_split, 1)
                nc.vector.tensor_tensor(brows[32:64, :], raw_b[32:64, :], b_hi[32:64, :].bitcast(FP32),
                                        ALU.subtract).then_inc(b_split, 1)
                for q, (W, _) in enumerate(loads):
                    dve.wait_ge(w_hi, q + 1)
                    nc.vector.tensor_tensor(flat(W[1][:, q // 2, :, :]), raw[:, q % 2, :],
                                            flat(W[0][:, q // 2, :, :]).bitcast(FP32), ALU.subtract).then_inc(w_lo, 1)

                def select(n, j, first):
                    if not first:
                        dve.wait_ge(up_done, 2 * n - 2)
                    nc.vector.tensor_scalar(sel[:, j, :], ones[:], tile_rows[:, bass.ds(n, 1)], None, ALU.mult
                                            ).then_inc(sel_ready, 1)

                def tokens_lo(n, j):
                    dve.wait_ge(t_hi, n + 1)
                    nc.vector.tensor_tensor(T[1][:, j, :, :], Tps[:], T[0][:, j, :, :].bitcast(FP32), ALU.subtract
                                            ).then_inc(t_lo, 1)

                def output(n, j, first):
                    dve.wait_ge(acc_done, n + 1)
                    if not first:
                        dve.wait_ge(stored[j], 8 * (n - j))
                    nc.vector.tensor_copy(out[:, j, :], acc[:, j, 0:D]).then_inc(out_ready, 1)

                def body(n, j, first, last):
                    if not last:
                        select(n + 1, 1 - j, first and j == 0)
                        tokens_lo(n + 1, 1 - j)
                    dve.wait_ge(gate_done, n + 1)
                    dve.wait_ge(up_done, 2 * n + 2)
                    if not first:
                        dve.wait_ge(g_done, n - 1)
                    nc.vector.tensor_tensor(hidden[:, j, :], up[:, j, 1, :], gate[:, j, :], ALU.mult
                                            ).then_inc(hid_done, 1)
                    if not (first and j == 0):
                        output(n - 1, 1 - j, first)

                dve.wait_ge(b_zero, 2)
                select(0, 0, True)
                tokens_lo(0, 0)
                pairs(dve, body)
                output(TILES - 1, 1, False)

            @block.tensor
            def _(pe):
                def tokens(n, j, loaded):
                    pe.wait_ge(rows_loaded[j], loaded)
                    for k in range(KD):
                        last = nc.tensor.transpose(Tps[:, k, :], rows[:, j, P * k:P * k + P], chip.ident[:])
                    last.then_inc(t_done, 1)

                def down(n, j, first):
                    pe.wait_ge(hid_done, n + 1)
                    if not (first and j == 0):
                        pe.wait_ge(g_copied, n)
                    for k in range(HM):
                        last = nc.tensor.transpose(Gps[:, k, :], hidden[:, j, P * k:P * k + P], chip.ident[:])
                    last.then_inc(g_done, 1)
                    expert = expert_of(n)
                    pe.wait_ge(g_copied, n + 1)
                    for k in range(HM):
                        last = nc.tensor.matmul(acc[:, j, 0:D], hT[:, j, k, :], W3[:, bass.ds(expert, 1), k, :],
                                                start=False, stop=k == HM - 1)
                    last.then_inc(acc_done, 1)

                def expert_of(n):
                    return nc.tensor.value_load(tile_expert[0:1, bass.ds(n, 1)], min_val=0, max_val=E - 1)

                def body(n, j, first, last):
                    if not last:
                        pe.wait_ge(t_lo, n + 1)
                        tokens(n + 1, 1 - j, 8 * (n + 1 - (1 - j)) + 16)
                    expert = expert_of(n)
                    pe.wait_ge(t_lo, n + 1)
                    pe.wait_ge(sel_ready, n + 1)
                    if not first:
                        pe.wait_ge(hid_done, n - 1)
                    for half, W in enumerate((W1, W2)):
                        bank = up[:, j, half, :]
                        nc.tensor.matmul(bank, sel[:, j, :], brows[:, half * H:half * H + H], start=True, stop=False)
                        for k in range(KD):
                            last_up = three_pass(nc, bank, [p[:, j, k, :] for p in T],
                                                 [p[:, bass.ds(expert, 1), k, :] for p in W], False, k == KD - 1)
                        if half == 0:
                            last_up.then_inc(up_done, 1)
                            if not first:
                                pe.wait_ge(out_ready, n - 1)
                            nc.tensor.matmul(acc[:, j, 0:D], sel[:, j, :], brows[:, 2 * H:WB], start=True, stop=False)
                    last_up.then_inc(up_done, 1)
                    if not (first and j == 0):
                        down(n - 1, 1 - j, first)

                pe.wait_ge(w_lo, len(loads))
                pe.wait_ge(w3_loaded, 16 * E)
                pe.wait_ge(b_split, 3)
                tokens(0, 0, 16)
                pairs(pe, body)
                down(TILES - 1, 1, False)

        for s in [*raw_loaded, *rows_loaded, *stored, *every]:
            nc.sync.sem_clear(s)
    nc.all_engine_barrier()


def rank_stage(chip, scores, router_b, w_dram, picked, row_index, picked_row, thresholds, limit):
    nc, NT, B = chip.nc, chip.NT, chip.B
    NA, S = scores.shape[1], chip.S
    K = 2 * P
    with ExitStack() as st:
        sb = lambda n, s, d=FP32: st.enter_context(nc.sbuf_tensor(f"k_{n}", s, d))
        pb = lambda n, s: st.enter_context(nc.psum_tensor(f"k_{n}", s, FP32))
        w, wT = sb("w", [P, NA]), sb("wT", [NA, P])
        row = sb("row", [P, B, S])
        junk, junk2 = sb("junk", [P, S]), sb("junk2", [P, P])
        earlier, last_row = sb("earlier", [P, P]), sb("last_row", [P, P])
        counts, rank = sb("counts", [P, NA, 3]), sb("rank", [P, NA])
        rank_no, index_cols = sb("rank_no", [P, K]), sb("index_cols", [P, NT, P])
        pairs = sb("pairs", [P, NA, 2])
        hot = sb("hot", [P, 4, K])
        clamped = sb("clamped", [P, B, 2])
        wT_ps = pb("wT_ps", [NA, P])
        list_ps = pb("list_ps", [P, 2, 512])
        row_ps, thr_ps = pb("row_ps", [P, K]), pb("thr_ps", [P, 1])
        (made, w_ready, wT_done, wT_copied, w_stored, row_loaded, chain, hot_ready, hot_used, listed, list_copied,
         thr_done) = every = chip.sems(
            st, *[f"k_{n}" for n in ("made", "w_ready", "wT_done", "wT_copied", "w_stored", "row_loaded", "chain",
                                     "hot_ready", "hot_used", "listed", "list_copied", "thr_done")])

        with nc.Block() as block:

            @block.gpsimd
            def _(pool):
                g = nc.gpsimd
                g.memset(earlier[:], 0.0).then_inc(made, 1)
                g.memset(last_row[:], 0.0).then_inc(made, 1)
                g.iota(rank_no[:], pattern=[[1, K]], base=0, channel_multiplier=0,
                       allow_small_or_imprecise_dtypes=True).then_inc(made, 1)
                g.iota(index_cols[:], pattern=[[P, NT], [0, P]], base=0, channel_multiplier=1,
                       allow_small_or_imprecise_dtypes=True).then_inc(made, 1)
                pool.wait_ge(made, 4)
                g.affine_select(out=earlier[:], in_=earlier[:], compare_op=ALU.is_ge, fill=1.0, base=0,
                                pattern=[[1, P]], channel_multiplier=-1).then_inc(made, 1)
                g.affine_select(out=last_row[:], in_=last_row[:], compare_op=ALU.not_equal, fill=1.0, base=-(P - 1),
                                pattern=[[0, P]], channel_multiplier=1).then_inc(made, 1)

            @block.sync
            def _(sp):
                sp.wait_ge(wT_copied, 1)
                sp.dma_start(w_dram.rearrange("(t p) -> t p", p=P), wT[:]).then_inc(w_stored, 16)
                sp.wait_ge(w_stored, 16)
                sp.dma_start(row[:].rearrange("p b s -> p (b s)"),
                             w_dram.rearrange("(o n) -> o n", o=1).to_broadcast([P, B * S])).then_inc(row_loaded, 16)

            @block.vector
            def _(dve):
                V = nc.vector
                links = [0]

                def link(ins):
                    links[0] += 1
                    ins.then_inc(chain, 1)
                    dve.wait_ge(chain, links[0])

                V.tensor_scalar(w[:], scores[:, :, 0], router_b[:], None, ALU.add).then_inc(w_ready, 1)
                dve.wait_ge(wT_done, 1)
                V.tensor_copy(wT[:], wT_ps[:]).then_inc(wT_copied, 1)
                dve.wait_ge(made, 6)
                V.tensor_copy(pairs[:, :, 1], w[:])
                for b in range(B):
                    link(V.tensor_copy(pairs[:, b * NT:(b + 1) * NT, 0], index_cols[:, :, 0]))
                link(V.memset(counts[:], 0.0))
                dve.wait_ge(row_loaded, 16)
                for b in range(B):
                    for i in range(NT):
                        t = b * NT + i
                        mine = w[:, t:t + 1]
                        if i:
                            V.tensor_scalar(junk[:, 0:P * i], row[:, b, 0:P * i], mine, None, ALU.is_ge, ALU.add,
                                            accum_out=counts[:, t, 0:1])
                        V.tensor_scalar(junk[:, P * i:S], row[:, b, P * i:S], mine, None, ALU.is_gt, ALU.add,
                                        accum_out=counts[:, t, 1:2])
                        ins = V.scalar_tensor_tensor(junk2[:], row[:, b, P * i:P * i + P], mine, earlier[:],
                                                     ALU.is_equal, ALU.mult, accum_out=counts[:, t, 2:3])
                        link(ins)
                link(V.tensor_reduce(rank[:], counts[:], AX.X, ALU.add))
                for b in range(B):
                    for i in range(NT):
                        t = b * NT + i
                        if t >= 4:
                            dve.wait_ge(hot_used, t - 3)
                        V.tensor_scalar(hot[:, t % 4, :], rank_no[:], rank[:, t:t + 1], None, ALU.is_equal
                                        ).then_inc(hot_ready, 1)
                    dve.wait_ge(listed, b + 1)
                    V.tensor_copy(picked[:, b, :, :], list_ps[:, :, 0:2])
                    V.tensor_scalar_min(picked_row[:, b, :], row_ps[:], float(limit)).then_inc(list_copied, 1)
                    dve.wait_ge(list_copied, b + 1)
                    link(V.tensor_scalar_add(row_index[:, b, :, 0], picked[:, b, :, 0], float(b * S)))
                    link(V.tensor_scalar(clamped[:, b, :], picked[:, b, :, 0], float(limit), float(b * (limit + 1)),
                                         ALU.min, ALU.add))
                    link(V.tensor_copy(row_index[:, b, :, 1], clamped[:, b, :]))
                    dve.wait_ge(thr_done, b + 1)
                    link(V.tensor_copy(thresholds[:, b:b + 1], thr_ps[:]))

            @block.tensor
            def _(pe):
                pe.wait_ge(w_ready, 1)
                nc.tensor.transpose(wT_ps[:], w[:], chip.ident[:]).then_inc(wT_done, 1)
                for b in range(B):
                    if b:
                        pe.wait_ge(list_copied, b)
                    for i in range(NT):
                        t = b * NT + i
                        pe.wait_ge(hot_ready, t + 1)
                        if i == 0 and b == 0:
                            pe.wait_ge(chain, B)
                        for h in range(2):
                            nc.tensor.matmul(list_ps[:, h, 0:2], hot[:, t % 4, P * h:P * h + P], pairs[:, t, :],
                                             start=i == 0, stop=i == NT - 1)
                        last = nc.tensor.matmul(row_ps[:], index_cols[:, i, :], hot[:, t % 4, :], start=i == 0,
                                                stop=i == NT - 1)
                        last.then_inc(hot_used, 1)
                        if i == NT - 1:
                            pe.wait_ge(hot_used, t + 1)
                            pe.sem_inc(listed, 1)
                    pe.wait_ge(list_copied, b + 1)
                    nc.tensor.matmul(thr_ps[:], last_row[:], picked[:, b, 1, 1:2], start=True, stop=True
                                     ).then_inc(thr_done, 1)

        for s in every:
            nc.sync.sem_clear(s)
    nc.all_engine_barrier()


def newton_rsqrt(nc, link, r, std, v, tmp):
    V = nc.vector
    link(V.reciprocal(r, std))
    link(V.tensor_tensor(tmp, r, r, ALU.mult))
    link(V.tensor_tensor(tmp, tmp, v, ALU.mult))
    link(V.tensor_scalar(tmp, tmp, -0.5, 1.5, ALU.mult, ALU.add))
    link(V.tensor_tensor(r, r, tmp, ALU.mult))


def picked_stage(chip, xn_dram, positions, mask, row_index, picked_row, picked, thresholds, inverse, ln1, ln2, w, w_ffn,
                 out_dram, HEADS):
    nc, B, D, KD = chip.nc, chip.B, chip.D, chip.KD
    G = 2 * B
    hd = D // HEADS
    HALF = hd // 2
    PAD = 32
    HG = P // PAD
    NH = HEADS // HG
    M = mask.shape[1]
    MT = M // P
    F = w_ffn["w1"][0].shape[2]
    FM = F // P
    TWO_PI = 6.283185307179586
    C1 = 6.28125
    C2 = round((TWO_PI - C1) * 2 ** 20) / 2 ** 20
    C3 = TWO_PI - C1 - C2
    PI_BELOW = 3.1415925

    with ExitStack() as outer:
        osb = lambda n, s, d=FP32: outer.enter_context(nc.sbuf_tensor(f"p_{n}", s, d))
        xs = osb("xs", [P, G, D])
        heads_T = {n: osb(f"{n}T", [P, G, NH, P]) for n in "qk"}
        vals = osb("vals", [P, G, D])
        msel = osb("msel", [P, G, 2 * P])
        o_all = osb("o_all", [P, G, D])
        small = lambda n: osb(n, [P, G])
        ss, vv, std, rr, tmp = (small(n) for n in ("ss", "vv", "std", "rr", "tmp"))

        with ExitStack() as st:
            sb = lambda n, s, d=FP32: st.enter_context(nc.sbuf_tensor(f"p_{n}", s, d))
            pb = lambda n, s: st.enter_context(nc.psum_tensor(f"p_{n}", s, FP32))
            pos, posf = sb("pos", [P, G], I32), sb("posf", [P, G])
            rows = sb("mask_rows", [P, 2, M])
            rowsT = sb("mask_rowsT", [P, MT, P])
            col_no = sb("col_no", [P, MT])
            hot = sb("col_hot", [P, MT, 2 * P])
            inv, ang, turns_i, turns = (sb("inv", [P, HALF]), sb("ang", [P, G, HALF]), sb("turns_i", [P, G, HALF], I32),
                                        sb("turns", [P, G, HALF]))
            ang2 = sb("ang2", [P, G, HALF])
            sin, cos = sb("sin", [P, G, HALF]), sb("cos", [P, G, HALF])
            sq, hn = sb("sq", [P, D]), sb("hn", [P, G, D])
            hT = [sb(f"hT{p}", [P, KD, G * P], FR) for p in "hl"]
            padded = sb("padded", [P, 2, HEADS, PAD])
            rot = [sb(f"rot{i}", [P, HEADS, HALF]) for i in range(2)]
            Tps, qkv = pb("Tps", [P, 2, 512]), pb("qkv", [P, 2, 512])
            Hps = pb("Hps", [P, 512])
            Mps, Sps = pb("Mps", [P, 2, 512]), pb("Sps", [P, 2 * P])
            m_loaded = chip.pool_sems("p_m_loaded0", "p_m_loaded1")
            x_loaded, p_loaded = chip.pool_sems("p_x_loaded", "p_p_loaded")
            (inv_loaded, made, chain, sq_done, v_ready, std_ready, hn_ready, t_done, t_hi, t_lo,
             qkv_done, qkv_read, pad_ready, ht_done, ht_copied, ang_ready, trig_ready, hot_ready, m_done, m_copied,
             s_done, s_copied) = every = chip.sems(
                st, *[f"p_{n}" for n in (
                    "inv_loaded", "made", "chain", "sq_done", "v_ready", "std_ready",
                    "hn_ready", "t_done", "t_hi", "t_lo", "qkv_done", "qkv_read", "pad_ready", "ht_done", "ht_copied",
                    "ang_ready", "trig_ready", "hot_ready", "m_done", "m_copied", "s_done", "s_copied")])
            offset = lambda g, which: bass.IndirectOffsetOnAxis(ap=row_index[:, g // 2, g % 2, which:which + 1], axis=0)

            value_bank = lambda g: Tps[:, g % 2, D:2 * D]

            with nc.Block() as block:

                @block.sync
                def _(sp):
                    sp.dma_start(inv[:], inverse.to_broadcast([P, HALF])).then_inc(inv_loaded, 16)

                @block.gpsimd
                def _(pool):
                    g_ = nc.gpsimd
                    for g in range(G):
                        g_.indirect_dma_start(out=xs[:, g, :], out_offset=None, in_=xn_dram[:, :],
                                              in_offset=offset(g, 0)).then_inc(x_loaded, 16)
                    for g in range(G):
                        g_.indirect_dma_start(out=pos[:, g:g + 1], out_offset=None, in_=positions[:, :],
                                              in_offset=offset(g, 1)).then_inc(p_loaded, 16)
                    g_.iota(col_no[:], pattern=[[P, MT]], base=0, channel_multiplier=1,
                            allow_small_or_imprecise_dtypes=True).then_inc(made, 1)
                    g_.memset(padded[:], 0.0).then_inc(made, 1)
                    for g in range(G):
                        if g >= 2:
                            pool.wait_ge(m_done, 2 * (g - 1))
                        g_.indirect_dma_start(out=rows[:, g % 2, :], out_offset=None, in_=mask[:, :],
                                              in_offset=offset(g, 1)).then_inc(m_loaded[g % 2], 16)

                @block.scalar
                def _(act):
                    act.wait_ge(x_loaded, 16 * G)
                    for g in range(G):
                        if g:
                            act.wait_ge(sq_done, g)
                        nc.scalar.activation(sq[:], xs[:, g, :], ACT.Square, accum_out=ss[:, g:g + 1]
                                             ).then_inc(sq_done, 1)
                    act.wait_ge(v_ready, 1)
                    nc.scalar.activation(std[:], vv[:], ACT.Sqrt).then_inc(std_ready, 1)
                    for g in range(G):
                        act.wait_ge(t_done, g + 1)
                        for k in range(KD):
                            nc.scalar.activation(hT[0][:, k, P * g:P * g + P], Tps[:, g % 2, P * k:P * k + P], ACT.Copy,
                                                 scale=ln1[:, k:k + 1]).then_inc(t_hi, 1)
                    act.wait_ge(ang_ready, 1)
                    nc.scalar.activation(sin[:], ang[:], ACT.Sin).then_inc(trig_ready, 1)
                    nc.scalar.activation(cos[:], ang2[:], ACT.Sin).then_inc(trig_ready, 1)
                    n = 0
                    for g in range(G):
                        act.wait_ge(qkv_done, 3 * g + 3)
                        nc.scalar.activation(vals[:, g, :], value_bank(g), ACT.Copy
                                             ).then_inc(qkv_read, 1)
                        for i, name in enumerate("qk"):
                            n += 1
                            act.wait_ge(ht_done, n)
                            nc.scalar.activation(heads_T[name][:, g, :, :], Hps[:].rearrange("p (a q) -> p a q", a=NH),
                                                 ACT.Copy).then_inc(ht_copied, 1)

                @block.vector
                def _(dve):
                    V = nc.vector
                    links = [0]

                    def link(ins):
                        links[0] += 1
                        ins.then_inc(chain, 1)
                        dve.wait_ge(chain, links[0])

                    dve.wait_ge(sq_done, G)
                    link(V.tensor_scalar(vv[:], ss[:], 1.0 / D, 1e-6, ALU.mult, ALU.add))
                    V.tensor_copy(tmp[:], vv[:]).then_inc(v_ready, 1)
                    dve.wait_ge(std_ready, 1)
                    newton_rsqrt(nc, link, rr[:], std[:], vv[:], tmp[:])
                    for g in range(G):
                        V.tensor_scalar(hn[:, g, :], xs[:, g, :], rr[:, g:g + 1], None, ALU.mult).then_inc(hn_ready, 1)
                    dve.wait_ge(p_loaded, 16 * G)
                    dve.wait_ge(inv_loaded, 16)
                    link(V.tensor_copy(posf[:], pos[:]))
                    wide = lambda a: a.rearrange("p (g o) -> p g o", o=1).to_broadcast([P, G, HALF])
                    link(V.tensor_tensor(ang[:], wide(posf[:]),
                                         inv[:].rearrange("p (o h) -> p o h", o=1).to_broadcast([P, G, HALF]), ALU.mult))
                    flat = lambda a: a[:].rearrange("p g h -> p (g h)")
                    link(V.tensor_scalar(flat(turns_i), flat(ang), 1.0 / TWO_PI, None, ALU.mult))
                    link(V.tensor_copy(turns[:], turns_i[:]))
                    for c in (C1, C2, C3):
                        link(V.scalar_tensor_tensor(flat(ang), flat(turns), -c, flat(ang), ALU.mult, ALU.add))
                    link(V.tensor_scalar_add(flat(ang2), flat(ang), TWO_PI / 4))
                    link(V.tensor_scalar(flat(turns), flat(ang2), TWO_PI / 2, -TWO_PI, ALU.is_gt, ALU.mult))
                    link(V.tensor_tensor(flat(ang2), flat(ang2), flat(turns), ALU.add))
                    for a in (ang, ang2):
                        link(V.tensor_scalar(flat(a), flat(a), PI_BELOW, -PI_BELOW, ALU.min, ALU.max))
                    V.tensor_copy(flat(turns), flat(ang2)).then_inc(ang_ready, 1)
                    for g in range(G):
                        for k in range(KD):
                            dve.wait_ge(t_hi, KD * (g + 1))
                            cols = slice(P * g, P * g + P)
                            V.scalar_tensor_tensor(hT[1][:, k, cols], Tps[:, g % 2, P * k:P * k + P], ln1[:, k:k + 1],
                                                   hT[0][:, k, cols].bitcast(FP32), ALU.mult, ALU.subtract
                                                   ).then_inc(t_lo, 1)
                    dve.wait_ge(trig_ready, 2)
                    dve.wait_ge(made, 2)
                    n = 0
                    for g in range(G):
                        bc = lambda a: a[:, g:g + 1, :].to_broadcast([P, HEADS, HALF])
                        for i, name in enumerate("qk"):
                            dve.wait_ge(qkv_done, 3 * g + i + 1)
                            t = qkv[:, i, 0:D].rearrange("p (h c) -> p h c", h=HEADS)
                            t1, t2 = t[:, :, 0:HALF], t[:, :, HALF:hd]
                            if n >= 2:
                                dve.wait_ge(ht_done, n - 1)
                            out = padded[:, i, :, :]
                            link(V.tensor_tensor(rot[0][:], t1, bc(cos), ALU.mult))
                            link(V.tensor_tensor(rot[1][:], t2, bc(sin), ALU.mult))
                            link(V.tensor_tensor(out[:, :, 0:HALF], rot[0][:], rot[1][:], ALU.subtract))
                            link(V.tensor_tensor(rot[0][:], t2, bc(cos), ALU.mult))
                            link(V.tensor_tensor(rot[1][:], t1, bc(sin), ALU.mult))
                            V.tensor_tensor(out[:, :, HALF:hd], rot[0][:], rot[1][:], ALU.add).then_inc(pad_ready, 1)
                            n += 1
                            dve.wait_ge(pad_ready, n)
                    for b in range(B):
                        if b:
                            dve.wait_ge(s_done, 2 * b)
                        for c in range(MT):
                            ins = V.tensor_scalar(hot[:, c, :], picked_row[:, b, :], col_no[:, c:c + 1], None,
                                                  ALU.is_equal)
                        ins.then_inc(hot_ready, 1)
                        for g in (2 * b, 2 * b + 1):
                            for h in range(2):
                                dve.wait_ge(m_done, 2 * g + h + 1)
                                if g and h == 0:
                                    dve.wait_ge(s_done, g)
                                V.tensor_copy(rowsT[:, 4 * h:4 * h + 4, :].rearrange("p a q -> p (a q)"), Mps[:, h, :]
                                              ).then_inc(m_copied, 1)
                            dve.wait_ge(s_done, g + 1)
                            link(V.tensor_copy(msel[:, g, :], Sps[:]))
                            V.memset(msel[:, g, 2 * P - 1:2 * P], MASKED).then_inc(s_copied, 1)

                @block.tensor
                def _(pe):
                    for g in range(G):
                        pe.wait_ge(hn_ready, g + 1)
                        if g >= 2:
                            pe.wait_ge(t_lo, KD * (g - 1))
                        for k in range(KD):
                            last = nc.tensor.transpose(Tps[:, g % 2, P * k:P * k + P], hn[:, g, P * k:P * k + P],
                                                       chip.ident[:])
                        last.then_inc(t_done, 1)
                    pe.wait_ge(t_lo, KD * G)
                    pe.wait_ge(made, 2)
                    n = 0
                    for g in range(G):
                        for i, name in enumerate(("wq", "wk", "wv")):
                            bank = qkv[:, i, 0:D] if i < 2 else value_bank(g)
                            if g and i < 2:
                                pe.wait_ge(pad_ready, 2 * g - 1 + i)
                            if g >= 2 and i == 2:
                                pe.wait_ge(qkv_read, g - 1)
                            for k in range(KD):
                                last = three_pass(nc, bank, [p[:, k, P * g:P * g + P] for p in hT],
                                                  [p[:, k, :] for p in w[name]], k == 0, k == KD - 1)
                            last.then_inc(qkv_done, 1)
                        for i in range(2):
                            pe.wait_ge(pad_ready, n + 1)
                            if n:
                                pe.wait_ge(ht_copied, n)
                            for a in range(NH):
                                src = padded[:, i, HG * a:HG * a + HG, :].rearrange("p h c -> p (h c)")
                                last = nc.tensor.transpose(Hps[:, P * a:P * a + P], src, chip.ident[:])
                            last.then_inc(ht_done, 1)
                            n += 1
                    for g in range(G):
                        pe.wait_ge(m_loaded[g % 2], 16 * (g // 2 + 1))
                        for h in range(2):
                            if g:
                                pe.wait_ge(m_copied, 2 * g - 1 + h)
                            for c in range(4):
                                last = nc.tensor.transpose(Mps[:, h, P * c:P * c + P],
                                                           rows[:, g % 2, P * (4 * h + c):P * (4 * h + c) + P],
                                                           chip.ident[:])
                            last.then_inc(m_done, 1)
                        pe.wait_ge(m_copied, 2 * g + 2)
                        pe.wait_ge(hot_ready, g // 2 + 1)
                        if g:
                            pe.wait_ge(s_copied, g)
                        for c in range(MT):
                            last = nc.tensor.matmul(Sps[:], rowsT[:, c, :], hot[:, c, :], start=c == 0, stop=c == MT - 1)
                        last.then_inc(s_done, 1)

            for s in [*m_loaded, x_loaded, p_loaded, *every]:
                nc.sync.sem_clear(s)
        nc.all_engine_barrier()

        with ExitStack() as st:
            sb = lambda n, s, d=FP32: st.enter_context(nc.sbuf_tensor(f"p_{n}", s, d))
            pb = lambda n, s: st.enter_context(nc.psum_tensor(f"p_{n}", s, FP32))
            masked, probs = sb("masked", [P, 2, 2, 2 * P]), sb("probs", [P, 2, 2, 2 * P])
            neg_max, sums = sb("neg_max", [P, G, HEADS]), sb("sums", [P, G, HEADS])
            pT = sb("pT", [P, 2, 4, P])
            S_ps, T_ps, O_ps = pb("S_ps", [P, 2, 2, 2 * P]), pb("T_ps", [P, 2, 4, P]), pb("O_ps", [P, 2, 512])
            (qk_done, masked_ready, max_done, exp_done, pt_done, pt_copied, pv_done, o_read, chain) = every = chip.sems(
                st, *[f"p_{n}" for n in ("qk_done", "masked_ready", "max_done", "exp_done", "pt_done", "pt_copied",
                                         "pv_done", "o_read", "chain2")])
            NP = HEADS // 2
            units = [(g, h2) for g in range(G) for h2 in range(NP)]
            head = lambda h2, j: (2 * (h2 // HG) + j) * HG + h2 % HG

            with nc.Block() as block:

                @block.tensor
                def _(pe):
                    def scores(n):
                        g, h2 = units[n]
                        if n >= 2:
                            pe.wait_ge(masked_ready, n - 1)
                        for j in range(2):
                            a, r = divmod(head(h2, j), HG)
                            rows_ = slice(PAD * r, PAD * r + PAD)
                            keys = heads_T["k"][rows_, 2 * (g // 2):2 * (g // 2) + 2, a, :]
                            last = nc.tensor.matmul(S_ps[:, n % 2, j, :].rearrange("p (t k) -> p t k", t=2),
                                                    heads_T["q"][rows_, g, a, :], keys, start=True, stop=True)
                        last.then_inc(qk_done, 1)

                    def products(n):
                        g, h2 = units[n]
                        pe.wait_ge(exp_done, 2 * n + 2)
                        if n >= 2:
                            pe.wait_ge(pt_copied, n - 1)
                        for j in range(2):
                            for t in range(2):
                                last = nc.tensor.transpose(T_ps[:, n % 2, 2 * j + t, :],
                                                           probs[:, n % 2, j, P * t:P * t + P], chip.ident[:])
                        last.then_inc(pt_done, 1)

                    def values(n):
                        g, h2 = units[n]
                        pe.wait_ge(pt_copied, n + 1)
                        if h2 == 0 and g >= 2:
                            pe.wait_ge(o_read, g - 1)
                        for j in range(2):
                            h = head(h2, j)
                            for t in range(2):
                                last = nc.tensor.matmul(O_ps[:, g % 2, hd * h:hd * h + hd], pT[:, n % 2, 2 * j + t, :],
                                                        vals[:, 2 * (g // 2) + t, hd * h:hd * h + hd],
                                                        start=t == 0, stop=t == 1)
                        last.then_inc(pv_done, 1)

                    N = len(units)
                    for n in range(N + 2):
                        if n < N:
                            scores(n)
                        if 1 <= n <= N:
                            products(n - 1)
                        if n >= 2:
                            values(n - 2)

                @block.vector
                def _(dve):
                    V = nc.vector
                    links = [0]

                    def link(ins):
                        links[0] += 1
                        ins.then_inc(chain, 1)
                        dve.wait_ge(chain, links[0])

                    def finish(g):
                        dve.wait_ge(pv_done, NP * (g + 1))
                        dve.wait_ge(exp_done, 2 * NP * (g + 1))
                        link(V.reciprocal(sums[:, g, :], sums[:, g, :]))
                        V.tensor_tensor(o_all[:, g, :].rearrange("p (h c) -> p h c", h=HEADS),
                                        O_ps[:, g % 2, 0:D].rearrange("p (h c) -> p h c", h=HEADS),
                                        sums[:, g, :].rearrange("p (h o) -> p h o", o=1).to_broadcast([P, HEADS, hd]),
                                        ALU.mult).then_inc(o_read, 1)

                    for n, (g, h2) in enumerate(units):
                        dve.wait_ge(qk_done, n + 1)
                        if n >= 2:
                            dve.wait_ge(exp_done, 2 * n - 2)
                        V.tensor_tensor(masked[:, n % 2, :, :], S_ps[:, n % 2, :, :],
                                        msel[:, g:g + 1, :].to_broadcast([P, 2, 2 * P]), ALU.add
                                        ).then_inc(masked_ready, 1)
                        dve.wait_ge(masked_ready, n + 1)
                        V.tensor_reduce(neg_max[:, g, 2 * h2:2 * h2 + 2], masked[:, n % 2, :, :], AX.X, ALU.max,
                                        negate=True).then_inc(max_done, 1)
                        if h2 == 3 and g:
                            finish(g - 1)
                    finish(G - 1)

                @block.scalar
                def _(act):
                    def exponentials(n):
                        g, h2 = units[n]
                        act.wait_ge(max_done, n + 1)
                        if n >= 2:
                            act.wait_ge(pt_done, n - 1)
                        for j in range(2):
                            h = head(h2, j)
                            nc.scalar.activation(probs[:, n % 2, j, :], masked[:, n % 2, j, :], ACT.Exp,
                                                 bias=neg_max[:, g, 2 * h2 + j:2 * h2 + j + 1], accum_out=sums[:, g, h:h + 1]
                                                 ).then_inc(exp_done, 1)

                    def copies(n):
                        act.wait_ge(pt_done, n + 1)
                        if n >= 2:
                            act.wait_ge(pv_done, n - 1)
                        nc.scalar.activation(pT[:, n % 2, :, :], T_ps[:, n % 2, :, :], ACT.Copy).then_inc(pt_copied, 1)

                    for n in range(len(units) + 1):
                        if n < len(units):
                            exponentials(n)
                        if n:
                            copies(n - 1)

            for s in every:
                nc.sync.sem_clear(s)
        nc.all_engine_barrier()

        with ExitStack() as st:
            sb = lambda n, s, d=FP32: st.enter_context(nc.sbuf_tensor(f"p_{n}", s, d))
            pb = lambda n, s: st.enter_context(nc.psum_tensor(f"p_{n}", s, FP32))
            oT = [sb(f"oT{p}", [P, KD, G * P], FR) for p in "hl"]
            fT = [sb(f"fT{p}", [P, KD, G * P], FR) for p in "hl"]
            x1, hn, sq = sb("x1", [P, G, D]), sb("hn2", [P, G, D]), sb("sq2", [P, D])
            gel = sb("gel", [P, 2, G * P])
            gT = [sb(f"gT{p}", [P, FM, G * P], FR) for p in "hl"]
            delta, sel = sb("delta", [P, G, D]), sb("sel", [P, G])
            Tps, acc, up = pb("Tps2", [P, 2, 512]), pb("acc2", [P, 2, 512]), pb("up2", [P, 2, 512])
            (t_done, t_hi, t_lo, wo_done, x1_ready, sq_done, v_ready, std_ready, hn_ready, up_done, gel_done, g_hi,
             g_lo, down_done, down_read, delta_ready, chain) = every = chip.sems(
                st, *[f"p3_{n}" for n in ("t_done", "t_hi", "t_lo", "wo_done", "x1_ready", "sq_done", "v_ready",
                                          "std_ready", "hn_ready", "up_done", "gel_done", "g_hi", "g_lo", "down_done",
                                          "down_read", "delta_ready", "chain")])
            (sent,) = chip.pool_sems("p3_sent")

            with nc.Block() as block:

                @block.tensor
                def _(pe):
                    def transposed(src, g, n):
                        if n >= 2:
                            pe.wait_ge(t_lo, KD * (n - 1))
                        for k in range(KD):
                            last = nc.tensor.transpose(Tps[:, n % 2, P * k:P * k + P], src[:, g, P * k:P * k + P],
                                                       chip.ident[:])
                        last.then_inc(t_done, 1)

                    for g in range(G):
                        transposed(o_all, g, g)
                    for g in range(G):
                        pe.wait_ge(t_lo, KD * (g + 1))
                        if g >= 2:
                            pe.wait_ge(x1_ready, g - 1)
                        for k in range(KD):
                            last = three_pass(nc, acc[:, g % 2, 0:D], [p[:, k, P * g:P * g + P] for p in oT],
                                              [p[:, k, :] for p in w["wo"]], k == 0, k == KD - 1)
                        last.then_inc(wo_done, 1)
                    for g in range(G):
                        pe.wait_ge(hn_ready, g + 1)
                        transposed(hn, g, G + g)
                    pe.wait_ge(t_lo, KD * 2 * G)
                    for m in range(FM):
                        if m >= 2:
                            pe.wait_ge(gel_done, m - 1)
                        for k in range(KD):
                            last = three_pass(nc, up[:, m % 2, :], [p[:, k, P * m:P * m + P] for p in w_ffn["w1"]],
                                              [p[:, k, :] for p in fT], k == 0, k == KD - 1)
                        last.then_inc(up_done, 1)
                    for g in range(G):
                        pe.wait_ge(x1_ready, G)
                        if g >= 2:
                            pe.wait_ge(down_read, g - 1)
                        for m in range(FM):
                            if g == 0:
                                pe.wait_ge(g_lo, m + 1)
                            last = three_pass(nc, acc[:, g % 2, 0:D], [p[:, m, P * g:P * g + P] for p in gT],
                                              [p[:, m, :] for p in w_ffn["w2"]], m == 0, m == FM - 1)
                        last.then_inc(down_done, 1)

                @block.scalar
                def _(act):
                    def transposed_hi(out, n, g, scale):
                        act.wait_ge(t_done, n + 1)
                        for k in range(KD):
                            nc.scalar.activation(out[:, k, P * g:P * g + P], Tps[:, n % 2, P * k:P * k + P], ACT.Copy,
                                                 scale=scale[:, k:k + 1] if scale is not None else 1.0
                                                 ).then_inc(t_hi, 1)

                    for g in range(G):
                        transposed_hi(oT[0], g, g, None)
                    for g in range(G):
                        act.wait_ge(x1_ready, g + 1)
                        if g:
                            act.wait_ge(sq_done, g)
                        nc.scalar.activation(sq[:], x1[:, g, :], ACT.Square, accum_out=ss[:, g:g + 1]
                                             ).then_inc(sq_done, 1)
                    act.wait_ge(v_ready, 1)
                    nc.scalar.activation(std[:], vv[:], ACT.Sqrt).then_inc(std_ready, 1)
                    for g in range(G):
                        transposed_hi(fT[0], G + g, g, ln2)
                    for m in range(FM):
                        act.wait_ge(up_done, m + 1)
                        if m >= 2:
                            act.wait_ge(g_lo, m - 1)
                        nc.scalar.activation(gel[:, m % 2, :], up[:, m % 2, :], ACT.Gelu_apprx_tanh
                                             ).then_inc(gel_done, 1)
                        act.wait_ge(gel_done, m + 1)
                        nc.scalar.activation(gT[0][:, m, :], gel[:, m % 2, :], ACT.Copy).then_inc(g_hi, 1)

                @block.vector
                def _(dve):
                    V = nc.vector
                    links = [0]

                    def link(ins):
                        links[0] += 1
                        ins.then_inc(chain, 1)
                        dve.wait_ge(chain, links[0])

                    def transposed_lo(out, n, g, scale):
                        cols = slice(P * g, P * g + P)
                        for k in range(KD):
                            dve.wait_ge(t_hi, KD * (n + 1))
                            V.scalar_tensor_tensor(out[1][:, k, cols], Tps[:, n % 2, P * k:P * k + P],
                                                   scale[:, k:k + 1] if scale is not None else 1.0,
                                                   out[0][:, k, cols].bitcast(FP32), ALU.mult, ALU.subtract
                                                   ).then_inc(t_lo, 1)

                    for g in range(G):
                        transposed_lo(oT, g, g, None)
                    for g in range(G):
                        dve.wait_ge(wo_done, g + 1)
                        V.tensor_tensor(x1[:, g, :], acc[:, g % 2, 0:D], xs[:, g, :], ALU.add).then_inc(x1_ready, 1)
                    dve.wait_ge(sq_done, G)
                    link(V.tensor_scalar(vv[:], ss[:], 1.0 / D, 1e-6, ALU.mult, ALU.add))
                    V.tensor_copy(tmp[:], vv[:]).then_inc(v_ready, 1)
                    dve.wait_ge(std_ready, 1)
                    newton_rsqrt(nc, link, rr[:], std[:], vv[:], tmp[:])
                    for g in range(G):
                        V.tensor_scalar(hn[:, g, :], x1[:, g, :], rr[:, g:g + 1], None, ALU.mult).then_inc(hn_ready, 1)
                    for b in range(B):
                        link(V.tensor_scalar(sel[:, 2 * b:2 * b + 2], picked[:, b, :, 1], thresholds[:, b:b + 1], -1.0,
                                             ALU.is_gt, ALU.mult))
                    for g in range(G):
                        link(V.tensor_scalar(delta[:, g, :], xs[:, g, :], sel[:, g:g + 1], None, ALU.mult))
                    for g in range(G):
                        transposed_lo(fT, G + g, g, ln2)
                    for m in range(FM):
                        dve.wait_ge(g_hi, m + 1)
                        V.tensor_tensor(gT[1][:, m, :], gel[:, m % 2, :], gT[0][:, m, :].bitcast(FP32), ALU.subtract
                                        ).then_inc(g_lo, 1)
                    for g in range(G):
                        dve.wait_ge(down_done, g + 1)
                        V.tensor_tensor(x1[:, g, :], acc[:, g % 2, 0:D], x1[:, g, :], ALU.add).then_inc(down_read, 1)
                        dve.wait_ge(down_read, g + 1)
                        V.scalar_tensor_tensor(delta[:, g, :], x1[:, g, :], picked[:, g // 2, g % 2, 1:2],
                                               delta[:, g, :], ALU.mult, ALU.add).then_inc(delta_ready, 1)

                @block.gpsimd
                def _(pool):
                    for g in range(G):
                        pool.wait_ge(delta_ready, g + 1)
                        n = P if g % 2 == 0 else P - 1
                        nc.gpsimd.indirect_dma_start(
                            out=out_dram[:, :],
                            out_offset=bass.IndirectOffsetOnAxis(ap=row_index[0:n, g // 2, g % 2, 0:1], axis=0),
                            in_=delta[0:n, g, :], in_offset=None, compute_op=ALU.add).then_inc(sent, 16)
                    pool.wait_ge(sent, 16 * G)

            for s in [sent, *every]:
                nc.sync.sem_clear(s)
        nc.all_engine_barrier()


def load_small(chip, stack, plan, scales={}):
    nc = chip.nc
    out = {name: stack.enter_context(nc.sbuf_tensor(f"c_{name}", shape, FP32)) for name, shape, _ in plan}
    with ExitStack() as st:
        loaded, scaled = chip.sems(st, "small_loaded", "small_scaled")
        with nc.Block() as block:

            @block.sync
            def _(sp):
                for name, _, view in plan:
                    sp.dma_start(out[name][:], view).then_inc(loaded, 16)
                sp.wait_ge(loaded, 16 * len(plan))

            @block.vector
            def _(dve):
                dve.wait_ge(loaded, 16 * len(plan))
                for name, scale in scales.items():
                    nc.vector.tensor_scalar(out[name][:], out[name][:], scale, None, ALU.mult).then_inc(scaled, 1)
                dve.wait_ge(scaled, len(scales))

        nc.sync.sem_clear(loaded), nc.sync.sem_clear(scaled)
    nc.all_engine_barrier()
    return out


def zero_rows(chip, dram):
    nc = chip.nc
    TILES, D = dram.shape[0] // P, dram.shape[1]
    PARTS = 8
    with ExitStack() as st:
        zeros = st.enter_context(nc.sbuf_tensor("zeros", [P, TILES // PARTS, D], FP32))
        made, stored = chip.sems(st, "zeros_made", "zeros_stored")
        with nc.Block() as block:

            @block.vector
            def _(dve):
                nc.vector.memset(zeros[:], 0.0).then_inc(made, 1)

            @block.sync
            def _(sp):
                sp.wait_ge(made, 1)
                for q in range(PARTS):
                    n = TILES // PARTS
                    sp.dma_start(dram.rearrange("(p t) d -> p t d", p=P)[:, q * n:q * n + n, :], zeros[:]
                                 ).then_inc(stored, 16)
                sp.wait_ge(stored, 16 * PARTS)

        nc.sync.sem_clear(made), nc.sync.sem_clear(stored)
    nc.all_engine_barrier()


def build(nc, a, out, B, S):
    N, D = a["x"].shape
    chip = Chip(nc, B, S, D)
    E = a["gate_w"].shape[1]
    HEADS = 16
    M = a["mask"].shape[1]
    TILES = 2 * N // P + E
    NA = N // P
    SCALE = float(D) ** -0.5
    HEAD_SCALE = float(D // HEADS) ** -0.5
    dram = lambda n, s: nc.dram_tensor(n, s, FP32, kind="Internal").ap()
    xn1, xn2, y1, y_shared, y2 = (dram(n, (N, D)) for n in ("xn1", "xn2", "y1", "y_shared", "y2"))
    sorted_rows, routed = dram("sorted_rows", (TILES * P, D)), dram("routed", (TILES * P, D))
    router_out = dram("router_out", (N,))
    wide = lambda v: v.to_broadcast([P, v.shape[1]])

    def token_buffers(st, tag):
        T = [st.enter_context(nc.sbuf_tensor(f"{tag}T_{p}", [P, chip.KD, S], FR)) for p in ("hi", "lo")]
        V = [st.enter_context(nc.sbuf_tensor(f"{tag}V_{p}", [P, chip.NT, D], FR)) for p in ("hi", "lo")]
        return T, V

    with ExitStack() as top:
        constants(chip, top)
        small = load_small(chip, top, [
            ("bq", [P, chip.KD], a["bq"]), ("bk", [P, chip.KD], a["bk"]), ("bv", [P, D], wide(a["bv"])),
            ("gate_b", [P, E], wide(a["gate_b"])), ("router_b", [P, 1], wide(a["router_b"])),
            ("ln1", [P, chip.KD], a["ln1"]), ("ln2", [P, chip.KD], a["ln2"])], {"bq": SCALE})
        zero_rows(chip, sorted_rows)

        with ExitStack() as layer:
            sb = lambda n, s, d=FP32: layer.enter_context(nc.sbuf_tensor(n, s, d))
            logits, gates, slots = sb("logits", [P, NA, E]), sb("gates", [P, NA, 2]), sb("slots", [P, NA, 2], I32)
            tile_expert, tile_rows = sb("tile_expert", [1, TILES], I32), sb("tile_rows", [64, TILES])
            with ExitStack() as st:
                w = split_weights(chip, st, [(n, a["a0_" + n]) for n in ("wq", "wk", "wv")] + [("gw", a["gate_w"])],
                                  {"wq": SCALE}, "l0_")
                gate_w = w.pop("gw")
                T, V = token_buffers(st, "l0_")
                with nc.Fori(0, B) as b:
                    norm_stage(chip, b, "n0", a["x"], xn1, T, V, w, gate_w, logits)
                    attention_stage(chip, b, "a0", T, V, w, {"q": small["bq"], "k": small["bk"]}, [a["x"]],
                                    small["bv"], y1)
            gating_stage(chip, logits, small["gate_b"], gates, slots, tile_expert, tile_rows, E, TILES)
            dispatch_stage(chip, xn1, slots, sorted_rows)
            shared_stage(chip, xn1, y1, a["sw1"], a["sb1"], a["sw2"], a["sb2"], a["sw3"], a["sb3"], y_shared)
            routed_stage(chip, sorted_rows, a["rw1"], a["rw2"], a["rw3"], a["rb1"], a["rb2"], a["rb3"], tile_expert,
                         tile_rows, routed)
            combine_stage(chip, y_shared, routed, slots, gates, y2)

        with ExitStack() as layer:
            sb = lambda n, s, d=FP32: layer.enter_context(nc.sbuf_tensor(n, s, d))
            scores, picked = sb("router_scores", [P, NA, 2]), sb("picked", [P, B, 2, 2])
            row_index, picked_row = sb("row_index", [P, B, 2, 2], I32), sb("picked_row", [P, B, 2 * P])
            thresholds = sb("thresholds", [P, B])
            with ExitStack() as st:
                w = split_weights(chip, st, [(n, a["a1_" + n]) for n in ("wq", "wk", "wv", "wo")] +
                                  [("rw", a["router_w"])], {"wq": SCALE}, "l1_")
                router_w = w.pop("rw")
                T, V = token_buffers(st, "l1_")
                with nc.Fori(0, B) as b:
                    norm_stage(chip, b, "n1", y2, xn2, T, V, w, router_w, scores)
                    attention_stage(chip, b, "a1", T, V, w, None, [y2, xn2], None, out)
            rank_stage(chip, scores, small["router_b"], router_out, picked, row_index, picked_row, thresholds, M - 1)
            with ExitStack() as st:
                w = split_weights(chip, st, [(n, a["f1_" + n]) for n in ("wq", "wk", "wv", "wo", "w1", "w2")],
                                  {"wq": HEAD_SCALE}, "f1_")
                picked_stage(chip, xn2, a["positions"], a["mask"], row_index, picked_row, picked, thresholds,
                             a["inverse"], small["ln1"], small["ln2"], w, w, out, HEADS)




def kernel(**inputs):
    import numpy as np
    import concourse.bacc as bacc
    from concourse.bass_utils import run_bass_kernel_spmd

    i = {name: np.asarray(v) for name, v in inputs.items()}
    B, S, D = i["L0_attn_x"].shape
    E, _, H = i["L0_ffn_rw1"].shape
    M = i["L1_ffn_attention_mask"].shape[-1]
    HALF = D // 16 // 2
    columns = lambda v: v.reshape(-1, P).T
    lay = {
        "x": i["L0_attn_x"].reshape(B * S, D),
        **{"a0_" + n.lower(): i["L0_attn_" + n].T for n in ("Wq", "Wk", "Wv")},
        "bq": columns(i["L0_attn_bq"]), "bk": columns(i["L0_attn_bk"]), "bv": i["L0_attn_bv"][None],
        "gate_w": i["L0_ffn_gate_w"], "gate_b": i["L0_ffn_gate_b"][None],
        **{n: i["L0_ffn_" + n] for n in ("rw1", "rw2", "rw3", "rb1", "rb2", "rb3", "sw1", "sw2", "sw3", "sb3")},
        **{n: i["L0_ffn_" + n].reshape(2, H // P, P).transpose(2, 0, 1) for n in ("sb1", "sb2")},
        **{"a1_" + n.lower(): i["L1_attn_" + n].T for n in ("Wq", "Wk", "Wv", "Wo")},
        "router_w": np.concatenate([i["L1_ffn_router_w"], np.zeros((D, 1), np.float32)], axis=1),
        "router_b": i["L1_ffn_router_b"][None],
        **{"f1_" + n: i["L1_ffn_" + n] for n in ("wq", "wk", "wv", "wo", "w1", "w2")},
        "ln1": columns(i["L1_ffn_ln1"]), "ln2": columns(i["L1_ffn_ln2"]),
        "mask": i["L1_ffn_attention_mask"].reshape(-1, M), "positions": i["L1_ffn_position_ids"].reshape(-1, 1),
        "inverse": (1.0 / np.float32(10000.0) ** (np.arange(0, 2 * HALF, 2, dtype=np.float32) / (2 * HALF))
                    ).astype(np.float32)[None],
    }
    nc = bacc.Bacc("TRN2", target_bir_lowering=False, num_devices=1)
    arrays, args = {}, {}
    for name, v in lay.items():
        arrays[f"in_{name}"] = np.ascontiguousarray(v)
        args[name] = nc.dram_tensor(f"in_{name}", v.shape, mybir.dt.from_np(v.dtype), kind="ExternalInput").ap()
    out = nc.dram_tensor("out", (B * S, D), FP32, kind="ExternalOutput").ap()
    build(nc, args, out, B, S)
    r = run_bass_kernel_spmd(nc, [arrays], core_ids=[0])
    return r.results[0]["out"].reshape(B, S, D)
```

```python
import concourse.bass as bass
from concourse import mybir
from contextlib import ExitStack

P = 128
FP32 = mybir.dt.float32
FR = mybir.dt.float32r
I32 = mybir.dt.int32
ACT = mybir.ActivationFunctionType
ALU = mybir.AluOpType
AX = mybir.AxisListType
MASKED = -1e30


class Chip:

    def __init__(self, nc, B, S, D):
        self.nc, self.B, self.S, self.D = nc, B, S, D
        self.NT = S // P
        self.KD = D // P
        self.NG = self.NT // 4

    def sems(self, stack, *names):
        return [stack.enter_context(self.nc.semaphore(n)) for n in names]

    def pool_sems(self, *names):
        return [self.nc.alloc_semaphore(name=n) for n in names]


def three_pass(nc, out, lhs, rhs, start, stop):
    (lh, ll), (rh, rl) = lhs, rhs
    nc.tensor.matmul(out, ll, rh, start=start, stop=False)
    nc.tensor.matmul(out, lh, rl, start=False, stop=False)
    return nc.tensor.matmul(out, lh, rh, start=False, stop=stop)


def constants(chip, stack):
    nc = chip.nc
    ident = stack.enter_context(nc.sbuf_tensor("ident", [P, P], FP32))
    ident_r = stack.enter_context(nc.sbuf_tensor("ident_r", [P, P], FR))
    causal_r = stack.enter_context(nc.sbuf_tensor("causal_r", [P, P], FR))
    with ExitStack() as st:
        causal = st.enter_context(nc.sbuf_tensor("causal", [P, P], FP32))
        filled, selected, copied = chip.sems(st, "const_filled", "const_selected", "const_copied")
        with nc.Block() as block:

            @block.gpsimd
            def _(pool):
                nc.gpsimd.memset(ident[:], 0.0).then_inc(filled, 1)
                nc.gpsimd.memset(causal[:], 0.0).then_inc(filled, 1)
                pool.wait_ge(filled, 2)
                nc.gpsimd.affine_select(out=ident[:], in_=ident[:], compare_op=ALU.not_equal, fill=1.0,
                                        base=0, pattern=[[-1, P]], channel_multiplier=1).then_inc(selected, 1)
                nc.gpsimd.affine_select(out=causal[:], in_=causal[:], compare_op=ALU.is_ge, fill=MASKED,
                                        base=0, pattern=[[-1, P]], channel_multiplier=1).then_inc(selected, 1)

            @block.vector
            def _(dve):
                dve.wait_ge(selected, 2)
                nc.vector.tensor_copy(ident_r[:], ident[:]).then_inc(copied, 1)
                nc.vector.tensor_copy(causal_r[:], causal[:]).then_inc(copied, 1)
                dve.wait_ge(copied, 2)

        nc.sync.sem_clear(filled), nc.sync.sem_clear(selected), nc.sync.sem_clear(copied)
    chip.ident, chip.ident_r, chip.causal_r = ident, ident_r, causal_r
    nc.all_engine_barrier()


def split_weights(chip, stack, named, scales={}, tag=""):
    nc = chip.nc
    out = {}
    with ExitStack() as keep:
        for name, w in named:
            k, n = w.shape
            out[name] = tuple(stack.enter_context(nc.sbuf_tensor(f"{tag}{name}_{part}", [P, k // P, n], FR))
                              for part in ("hi", "lo"))
        raws = [keep.enter_context(nc.sbuf_tensor(f"{tag}{name}_raw", [P, w.shape[0] // P, w.shape[1]], FP32))
                for name, w in named]
        loaded = chip.sems(keep, *[f"{tag}{name}_loaded" for name, _ in named])
        (hi_done, lo_done) = chip.sems(keep, tag + "w_hi_done", tag + "w_lo_done")
        with nc.Block() as block:

            @block.sync
            def _(sp):
                for (name, w), raw, sem in zip(named, raws, loaded):
                    sp.dma_start(raw[:], w.rearrange("(k p) n -> p k n", p=P)).then_inc(sem, 16)

            @block.scalar
            def _(act):
                for (name, w), raw, sem in zip(named, raws, loaded):
                    act.wait_ge(sem, 16)
                    nc.scalar.activation(out[name][0][:], raw[:], ACT.Copy, scale=scales.get(name, 1.0)
                                         ).then_inc(hi_done, 1)

            @block.vector
            def _(dve):
                for n, ((name, w), raw) in enumerate(zip(named, raws)):
                    dve.wait_ge(hi_done, n + 1)
                    flat = lambda a: a.rearrange("p k n -> p (k n)")
                    nc.vector.scalar_tensor_tensor(flat(out[name][1][:]), flat(raw[:]), scales.get(name, 1.0),
                                                   flat(out[name][0][:]).bitcast(FP32), ALU.mult,
                                                   ALU.subtract).then_inc(lo_done, 1)
                dve.wait_ge(lo_done, len(named))

        for s in [*loaded, hi_done, lo_done]:
            nc.sync.sem_clear(s)
    nc.all_engine_barrier()
    return out


def norm_stage(chip, b, tag, src, xn_dram, T, V, w, extra, scores):
    nc, NT, KD, NG, D = chip.nc, chip.NT, chip.KD, chip.NG, chip.D
    E = scores.shape[2]
    AHEAD = 2
    with ExitStack() as st:
        sb = lambda n, s, d=FP32: st.enter_context(nc.sbuf_tensor(f"{tag}_{n}", s, d))
        pb = lambda n, s: st.enter_context(nc.psum_tensor(f"{tag}_{n}", s, FP32))
        X, XN = sb("x", [P, NT, D]), sb("xn", [P, NT, D])
        stats, mv = sb("stats", [P, NT, 6]), sb("mv", [P, NT, 2])
        ve, std, rstd, tmp = (sb(n, [P, NT]) for n in ("ve", "std", "rstd", "tmp"))
        Tps, Vps = pb("Tps", [P, 2, 512]), pb("Vps", [P, 2, 512])
        Gps = pb("Gps", [P, NT, E])
        loaded = chip.sems(st, *[f"{tag}_x_loaded{g}" for g in range(NG)])
        (var_ready, std_ready, xn_ready, t_done, t_hi, t_lo, v_done, v_hi, v_lo, stored, chain) = every = chip.sems(
            st, *[f"{tag}_{n}" for n in ("var_ready", "std_ready", "xn_ready", "t_done", "t_hi", "t_lo", "v_done",
                                         "v_hi", "v_lo", "xn_stored", "dve_chain")])
        x_view = src.rearrange("(t p) d -> p t d", p=P)
        xn_view = xn_dram.rearrange("(t p) d -> p t d", p=P)

        with nc.Block() as block:

            @block.sync
            def _(sp):
                for g in range(NG):
                    sp.dma_start(X[:, 4 * g:4 * g + 4, :], x_view[:, bass.ds(b * NT + 4 * g, 4), :]
                                 ).then_inc(loaded[g], 16)
                for g in range(NG):
                    sp.wait_ge(xn_ready, 4 * (g + 1))
                    sp.dma_start(xn_view[:, bass.ds(b * NT + 4 * g, 4), :], XN[:, 4 * g:4 * g + 4, :]
                                 ).then_inc(stored, 16)
                sp.wait_ge(stored, 16 * NG)

            @block.vector
            def _(dve):
                links = [0]

                def link(ins):
                    links[0] += 1
                    ins.then_inc(chain, 1)
                    dve.wait_ge(chain, links[0])

                def values_lo(g):
                    for h in range(2):
                        n = 2 * g + h
                        pair = slice(2 * n, 2 * n + 2)
                        dve.wait_ge(v_hi, n + 1)
                        nc.vector.tensor_tensor(
                            V[1][:, pair, :].rearrange("p t d -> p (t d)"), Vps[:, n % 2, :],
                            V[0][:, pair, :].rearrange("p t d -> p (t d)").bitcast(FP32),
                            ALU.subtract).then_inc(v_lo, 1)

                def normalise(g):
                    four = slice(4 * g, 4 * g + 4)
                    dve.wait_ge(loaded[g], 16)
                    for t in range(4 * g, 4 * g + 4):
                        ins = nc.vector.bn_stats(stats[:, t, :], X[:, t, :])
                    link(ins)
                    for t in range(4 * g, 4 * g + 4):
                        ins = nc.vector.bn_aggr(mv[:, t, :], stats[:, t, :])
                    link(ins)
                    nc.vector.tensor_scalar_add(ve[:, four], mv[:, four, 1], 1e-5).then_inc(var_ready, 1)
                    dve.wait_ge(std_ready, g + 1)
                    link(nc.vector.reciprocal(rstd[:, four], std[:, four]))
                    link(nc.vector.tensor_tensor(tmp[:, four], rstd[:, four], rstd[:, four], ALU.mult))
                    link(nc.vector.tensor_tensor(tmp[:, four], tmp[:, four], ve[:, four], ALU.mult))
                    link(nc.vector.tensor_scalar(tmp[:, four], tmp[:, four], -0.5, 1.5, ALU.mult, ALU.add))
                    link(nc.vector.tensor_tensor(rstd[:, four], rstd[:, four], tmp[:, four], ALU.mult))
                    for t in range(4 * g, 4 * g + 4):
                        nc.vector.tensor_scalar(XN[:, t, :], X[:, t, :], mv[:, t, 0:1], rstd[:, t:t + 1],
                                                ALU.subtract, ALU.mult).then_inc(xn_ready, 1)

                for g in range(AHEAD):
                    normalise(g)
                for g in range(NG):
                    if g + AHEAD < NG:
                        normalise(g + AHEAD)
                    for k in range(KD):
                        n = KD * g + k
                        dve.wait_ge(t_hi, n + 1)
                        tok = slice(512 * g, 512 * g + 512)
                        nc.vector.tensor_tensor(T[1][:, k, tok], Tps[:, n % 2, :], T[0][:, k, tok].bitcast(FP32),
                                                ALU.subtract).then_inc(t_lo, 1)
                    if g:
                        values_lo(g - 1)
                values_lo(NG - 1)
                nc.vector.tensor_copy(scores[:, bass.ds(b * NT, NT), :], Gps[:]).then_inc(chain, 1)

            @block.scalar
            def _(act):
                def values_hi(g):
                    for h in range(2):
                        n = 2 * g + h
                        act.wait_ge(v_done, n + 1)
                        nc.scalar.activation(V[0][:, 2 * n:2 * n + 2, :].rearrange("p t d -> p (t d)"),
                                             Vps[:, n % 2, :], ACT.Copy).then_inc(v_hi, 1)

                def root(g):
                    four = slice(4 * g, 4 * g + 4)
                    act.wait_ge(var_ready, g + 1)
                    nc.scalar.activation(std[:, four], ve[:, four], ACT.Sqrt).then_inc(std_ready, 1)

                for g in range(AHEAD):
                    root(g)
                for g in range(NG):
                    if g + AHEAD < NG:
                        root(g + AHEAD)
                    for k in range(KD):
                        n = KD * g + k
                        act.wait_ge(t_done, n + 1)
                        nc.scalar.activation(T[0][:, k, 512 * g:512 * g + 512], Tps[:, n % 2, :],
                                             ACT.Copy).then_inc(t_hi, 1)
                    if g:
                        values_hi(g - 1)
                values_hi(NG - 1)

            @block.tensor
            def _(pe):
                def values(g):
                    pe.wait_ge(t_lo, KD * (g + 1))
                    for h in range(2):
                        n = 2 * g + h
                        if n >= 2:
                            pe.wait_ge(v_lo, n - 1)
                        for j in range(2):
                            t = 2 * n + j
                            x = [[part[:, k, P * t:P * t + P] for part in T] for k in range(KD)]
                            for k in range(KD):
                                three_pass(nc, Gps[:, t, :], x[k], [part[:, k, :] for part in extra],
                                           k == 0, k == KD - 1)
                            for k in range(KD):
                                last = three_pass(nc, Vps[:, n % 2, D * j:D * j + D], x[k],
                                                  [part[:, k, :] for part in w["wv"]], k == 0, k == KD - 1)
                        last.then_inc(v_done, 1)

                for g in range(NG):
                    pe.wait_ge(xn_ready, 4 * (g + 1))
                    for k in range(KD):
                        n = KD * g + k
                        if n >= 2:
                            pe.wait_ge(t_lo, n - 1)
                        for j in range(4):
                            last = nc.tensor.transpose(Tps[:, n % 2, P * j:P * j + P],
                                                       XN[:, 4 * g + j, P * k:P * k + P], chip.ident[:])
                        last.then_inc(t_done, 1)
                    if g:
                        values(g - 1)
                values(NG - 1)

        for s in [*loaded, *every]:
            nc.sync.sem_clear(s)
    nc.all_engine_barrier()


class Ranking:

    def __init__(self, chip, stack, scores, router_b, order):
        sb = lambda n, s: stack.enter_context(chip.nc.sbuf_tensor(f"k_{n}", s, FP32))
        self.scores, self.router_b, self.order = scores, router_b, order
        self.weights, self.rank = sb("weights", [P, chip.B * chip.NT]), sb("rank", [P, chip.B * chip.NT])
        self.earlier = sb("earlier", [P, P])


def attention_stage(chip, b, tag, T, V, w, biases, bases, value_bias, dst, ranking=None, background=()):
    nc, NT, KD, NG, D = chip.nc, chip.NT, chip.KD, chip.NG, chip.D
    has_o = "wo" in w
    SLOTS = 4
    TBANKS = 3
    FRONTS = 3
    SBUFS = 3
    AHEAD = 2
    LAG = 2
    COUNT_FROM = 8

    steps, of_tile = [], []
    for i in range(NT):
        groups = [("p", i, k0, min(4, i + 1 - k0)) for k0 in range(0, i + 1, 4)]
        if has_o and i >= 2:
            groups.append(("o", i - 2, 0, KD))
        if has_o and i == NT - 1:
            groups += [("o", i - 1, 0, KD)]
        of_tile.append(range(len(steps), len(steps) + len(groups)))
        steps += groups
    body_steps = len(steps)
    if has_o:
        steps.append(("o", NT - 1, 0, KD))
    last_p = {i: max(n for n, s in enumerate(steps) if s[0] == "p" and s[1] == i) for i in range(NT)}
    o_step = {s[1]: n for n, s in enumerate(steps) if s[0] == "o"}
    chunks = lambda i: i // 4 + 1
    chunks_before = lambda i: sum(chunks(j) for j in range(i))
    acc_use = {}
    for kind, i, k0, _ in steps:
        if k0 == 0:
            acc_use[(kind, i)] = len(acc_use)

    project = lambda c: [(kind, c, m) for kind in "kq" for m in range(KD)]
    score = lambda i: [("s", i, j) for j in range(chunks(i))]
    first_units = project(0) + [u for i in range(AHEAD) for u in score(i)]
    front_at = {n: [] for n in range(len(steps))}
    for i in range(NT):
        units = score(i + AHEAD) if i + AHEAD < NT else []
        c = (i + AHEAD + 1) // 4
        if (i + AHEAD + 1) % 4 == 0 and c < NG:
            units = units + project(c)
        for q, u in enumerate(units):
            front_at[of_tile[i][q * len(of_tile[i]) // len(units)]].append(u)
    every_unit = first_units + [u for n in range(len(steps)) for u in front_at[n]]
    unit_no = {u: n for n, u in enumerate(every_unit)}
    proj_no = {u: n for n, u in enumerate(u for u in every_unit if u[0] != "s")}
    exp_at = {of_tile[i - 1][0]: i for i in range(1, NT)}

    with ExitStack() as st:
        sb = lambda n, s, d=FP32: st.enter_context(nc.sbuf_tensor(f"{tag}_{n}", s, d))
        pb = lambda n, s: st.enter_context(nc.psum_tensor(f"{tag}_{n}", s, FP32))
        kT = [sb(f"kT{p}", [P, KD, chip.S], FR) for p in "hl"]
        qT = [sb(f"qT{p}", [P, 2, KD, 512], FR) for p in "hl"]
        probs = sb("probs", [P, SBUFS, chip.S])
        pT = [sb(f"pT{p}", [P, SLOTS, 512], FR) for p in "hl"]
        base = sb("base", [P, 2, 4, D])
        base2 = sb("base2", [P, 2, 4, D]) if len(bases) > 1 else None
        if has_o:
            heads = sb("o_norm", [P, 2, D])
        part_min, neg_max = sb("part_min", [P, NT, 4]), sb("neg_max", [P, NT])
        sums, rsum = sb("sums", [P, NT]), sb("rsum", [P, NT])
        front, Tps, acc = pb("front", [P, FRONTS, 512]), pb("Tps", [P, TBANKS, 512]), pb("acc", [P, 2, 512])
        base_loaded = chip.sems(st, f"{tag}_base_loaded0", f"{tag}_base_loaded1")
        (proj_done, proj_hi, front_free, acc_free, s_done, max_done, exp_done, t_done, t_hi, t_lo, pv_done, rs_ready,
         base_ready, y_stored) = every = chip.sems(
            st, *[f"{tag}_{n}" for n in (
                "proj_done", "proj_hi", "front_free", "acc_free", "scores_done", "max_done", "exp_done", "t_done",
                "t_hi", "t_lo", "pv_done", "rsum_ready", "base_ready", "y_stored")])
        if ranking:
            mine, row, counts = sb("rank_mine", [P, NT]), sb("rank_row", [P, chip.S]), sb("rank_counts", [P, NT, 5])
            marks = sb("rank_marks", [P, NT // 2, P], mybir.dt.bfloat16)
            rank_sems = chip.sems(st, *[f"{tag}_rank_{n}" for n in ("mine_ready", "stored", "row_loaded", "chain",
                                                                    "counted")])
            RANK_LINKS = 6
            mine_ready, rank_stored, row_loaded, rank_chain, counted = rank_sems
        stored_as = "o" if has_o else "p"
        view = lambda a: a.rearrange("(t p) d -> p t d", p=P)
        bank_of = lambda u: front[:, unit_no[u] % FRONTS, :]

        def projected(u, part):
            kind, c, m = u
            return qT[part][:, c % 2, m, :] if kind == "q" else kT[part][:, m, 512 * c:512 * c + 512]

        with nc.Block() as block:

            @block.sync
            def _(sp):
                for c in range(NG):
                    if c >= 2:
                        sp.wait_ge(y_stored, 16 * (c - 1))
                    tiles = bass.ds(b * NT + 4 * c, 4)
                    sp.dma_start(base[:, c % 2, :, :], view(bases[0])[:, tiles, :]).then_inc(base_loaded[c % 2], 16)
                    if base2 is not None:
                        sp.dma_start(base2[:, c % 2, :, :], view(bases[1])[:, tiles, :]
                                     ).then_inc(base_loaded[c % 2], 16)
                    if c == 0:
                        for into, src, sem in background:
                            sp.dma_start(into, src).then_inc(sem, 16)
                    if ranking and c == 1:
                        sp.wait_ge(mine_ready, 1)
                        sp.dma_start(ranking.order.rearrange("(b p t) -> p b t", p=P, t=NT)[:, bass.ds(b, 1), :],
                                     mine[:].rearrange("p (o t) -> p o t", o=1)).then_inc(rank_stored, 16)
                        sp.wait_ge(rank_stored, 16)
                        everyone = ranking.order.rearrange("(o n) -> o n", o=1)[:, bass.ds(b * chip.S, chip.S)]
                        sp.dma_start(row[:], everyone.to_broadcast([P, chip.S])).then_inc(row_loaded, 16)
                    if c:
                        sp.wait_ge(acc_free, acc_use[(stored_as, 4 * c - 1)] + 1)
                        sp.dma_start(view(dst)[:, bass.ds(b * NT + 4 * (c - 1), 4), :], base[:, (c - 1) % 2, :, :]
                                     ).then_inc(y_stored, 16)
                sp.wait_ge(acc_free, acc_use[(stored_as, NT - 1)] + 1)
                sp.dma_start(view(dst)[:, bass.ds(b * NT + 4 * (NG - 1), 4), :], base[:, (NG - 1) % 2, :, :]
                             ).then_inc(y_stored, 16)
                sp.wait_ge(y_stored, 16 * NG)

            @block.gpsimd
            def _(pool):
                g = nc.gpsimd
                links = [0]

                def link(ins):
                    links[0] += 1
                    ins.then_inc(rank_chain, 1)
                    pool.wait_ge(rank_chain, links[0])

                def add_bases(c):
                    pool.wait_ge(base_loaded[c % 2], 16 * len(bases) * (c // 2 + 1))
                    slot = base[:, c % 2, :, :]
                    if base2 is not None:
                        other = base2[:, c % 2, :, :]
                    else:
                        other = value_bias[:].rearrange("p (a d) -> p a d", a=1).to_broadcast([P, 4, D])
                    g.tensor_tensor(slot, slot, other, ALU.add).then_inc(base_ready, 1)

                def own_weights():
                    link(g.memset(ranking.earlier[:], 0.0))
                    link(g.affine_select(out=ranking.earlier[:], in_=ranking.earlier[:], compare_op=ALU.is_ge, fill=1.0,
                                         base=0, pattern=[[1, P]], channel_multiplier=-1))
                    link(g.tensor_copy(mine[:], ranking.scores[:, bass.ds(b * NT, NT), 0]))
                    link(g.tensor_scalar(mine[:], mine[:], ranking.router_b[:], None, ALU.add))
                    link(g.tensor_copy(ranking.weights[:, bass.ds(b * NT, NT)], mine[:]))
                    pool.sem_inc(mine_ready, 1)

                if ranking:
                    link(g.memset(counts[:], 0.0))
                    own_weights()
                for c in range(NG):
                    add_bases(c)

            @block.scalar
            def _(act):
                def project_hi(u):
                    kind, c, m = u
                    act.wait_ge(proj_done, proj_no[u] + 1)
                    if kind == "q" and c >= 2 and m == 0:
                        act.wait_ge(s_done, chunks_before(4 * (c - 1)))
                    if biases:
                        ins = nc.scalar.activation(projected(u, 0), bank_of(u), ACT.Identity,
                                                   bias=biases[kind][:, m:m + 1])
                    else:
                        ins = nc.scalar.activation(projected(u, 0), bank_of(u), ACT.Copy)
                    ins.then_inc(proj_hi, 1)

                def exponentials(i):
                    act.wait_ge(max_done, i + 1)
                    both = probs[:, i % SBUFS, 0:P * (i + 1)]
                    nc.scalar.activation(both, both, ACT.Exp, scale=-1.0, bias=neg_max[:, i:i + 1],
                                         accum_out=sums[:, i:i + 1]).then_inc(exp_done, 1)

                def transposed_hi(n):
                    act.wait_ge(t_done, n + 1)
                    if n >= SLOTS:
                        act.wait_ge(pv_done, n - SLOTS + 1)
                    width = P * steps[n][3]
                    nc.scalar.activation(pT[0][:, n % SLOTS, 0:width], Tps[:, n % TBANKS, 0:width],
                                         ACT.Copy).then_inc(t_hi, 1)

                for u in project(0):
                    project_hi(u)
                exponentials(0)
                for n in range(len(steps)):
                    transposed_hi(n)
                    if n in exp_at:
                        exponentials(exp_at[n])
                    for u in front_at[n]:
                        if u[0] != "s":
                            project_hi(u)

            @block.vector
            def _(dve):
                def front_read(u):
                    if u[0] != "s":
                        dve.wait_ge(proj_hi, proj_no[u] + 1)
                        hi = projected(u, 0).bitcast(FP32)
                        if biases:
                            ins = nc.vector.scalar_tensor_tensor(projected(u, 1), bank_of(u),
                                                                 biases[u[0]][:, u[2]:u[2] + 1], hi, ALU.add,
                                                                 ALU.subtract)
                        else:
                            ins = nc.vector.tensor_tensor(projected(u, 1), bank_of(u), hi, ALU.subtract)
                        ins.then_inc(front_free, 1)
                        return
                    _, i, j = u
                    dve.wait_ge(s_done, chunks_before(i) + j + 1)
                    if i >= SBUFS and j == 0:
                        dve.wait_ge(t_done, last_p[i - SBUFS] + 1)
                    width = min(512, P * (i + 1) - 512 * j)
                    one = chunks(i) == 1
                    nc.vector.tensor_scalar(probs[:, i % SBUFS, 512 * j:512 * j + width], bank_of(u)[:, 0:width],
                                            -1.0, None, ALU.mult, ALU.min,
                                            accum_out=neg_max[:, i:i + 1] if one else part_min[:, i, j:j + 1]
                                            ).then_inc(front_free, 1)
                    if j == chunks(i) - 1:
                        dve.wait_ge(front_free, unit_no[u] + 1)
                        if one:
                            dve.sem_inc(max_done, 1)
                        else:
                            nc.vector.tensor_reduce(neg_max[:, i:i + 1], part_min[:, i, 0:chunks(i)], AX.X, ALU.min
                                                    ).then_inc(max_done, 1)

                def transposed_lo(n):
                    dve.wait_ge(t_hi, n + 1)
                    width = P * steps[n][3]
                    nc.vector.tensor_tensor(pT[1][:, n % SLOTS, 0:width], Tps[:, n % TBANKS, 0:width],
                                            pT[0][:, n % SLOTS, 0:width].bitcast(FP32),
                                            ALU.subtract).then_inc(t_lo, 1)

                def finish(n):
                    kind, i = steps[n][:2]
                    if kind == "p" and n != last_p[i]:
                        return
                    bank = acc[:, acc_use[(kind, i)] % 2, 0:D]
                    slot = base[:, (i // 4) % 2, i % 4, :]
                    if kind == "p":
                        dve.wait_ge(exp_done, i + 1)
                        nc.vector.reciprocal(rsum[:, i:i + 1], sums[:, i:i + 1]).then_inc(rs_ready, 1)
                        dve.wait_ge(rs_ready, i + 1)
                    dve.wait_ge(pv_done, n + 1)
                    if kind == "p" and has_o:
                        if i >= 2:
                            dve.wait_ge(t_done, o_step[i - 2] + 1)
                        nc.vector.tensor_scalar(heads[:, i % 2, :], bank, rsum[:, i:i + 1], None,
                                                ALU.mult).then_inc(acc_free, 1)
                        return
                    dve.wait_ge(base_ready, i // 4 + 1)
                    if kind == "p":
                        ins = nc.vector.scalar_tensor_tensor(slot, bank, rsum[:, i:i + 1], slot, ALU.mult, ALU.add)
                    else:
                        ins = nc.vector.tensor_tensor(slot, bank, slot, ALU.add)
                    ins.then_inc(acc_free, 1)

                def count(i, half):
                    links = 2 * i + half
                    if i == 0 and half == 0:
                        dve.wait_ge(mine_ready, 1)
                        dve.wait_ge(row_loaded, 16)
                    else:
                        dve.wait_ge(counted, links)
                    by_token = row[:].rearrange("q (p t) -> q t p", t=NT)
                    own = mine[:, i:i + 1]
                    lo, hi = NT // 2 * half, NT // 2 * (half + 1)
                    split = min(max(i, lo), hi)
                    if split > lo:
                        ins = nc.vector.tensor_scalar(marks[:, 0:split - lo, :], by_token[:, lo:split, :], own, None,
                                                      ALU.is_ge, ALU.add, accum_out=counts[:, i, half:half + 1])
                    if split < hi:
                        ins = nc.vector.tensor_scalar(marks[:, split - lo:hi - lo, :], by_token[:, split:hi, :], own,
                                                      None, ALU.is_gt, ALU.add,
                                                      accum_out=counts[:, i, 2 + half:3 + half])
                    ins.then_inc(counted, 1)
                    if half == 1:
                        dve.wait_ge(counted, links + 1)
                        nc.vector.scalar_tensor_tensor(marks[:, 0, :], by_token[:, i, :], own, ranking.earlier[:],
                                                       ALU.is_equal, ALU.mult, accum_out=counts[:, i, 4:5]
                                                       ).then_inc(rank_chain, 1)
                        dve.wait_ge(rank_chain, RANK_LINKS + i + 1)

                for u in first_units:
                    front_read(u)
                for n in range(len(steps)):
                    if n > LAG:
                        finish(n - LAG - 1)
                    transposed_lo(n)
                    for u in front_at[n]:
                        front_read(u)
                    if ranking:
                        left = len(steps) - COUNT_FROM
                        for q in range(2 * NT):
                            if n == COUNT_FROM + q * left // (2 * NT):
                                count(q // 2, q % 2)
                for n in range(len(steps) - LAG - 1, len(steps)):
                    finish(n)
                if ranking:
                    nc.vector.tensor_reduce(ranking.rank[:, bass.ds(b * NT, NT)], counts[:], AX.X, ALU.add
                                            ).then_inc(counted, 1)

            @block.tensor
            def _(pe):
                def front_unit(u):
                    kind, c, m = u
                    if unit_no[u] >= FRONTS:
                        pe.wait_ge(front_free, unit_no[u] - FRONTS + 1)
                    if kind != "s":
                        for k in range(KD):
                            last = three_pass(nc, bank_of(u), [p[:, k, P * m:P * m + P] for p in w["w" + kind]],
                                              [p[:, k, 512 * c:512 * c + 512] for p in T], k == 0, k == KD - 1)
                        last.then_inc(proj_done, 1)
                        return
                    _, i, j = u
                    if i % 4 == 0 and j == 0:
                        pe.wait_ge(front_free, unit_no[("q", i // 4, KD - 1)] + 1)
                    rows = slice(P * (i % 4), P * (i % 4) + P)
                    cols = slice(512 * j, min(512 * j + 512, P * (i + 1)))
                    width = cols.stop - cols.start
                    diagonal = j == chunks(i) - 1
                    for k in range(KD):
                        last = three_pass(nc, bank_of(u)[:, 0:width], [p[:, (i // 4) % 2, k, rows] for p in qT],
                                          [p[:, k, cols] for p in kT], k == 0, k == KD - 1 and not diagonal)
                    if diagonal:
                        last = nc.tensor.matmul(bank_of(u)[:, width - P:width], chip.ident_r[:], chip.causal_r[:],
                                                start=False, stop=True)
                    last.then_inc(s_done, 1)

                def transposes(n):
                    kind, i, k0, count = steps[n]
                    if n >= TBANKS:
                        pe.wait_ge(t_lo, n - TBANKS + 1)
                    if kind == "p":
                        pe.wait_ge(exp_done, i + 1)
                        src = probs[:, i % SBUFS, :]
                    else:
                        pe.wait_ge(acc_free, acc_use[("p", i)] + 1)
                        src = heads[:, i % 2, :]
                    for j in range(count):
                        last = nc.tensor.transpose(Tps[:, n % TBANKS, P * j:P * j + P],
                                                   src[:, P * (k0 + j):P * (k0 + j) + P], chip.ident[:])
                    last.then_inc(t_done, 1)

                def products(n):
                    kind, i, k0, count = steps[n]
                    pe.wait_ge(t_lo, n + 1)
                    u = acc_use[(kind, i)]
                    if k0 == 0 and u >= 2:
                        pe.wait_ge(acc_free, u - 1)
                    ends = kind == "o" or n == last_p[i]
                    for j in range(count):
                        rhs = [p[:, k0 + j, :] for p in (V if kind == "p" else w["wo"])]
                        last = three_pass(nc, acc[:, u % 2, 0:D], [p[:, n % SLOTS, P * j:P * j + P] for p in pT],
                                          rhs, k0 + j == 0, ends and j == count - 1)
                    last.then_inc(pv_done, 1)

                for u in first_units:
                    front_unit(u)
                for n in range(body_steps):
                    transposes(n)
                    if n >= LAG:
                        products(n - LAG)
                    for u in front_at[n]:
                        front_unit(u)
                if has_o:
                    products(body_steps - 2)
                    products(body_steps - 1)
                    transposes(body_steps)
                    products(body_steps)
                else:
                    products(body_steps - 2)
                    products(body_steps - 1)

        for s in [*base_loaded, *(rank_sems if ranking else ()), *every]:
            nc.sync.sem_clear(s)
    nc.all_engine_barrier()


def gating_stage(chip, logits, gate_b, meta, slots, tile_expert, tile_rows, E, TILES):
    nc = chip.nc
    NA = logits.shape[1]
    with ExitStack() as st:
        sb = lambda n, s, d=FP32: st.enter_context(nc.sbuf_tensor(f"g_{n}", s, d))
        ones, before, rev = sb("ones", [P, P]), sb("before", [P, P]), sb("rev", [P, E])
        tile_no, row_no = sb("tile_no", [P, TILES]), sb("row_no", [64, 1])
        L, L2, ex, eq = (sb(n, [P, NA, E]) for n in ("L", "L2", "ex", "eq"))
        oh = [sb(f"oh{k}", [P, NA, E]) for k in range(2)]
        m = [sb(f"m{k}", [P, NA]) for k in range(2)]
        mx, total = sb("mx", [P, NA]), sb("total", [P, NA])
        picked, where = sb("picked", [P, NA, E]), sb("where", [P, NA, E])
        gsum = sb("gsum", [P, NA])
        token_no = sb("token_no", [P, NA], I32)
        counts, running = sb("counts", [P, NA, E]), sb("running", [P, NA, E])
        tiles_i, tiles_f, end_tile, start_row = (sb("tiles_i", [P, E], I32), sb("tiles_f", [P, E]),
                                                 sb("end_tile", [P, E]), sb("start_row", [P, E]))
        expert_f = sb("expert_f", [P, TILES])
        slot_f = sb("slot_f", [P, NA])
        onesE = sb("onesE", [P, max(NA, E)])
        within = st.enter_context(nc.psum_tensor("g_within", [P, NA, E], FP32))
        in_tile = st.enter_context(nc.psum_tensor("g_in_tile", [P, NA, E], FP32))
        chain, made, exp_ready, picked_ready, counted = every = chip.sems(
            st, "g_chain", "g_made", "g_exp_ready", "g_picked_ready", "g_counted")
        wide = lambda a: a.rearrange("p (t o) -> p t o", o=1).to_broadcast([P, NA, E])
        tall = lambda a: a.rearrange("p (o e) -> p o e", o=1).to_broadcast([P, NA, E])

        with nc.Block() as block:

            @block.gpsimd
            def _(pool):
                nc.gpsimd.memset(ones[:], 1.0).then_inc(made, 1)
                nc.gpsimd.memset(before[:], 1.0).then_inc(made, 1)
                nc.gpsimd.memset(onesE[:], 1.0).then_inc(made, 1)
                nc.gpsimd.iota(rev[:], pattern=[[-1, E]], base=E, channel_multiplier=0,
                               allow_small_or_imprecise_dtypes=True).then_inc(made, 1)
                nc.gpsimd.iota(tile_no[:], pattern=[[1, TILES]], base=0, channel_multiplier=0,
                               allow_small_or_imprecise_dtypes=True).then_inc(made, 1)
                nc.gpsimd.iota(row_no[:], pattern=[[0, 1]], base=0, channel_multiplier=1,
                               allow_small_or_imprecise_dtypes=True).then_inc(made, 1)
                nc.gpsimd.iota(token_no[:], pattern=[[P, NA]], base=0, channel_multiplier=1).then_inc(made, 1)
                pool.wait_ge(made, 7)
                nc.gpsimd.affine_select(out=before[:], in_=before[:], compare_op=ALU.is_gt, fill=0.0, base=0,
                                        pattern=[[1, P]], channel_multiplier=-1).then_inc(made, 1)

            @block.vector
            def _(dve):
                links = [0]

                def link(ins):
                    links[0] += 1
                    ins.then_inc(chain, 1)
                    dve.wait_ge(chain, links[0])

                tt, V = nc.vector.tensor_tensor, nc.vector
                dve.wait_ge(made, 8)
                link(tt(L[:], logits[:], tall(gate_b[:]), ALU.add))
                link(V.tensor_reduce(m[0][:], L[:], AX.X, ALU.max))
                tt(ex[:], L[:], wide(m[0][:]), ALU.subtract).then_inc(exp_ready, 1)
                src = L
                for k in range(2):
                    link(tt(eq[:], src[:], wide(m[k][:]), ALU.is_equal))
                    link(tt(eq[:], eq[:], tall(rev[:]), ALU.mult))
                    link(V.tensor_reduce(mx[:], eq[:], AX.X, ALU.max))
                    link(tt(oh[k][:], eq[:], wide(mx[:]), ALU.is_equal))
                    if k == 0:
                        flat = lambda a: a.rearrange("p t e -> p (t e)")
                        link(V.scalar_tensor_tensor(flat(L2[:]), flat(oh[0][:]), MASKED, flat(L[:]), ALU.mult, ALU.add))
                        link(V.tensor_reduce(m[1][:], L2[:], AX.X, ALU.max))
                        src = L2
                tt(picked[:], oh[0][:], oh[1][:], ALU.add).then_inc(picked_ready, 1)
                dve.wait_ge(exp_ready, 2)
                link(V.tensor_reduce(total[:], ex[:], AX.X, ALU.add))
                link(V.reciprocal(total[:], total[:]))
                for k in range(2):
                    link(tt(eq[:], ex[:], oh[k][:], ALU.mult))
                    link(V.tensor_reduce(gsum[:], eq[:], AX.X, ALU.add))
                    link(V.tensor_copy(meta[:, :, k, 0].bitcast(I32), token_no[:]))
                    link(tt(meta[:, :, k, 1], gsum[:], total[:], ALU.mult))
                dve.wait_ge(counted, 1)
                link(V.tensor_copy(counts[:], in_tile[:]))
                for e in range(E):
                    ins = V.tensor_tensor_scan(running[:, :, e], onesE[:, 0:NA], counts[:, :, e], 0.0,
                                               ALU.mult, ALU.add)
                link(ins)
                link(V.tensor_scalar_add(tiles_i[:], running[:, NA - 1, :], float(P - 1)))
                link(V.tensor_single_scalar(tiles_i[:], tiles_i[:], 7, ALU.logical_shift_right))
                link(V.tensor_copy(tiles_f[:], tiles_i[:]))
                link(V.tensor_tensor_scan(end_tile[:], onesE[:, 0:E], tiles_f[:], 0.0, ALU.mult, ALU.add))
                link(tt(start_row[:], end_tile[:], tiles_f[:], ALU.subtract))
                link(V.tensor_single_scalar(start_row[:], start_row[:], float(P), ALU.mult))
                link(tt(running[:], running[:], counts[:], ALU.subtract))
                link(tt(where[:], running[:], within[:], ALU.add))
                link(tt(where[:], where[:], tall(start_row[:]), ALU.add))
                for k in range(2):
                    link(tt(eq[:], where[:], oh[k][:], ALU.mult))
                    link(V.tensor_reduce(slot_f[:], eq[:], AX.X, ALU.add))
                    link(V.tensor_copy(slots[:, :, k], slot_f[:]))
                link(V.tensor_scalar(expert_f[:], tile_no[:], end_tile[:, 0:1], None, ALU.is_ge))
                for e in range(1, E - 1):
                    link(V.scalar_tensor_tensor(expert_f[:], tile_no[:], end_tile[:, e:e + 1], expert_f[:],
                                                ALU.is_ge, ALU.add))
                V.tensor_scalar(tile_rows[0:32, :], expert_f[0:32, :], row_no[0:32, :], None, ALU.is_equal)
                V.tensor_scalar(tile_rows[32:64, :], expert_f[32:64, :], 32.0, row_no[32:64, :], ALU.add, ALU.is_equal)
                link(V.tensor_copy(tile_expert[:], expert_f[0:1, :]))

            @block.scalar
            def _(act):
                act.wait_ge(exp_ready, 1)
                nc.scalar.activation(ex[:], ex[:], ACT.Exp).then_inc(exp_ready, 1)

            @block.tensor
            def _(pe):
                pe.wait_ge(picked_ready, 1)
                nc.tensor.matmul(within[:], before[:], picked[:], start=True, stop=True)
                nc.tensor.matmul(in_tile[:], ones[:], picked[:], start=True, stop=True).then_inc(counted, 1)

        for s in every:
            nc.sync.sem_clear(s)
    nc.all_engine_barrier()


def shared_stage(chip, xn_dram, base_dram, w1, b1, w2, b2, w3, b3, slots, meta, sorted_dram, sorted_meta, fill,
                 prefetch, dst):
    nc, D, KD = chip.nc, chip.D, chip.KD
    n_sh, _, H = w1.shape
    HM = H // P
    U = n_sh * HM
    NC = xn_dram.shape[0] // 512
    view = lambda a: a.rearrange("(t p) d -> p t d", p=P)
    with ExitStack() as st:
        sb = lambda n, s, d=FP32: st.enter_context(nc.sbuf_tensor(f"s_{n}", s, d))
        pb = lambda n, s: st.enter_context(nc.psum_tensor(f"s_{n}", s, FP32))
        W1 = [sb(f"w1{p}", [P, n_sh, KD, H], FR) for p in "hl"]
        W2 = [sb(f"w2{p}", [P, n_sh, KD, H], FR) for p in "hl"]
        W3 = [sb(f"w3{p}", [P, n_sh, HM, D], FR) for p in "hl"]
        raw = sb("raw", [P, 3, KD * H])
        B1, B2, B3 = sb("b1", [P, n_sh, HM]), sb("b2", [P, n_sh, HM]), sb("b3", [P, n_sh, D])
        rows, base = sb("rows", [P, 2, 4, D]), sb("base", [P, 2, 4, D])
        T = [sb(f"T{p}", [P, 2, KD, 512], FR) for p in "hl"]
        gate, hidden = sb("gate", [P, 2, 512]), sb("hidden", [P, 2, 512])
        hT = [sb(f"hT{p}", [P, U, 512], FR) for p in "hl"]
        Tps, up, acc = pb("Tps", [P, 2, 512]), pb("up", [P, 2, 2, 512]), pb("acc", [P, 2, 512])
        raw_loaded = chip.sems(st, *[f"s_raw_loaded{r}" for r in range(3)])
        rows_loaded = chip.sems(st, "s_rows_loaded0", "s_rows_loaded1")
        base_loaded = chip.sems(st, "s_base_loaded0", "s_base_loaded1")
        stored = chip.sems(st, "s_stored0", "s_stored1")
        sent = chip.pool_sems("s_sent0", "s_sent1")
        (prefetched,) = chip.sems(st, "s_prefetched")
        filled, fill_count, _ = fill
        SENDS = 4 * 2 * 2
        (biases, w_hi, w_lo, b3_ready, t_done, t_hi, t_lo, up_done, gate_done, hid_done, hid_hi, hid_lo, acc_done,
         acc_free, base_ready) = every = chip.sems(
            st, *[f"s_{n}" for n in ("biases", "w_hi", "w_lo", "b3_ready", "t_done", "t_hi", "t_lo", "up_done",
                                     "gate_done", "hid_done", "hid_hi", "hid_lo", "acc_done", "acc_free",
                                     "base_ready")])
        loads = []
        for n in range(n_sh):
            for W, w in ((W1, w1), (W2, w2), (W3, w3)):
                loads.append((W, n, w[n].rearrange("(k p) h -> p k h", p=P)))
        parts_of = lambda W, n: [p[:, n, :, :].rearrange("p k h -> p (k h)") for p in W]

        with nc.Block() as block:

            @block.sync
            def _(sp):
                for c in range(2):
                    sp.dma_start(rows[:, c, :, :], view(xn_dram)[:, 4 * c:4 * c + 4, :]).then_inc(rows_loaded[c], 16)
                for q, (W, n, src) in enumerate(loads):
                    if q >= 3:
                        sp.wait_ge(w_lo, q - 2)
                    sp.dma_start(raw[:, q % 3, :].rearrange("p (k h) -> p k h", k=src.shape[1]), src
                                 ).then_inc(raw_loaded[q % 3], 16)
                    if q == 0:
                        sp.dma_start(B1[:], b1).then_inc(biases, 16)
                        sp.dma_start(B2[:], b2).then_inc(biases, 16)
                        sp.dma_start(B3[:], b3.rearrange("(o n) d -> o n d", o=1).to_broadcast([P, n_sh, D])
                                     ).then_inc(biases, 16)
                for c in range(NC):
                    r = c % 2
                    if c >= 2:
                        sp.wait_ge(t_done, KD * (c - 1))
                        sp.wait_ge(sent[r], 16 * SENDS * (c // 2))
                        sp.dma_start(rows[:, r, :, :], view(xn_dram)[:, 4 * c:4 * c + 4, :]
                                     ).then_inc(rows_loaded[r], 16)
                        sp.wait_ge(stored[r], 16 * (c // 2))
                    sp.dma_start(base[:, r, :, :], view(base_dram)[:, 4 * c:4 * c + 4, :]).then_inc(base_loaded[r], 16)
                    for tile, src in prefetch[c]:
                        sp.dma_start(tile, src).then_inc(prefetched, 16)
                sp.wait_ge(prefetched, 16 * sum(len(part) for part in prefetch))

            @block.gpsimd
            def _(pool):
                pool.wait_ge(biases, 48)
                for n in range(1, n_sh):
                    nc.gpsimd.tensor_tensor(B3[:, 0, :], B3[:, 0, :], B3[:, n, :], ALU.add).then_inc(b3_ready, 1)
                    pool.wait_ge(b3_ready, n)
                nc.gpsimd.tensor_scalar(B3[:, 0, :], B3[:, 0, :], 1.0 / n_sh, 0.0, ALU.mult, ALU.add).then_inc(b3_ready, 1)
                pool.wait_ge(b3_ready, n_sh)
                for c in range(NC):
                    pool.wait_ge(base_loaded[c % 2], 16 * (c // 2 + 1))
                    slot = base[:, c % 2, :, :]
                    nc.gpsimd.tensor_tensor(slot, slot, B3[:, 0:1, :].to_broadcast([P, 4, D]), ALU.add
                                            ).then_inc(base_ready, 1)
                    if c == 0:
                        pool.wait_ge(filled, fill_count)
                    pool.wait_ge(rows_loaded[c % 2], 16 * (c // 2 + 1))
                    for j in range(4):
                        for k in range(2):
                            t = 4 * c + j
                            place = bass.IndirectOffsetOnAxis(ap=slots[:, t, k:k + 1], axis=0)
                            nc.gpsimd.indirect_dma_start(out=sorted_dram[:, :], out_offset=place,
                                                         in_=rows[:, c % 2, j, :], in_offset=None
                                                         ).then_inc(sent[c % 2], 16)
                            nc.gpsimd.indirect_dma_start(out=sorted_meta[:, :], out_offset=place,
                                                         in_=meta[:, t, k, :], in_offset=None
                                                         ).then_inc(sent[c % 2], 16)
                for r in range(2):
                    pool.wait_ge(sent[r], 16 * SENDS * (NC // 2))

            @block.scalar
            def _(act):
                def weights_hi(q):
                    W, n, _ = loads[q]
                    act.wait_ge(raw_loaded[q % 3], 16 * (q // 3 + 1))
                    nc.scalar.activation(parts_of(W, n)[0], raw[:, q % 3, :], ACT.Copy).then_inc(w_hi, 1)

                def tokens_hi(c):
                    for k in range(KD):
                        n = KD * c + k
                        act.wait_ge(t_done, n + 1)
                        if c >= 2 and k == 0:
                            act.wait_ge(up_done, 2 * U * (c - 1))
                        nc.scalar.activation(T[0][:, c % 2, k, :], Tps[:, n % 2, :], ACT.Copy).then_inc(t_hi, 1)

                tokens_hi(0)
                for q in range(3):
                    weights_hi(q)
                act.wait_ge(biases, 48)
                for c in range(NC):
                    for u in range(U):
                        n = c * U + u
                        e, m = divmod(u, HM)
                        act.wait_ge(up_done, 2 * n + 1)
                        if n >= 2:
                            act.wait_ge(hid_done, n - 1)
                        nc.scalar.activation(gate[:, n % 2, :], up[:, n % 2, 0, :], ACT.Silu,
                                             bias=B1[:, e, m:m + 1]).then_inc(gate_done, 1)
                        if c == 0 and u == 0:
                            for q in range(3, len(loads)):
                                weights_hi(q)
                        act.wait_ge(hid_done, n + 1)
                        if c and u == 0:
                            act.wait_ge(acc_done, 4 * c)
                        nc.scalar.activation(hT[0][:, u, :], hidden[:, n % 2, :], ACT.Copy).then_inc(hid_hi, 1)
                        if u == U // 2 and c + 1 < NC:
                            tokens_hi(c + 1)
                    if c:
                        act.wait_ge(acc_free, 4 * c)
                        act.dma_start(view(dst)[:, 4 * c - 4:4 * c, :], base[:, (c - 1) % 2, :, :]
                                      ).then_inc(stored[(c - 1) % 2], 16)
                act.wait_ge(acc_free, 4 * NC)
                act.dma_start(view(dst)[:, 4 * NC - 4:4 * NC, :], base[:, (NC - 1) % 2, :, :]
                              ).then_inc(stored[(NC - 1) % 2], 16)
                for r in range(2):
                    act.wait_ge(stored[r], 16 * (NC // 2))

            @block.vector
            def _(dve):
                def weights_lo(q):
                    W, n, _ = loads[q]
                    hi, lo = parts_of(W, n)
                    dve.wait_ge(w_hi, q + 1)
                    nc.vector.tensor_tensor(lo, raw[:, q % 3, :], hi.bitcast(FP32), ALU.subtract).then_inc(w_lo, 1)

                def tokens_lo(c):
                    for k in range(KD):
                        n = KD * c + k
                        dve.wait_ge(t_hi, n + 1)
                        nc.vector.tensor_tensor(T[1][:, c % 2, k, :], Tps[:, n % 2, :],
                                                T[0][:, c % 2, k, :].bitcast(FP32), ALU.subtract).then_inc(t_lo, 1)

                def results(c):
                    for j in range(4):
                        n = 4 * c + j
                        dve.wait_ge(acc_done, n + 1)
                        if j == 0:
                            dve.wait_ge(base_ready, c + 1)
                        slot = base[:, c % 2, j, :]
                        nc.vector.scalar_tensor_tensor(slot, acc[:, n % 2, 0:D], 1.0 / n_sh, slot, ALU.mult, ALU.add
                                                       ).then_inc(acc_free, 1)

                tokens_lo(0)
                for q in range(3):
                    weights_lo(q)
                dve.wait_ge(biases, 48)
                for c in range(NC):
                    for u in range(U):
                        n = c * U + u
                        e, m = divmod(u, HM)
                        if c == 0 and u == 1:
                            for q in range(3, len(loads)):
                                weights_lo(q)
                        dve.wait_ge(gate_done, n + 1)
                        dve.wait_ge(up_done, 2 * n + 2)
                        if n >= 2:
                            dve.wait_ge(hid_lo, n - 1)
                        nc.vector.scalar_tensor_tensor(hidden[:, n % 2, :], up[:, n % 2, 1, :], B2[:, e, m:m + 1],
                                                       gate[:, n % 2, :], ALU.add, ALU.mult).then_inc(hid_done, 1)
                        dve.wait_ge(hid_hi, n + 1)
                        nc.vector.tensor_tensor(hT[1][:, u, :], hidden[:, n % 2, :], hT[0][:, u, :].bitcast(FP32),
                                                ALU.subtract).then_inc(hid_lo, 1)
                        if u == U // 2 and c + 1 < NC:
                            tokens_lo(c + 1)
                    results(c)

            @block.tensor
            def _(pe):
                def tokens(c):
                    pe.wait_ge(rows_loaded[c % 2], 16 * (c // 2 + 1))
                    for k in range(KD):
                        n = KD * c + k
                        if n >= 2:
                            pe.wait_ge(t_lo, n - 1)
                        for j in range(4):
                            last = nc.tensor.transpose(Tps[:, n % 2, P * j:P * j + P],
                                                       rows[:, c % 2, j, P * k:P * k + P], chip.ident[:])
                        last.then_inc(t_done, 1)

                def down(c):
                    for j in range(4):
                        n = 4 * c + j
                        if n >= 2:
                            pe.wait_ge(acc_free, n - 1)
                        for u in range(U):
                            if j == 0:
                                pe.wait_ge(hid_lo, c * U + u + 1)
                            last = three_pass(nc, acc[:, n % 2, 0:D], [p[:, u, P * j:P * j + P] for p in hT],
                                              [p[:, u // HM, u % HM, :] for p in W3], u == 0, u == U - 1)
                        last.then_inc(acc_done, 1)

                tokens(0)
                for c in range(NC):
                    pe.wait_ge(t_lo, KD * (c + 1))
                    for u in range(U):
                        n = c * U + u
                        e, m = divmod(u, HM)
                        if n >= 2:
                            pe.wait_ge(hid_done, n - 1)
                        for half, W in enumerate((W1, W2)):
                            if c == 0 and m == 0:
                                pe.wait_ge(w_lo, 3 * e + half + 1)
                            for k in range(KD):
                                last = three_pass(nc, up[:, n % 2, half, :], [p[:, e, k, P * m:P * m + P] for p in W],
                                                  [p[:, c % 2, k, :] for p in T], k == 0, k == KD - 1)
                            last.then_inc(up_done, 1)
                        if u == U // 2 and c + 1 < NC:
                            tokens(c + 1)
                    if c == 0:
                        pe.wait_ge(w_lo, len(loads))
                    down(c)

        for s in [*raw_loaded, *rows_loaded, *base_loaded, *stored, *sent, prefetched, filled, *every]:
            nc.sync.sem_clear(s)
    nc.all_engine_barrier()


def routed_buffers(chip, stack, w1, w3):
    E, D, H = w1.shape
    sb = lambda n, s, d: stack.enter_context(chip.nc.sbuf_tensor(f"r_{n}", s, d))
    return sb("w1l", [P, E, D // P, H], FR), sb("w3", [P, E, H // P, D], FP32)


def routed_stage(chip, sorted_dram, sorted_meta, W1_raw, w2, W3, b1, b2, b3, tile_expert, tile_rows, dst):
    nc, D, KD = chip.nc, chip.D, chip.KD
    E, _, H = w2.shape
    HM = H // P
    TILES = tile_expert.shape[1]
    WB = 2 * H + D
    with ExitStack() as st:
        sb = lambda n, s, d=FP32: st.enter_context(nc.sbuf_tensor(f"r_{n}", s, d))
        pb = lambda n, s: st.enter_context(nc.psum_tensor(f"r_{n}", s, FP32))
        W1 = [sb("w1h", [P, E, KD, H], FR), W1_raw]
        W2 = [sb(f"w2{p}", [P, E, KD, H], FR) for p in "hl"]
        b_hi = sb("b_hi", [64, WB], FR)[:]
        brows = sb("brows", [64, WB], FR)
        ones = sb("ones", [64, P])
        sel = sb("sel", [64, 2, P], FR)
        rows, out, row_meta = sb("rows", [P, 2, D]), sb("out", [P, 2, D]), sb("row_meta", [P, 2, 2])
        T = [sb(f"T{p}", [P, 2, KD, P], FR) for p in "hl"]
        gate_hidden, hT = sb("gate_hidden", [P, 4, H]), sb("hT", [P, 2, HM, P])
        gate, hidden = gate_hidden[:, 0:2, :], gate_hidden[:, 2:4, :]
        raw_b = gate_hidden[0:64, :, :].rearrange("p a h -> p (a h)")[:, 0:WB]
        up, Tps, Gps, acc = (pb("up", [P, 2, 2, H]), pb("Tps", [P, KD, P]), pb("Gps", [P, HM, P]),
                             pb("acc", [P, 2, 512]))
        rows_loaded = chip.sems(st, "r_rows_loaded0", "r_rows_loaded1")
        meta_loaded = chip.sems(st, "r_meta_loaded0", "r_meta_loaded1")
        w2_loaded = chip.sems(st, *[f"r_w2_loaded{e}" for e in range(E)])
        (added,) = chip.pool_sems("r_added")
        (b_loaded, w_hi, w_lo, b_zero, b_split, sel_ready, t_done, t_hi, t_lo, up_done, gate_done,
         hid_done, g_done, g_copied, acc_done, out_ready, handed) = every = chip.sems(
            st, *[f"r_{n}" for n in ("b_loaded", "w_hi", "w_lo", "b_zero", "b_split", "sel_ready",
                                     "t_done", "t_hi", "t_lo", "up_done", "gate_done", "hid_done", "g_done",
                                     "g_copied", "acc_done", "out_ready", "handed")])
        splits = [(W, e) for e in range(E) for W in (W1, W2)]
        flat = lambda a: a.rearrange("p k h -> p (k h)")

        def pairs(engine, body):
            for j in range(2):
                body(j, j, True, False)
            with engine.Fori(1, TILES // 2 - 1) as i:
                for j in range(2):
                    body(2 * i + j, j, False, False)
            for j in range(2):
                body(TILES - 2 + j, j, False, j == 1)

        with nc.Block() as block:

            @block.sync
            def _(sp):
                sp.wait_ge(b_zero, 2)
                for half in range(2):
                    for col, b in ((0, b1), (H, b2), (2 * H, b3)):
                        sp.dma_start(raw_b[32 * half:32 * half + E, col:col + b.shape[1]], b).then_inc(b_loaded, 16)
                for e in range(E):
                    sp.dma_start(W2[1][:, e, :, :].bitcast(FP32), w2[e].rearrange("(k p) h -> p k h", p=P)
                                 ).then_inc(w2_loaded[e], 16)

                def load_rows(n, j):
                    sp.dma_start(rows[:, j, :], sorted_dram[bass.ds(n * P, P), :]).then_inc(rows_loaded[j], 16)

                def body(n, j, first, last):
                    if not last:
                        if not (first and j == 0):
                            sp.wait_ge(t_done, n)
                        load_rows(n + 1, 1 - j)
                    if not first:
                        sp.wait_ge(added, 16 * (n - 1))
                    sp.dma_start(row_meta[:, j, :], sorted_meta[bass.ds(n * P, P), :]).then_inc(meta_loaded[j], 16)

                load_rows(0, 0)
                pairs(sp, body)

            @block.gpsimd
            def _(pool):
                nc.gpsimd.memset(ones[:], 1.0).then_inc(b_zero, 1)
                nc.gpsimd.memset(raw_b, 0.0).then_inc(b_zero, 1)

                def body(n, j, first, last):
                    pool.wait_ge(out_ready, n + 1)
                    if not (first and j == 0):
                        pool.wait_ge(added, 16 * n)
                    pool.sem_inc(handed, 1)
                    nc.gpsimd.indirect_dma_start(
                        out=dst[:, :], out_offset=bass.IndirectOffsetOnAxis(ap=row_meta[:, j, 0:1].bitcast(I32), axis=0),
                        in_=out[:, j, :], in_offset=None, compute_op=ALU.add).then_inc(added, 16)

                pairs(pool, body)
                pool.wait_ge(added, 16 * TILES)

            @block.scalar
            def _(act):
                act.wait_ge(b_loaded, 96)
                nc.scalar.activation(b_hi, raw_b, ACT.Copy).then_inc(b_split, 1)
                for W, e in splits:
                    if W is W2:
                        act.wait_ge(w2_loaded[e], 16)
                    nc.scalar.activation(flat(W[0][:, e, :, :]), flat(W[1][:, e, :, :]).bitcast(FP32), ACT.Copy
                                         ).then_inc(w_hi, 1)

                def tokens_hi(n, j, first):
                    act.wait_ge(t_done, n + 1)
                    if not first:
                        act.wait_ge(up_done, 2 * n - 2)
                    nc.scalar.activation(T[0][:, j, :, :], Tps[:], ACT.Copy).then_inc(t_hi, 1)

                def body(n, j, first, last):
                    act.wait_ge(up_done, 2 * n + 1)
                    if not first:
                        act.wait_ge(hid_done, n - 1)
                    nc.scalar.activation(gate[:, j, :], up[:, j, 0, :], ACT.Silu).then_inc(gate_done, 1)
                    if not (first and j == 0):
                        copied(n - 1, 1 - j, first)
                    if not last:
                        tokens_hi(n + 1, 1 - j, first and j == 0)

                def copied(n, j, first):
                    act.wait_ge(g_done, n + 1)
                    if not first:
                        act.wait_ge(acc_done, n - 1)
                    nc.scalar.activation(hT[:, j, :, :], Gps[:], ACT.Copy).then_inc(g_copied, 1)

                tokens_hi(0, 0, True)
                pairs(act, body)
                copied(TILES - 1, 1, False)

            @block.vector
            def _(dve):
                dve.wait_ge(b_split, 1)
                nc.vector.tensor_copy(brows[0:32, :], b_hi[0:32, :].bitcast(FP32)).then_inc(b_split, 1)
                nc.vector.tensor_tensor(brows[32:64, :], raw_b[32:64, :], b_hi[32:64, :].bitcast(FP32),
                                        ALU.subtract).then_inc(b_split, 1)
                for q, (W, e) in enumerate(splits):
                    dve.wait_ge(w_hi, q + 1)
                    hi, lo = (flat(part[:, e, :, :]) for part in W)
                    nc.vector.tensor_tensor(lo, lo.bitcast(FP32), hi.bitcast(FP32), ALU.subtract).then_inc(w_lo, 1)

                def select(n, j, first):
                    if not first:
                        dve.wait_ge(up_done, 2 * n - 2)
                    nc.vector.tensor_scalar(sel[:, j, :], ones[:], tile_rows[:, bass.ds(n, 1)], None, ALU.mult
                                            ).then_inc(sel_ready, 1)

                def tokens_lo(n, j):
                    dve.wait_ge(t_hi, n + 1)
                    nc.vector.tensor_tensor(T[1][:, j, :, :], Tps[:], T[0][:, j, :, :].bitcast(FP32), ALU.subtract
                                            ).then_inc(t_lo, 1)

                def output(n, j, first):
                    dve.wait_ge(acc_done, n + 1)
                    if not first:
                        dve.wait_ge(added, 16 * (n - 1))
                    dve.wait_ge(meta_loaded[j], 16 if first else 8 * (n - j) + 16)
                    nc.vector.tensor_scalar(out[:, j, :], acc[:, j, 0:D], row_meta[:, j, 1:2], None, ALU.mult
                                            ).then_inc(out_ready, 1)

                def body(n, j, first, last):
                    if not last:
                        select(n + 1, 1 - j, first and j == 0)
                        tokens_lo(n + 1, 1 - j)
                    dve.wait_ge(gate_done, n + 1)
                    dve.wait_ge(up_done, 2 * n + 2)
                    if not first:
                        dve.wait_ge(g_done, n - 1)
                    nc.vector.tensor_tensor(hidden[:, j, :], up[:, j, 1, :], gate[:, j, :], ALU.mult
                                            ).then_inc(hid_done, 1)
                    if not (first and j == 0):
                        output(n - 1, 1 - j, first)

                dve.wait_ge(b_zero, 2)
                select(0, 0, True)
                tokens_lo(0, 0)
                pairs(dve, body)
                output(TILES - 1, 1, False)

            @block.tensor
            def _(pe):
                def tokens(n, j, loaded):
                    pe.wait_ge(rows_loaded[j], loaded)
                    for k in range(KD):
                        last = nc.tensor.transpose(Tps[:, k, :], rows[:, j, P * k:P * k + P], chip.ident[:])
                    last.then_inc(t_done, 1)

                def turned(n, j, first):
                    pe.wait_ge(hid_done, n + 1)
                    if not (first and j == 0):
                        pe.wait_ge(g_copied, n)
                    for k in range(HM):
                        last = nc.tensor.transpose(Gps[:, k, :], hidden[:, j, P * k:P * k + P], chip.ident[:])
                    last.then_inc(g_done, 1)

                def down(n, j, first):
                    expert = expert_of(n)
                    pe.wait_ge(g_copied, n + 1)
                    for k in range(HM):
                        last = nc.tensor.matmul(acc[:, j, 0:D], hT[:, j, k, :], W3[:, bass.ds(expert, 1), k, :],
                                                start=False, stop=k == HM - 1)
                    last.then_inc(acc_done, 1)

                def expert_of(n):
                    return nc.tensor.value_load(tile_expert[0:1, bass.ds(n, 1)], min_val=0, max_val=E - 1)

                def body(n, j, first, last):
                    expert = expert_of(n)
                    pe.wait_ge(t_lo, n + 1)
                    pe.wait_ge(sel_ready, n + 1)
                    if not first:
                        pe.wait_ge(hid_done, n - 1)
                    for half, W in enumerate((W1, W2)):
                        bank = up[:, j, half, :]
                        nc.tensor.matmul(bank, sel[:, j, :], brows[:, half * H:half * H + H], start=True, stop=False)
                        for k in range(KD):
                            last_up = three_pass(nc, bank, [p[:, j, k, :] for p in T],
                                                 [p[:, bass.ds(expert, 1), k, :] for p in W], False, k == KD - 1)
                        if half == 0:
                            last_up.then_inc(up_done, 1)
                            if not (first and j == 0):
                                turned(n - 1, 1 - j, first)
                            if not last:
                                tokens(n + 1, 1 - j, 8 * (n + 1 - (1 - j)) + 16)
                            if not first:
                                pe.wait_ge(out_ready, n - 1)
                            nc.tensor.matmul(acc[:, j, 0:D], sel[:, j, :], brows[:, 2 * H:WB], start=True, stop=False)
                    last_up.then_inc(up_done, 1)
                    if not (first and j == 0):
                        down(n - 1, 1 - j, first)

                pe.wait_ge(w_lo, len(splits))
                pe.wait_ge(b_split, 3)
                tokens(0, 0, 16)
                pairs(pe, body)
                turned(TILES - 1, 1, False)
                down(TILES - 1, 1, False)

        for s in [*w2_loaded, *rows_loaded, *meta_loaded, added, *every]:
            nc.sync.sem_clear(s)
    nc.all_engine_barrier()


def rank_stage(chip, ranking, picked, row_index, picked_row, thresholds, limit):
    nc, NT, B = chip.nc, chip.NT, chip.B
    NA, S = B * NT, chip.S
    w, rank = ranking.weights, ranking.rank
    K = 2 * P
    with ExitStack() as st:
        sb = lambda n, s, d=FP32: st.enter_context(nc.sbuf_tensor(f"k_{n}", s, d))
        pb = lambda n, s: st.enter_context(nc.psum_tensor(f"k_{n}", s, FP32))
        last_row = sb("last_row", [P, P])
        rank_no, index_cols = sb("rank_no", [P, K]), sb("index_cols", [P, NT, P])
        pairs = sb("pairs", [P, NA, 2])
        hot = sb("hot", [P, 4, K])
        clamped = sb("clamped", [P, B, 2])
        list_ps = pb("list_ps", [P, 2, 512])
        row_ps, thr_ps = pb("row_ps", [P, K]), pb("thr_ps", [P, 1])
        made, chain, hot_ready, hot_used, listed, list_copied, thr_done = every = chip.sems(
            st, *[f"k_{n}" for n in ("made", "chain", "hot_ready", "hot_used", "listed", "list_copied", "thr_done")])

        with nc.Block() as block:

            @block.gpsimd
            def _(pool):
                g = nc.gpsimd
                g.memset(last_row[:], 0.0).then_inc(made, 1)
                g.iota(rank_no[:], pattern=[[1, K]], base=0, channel_multiplier=0,
                       allow_small_or_imprecise_dtypes=True).then_inc(made, 1)
                g.iota(index_cols[:], pattern=[[P, NT], [0, P]], base=0, channel_multiplier=1,
                       allow_small_or_imprecise_dtypes=True).then_inc(made, 1)
                pool.wait_ge(made, 3)
                g.affine_select(out=last_row[:], in_=last_row[:], compare_op=ALU.not_equal, fill=1.0, base=-(P - 1),
                                pattern=[[0, P]], channel_multiplier=1).then_inc(made, 1)

            @block.vector
            def _(dve):
                V = nc.vector
                links = [0]

                def link(ins):
                    links[0] += 1
                    ins.then_inc(chain, 1)
                    dve.wait_ge(chain, links[0])

                dve.wait_ge(made, 4)
                V.tensor_copy(pairs[:, :, 1], w[:])
                for b in range(B):
                    link(V.tensor_copy(pairs[:, b * NT:(b + 1) * NT, 0], index_cols[:, :, 0]))
                for b in range(B):
                    for i in range(NT):
                        t = b * NT + i
                        if t >= 4:
                            dve.wait_ge(hot_used, t - 3)
                        V.tensor_scalar(hot[:, t % 4, :], rank_no[:], rank[:, t:t + 1], None, ALU.is_equal
                                        ).then_inc(hot_ready, 1)
                    dve.wait_ge(listed, b + 1)
                    V.tensor_copy(picked[:, b, :, :], list_ps[:, :, 0:2])
                    V.tensor_scalar_min(picked_row[:, b, :], row_ps[:], float(limit)).then_inc(list_copied, 1)
                    dve.wait_ge(list_copied, b + 1)
                    link(V.tensor_scalar_add(row_index[:, b, :, 0], picked[:, b, :, 0], float(b * S)))
                    link(V.tensor_scalar(clamped[:, b, :], picked[:, b, :, 0], float(limit), float(b * (limit + 1)),
                                         ALU.min, ALU.add))
                    link(V.tensor_copy(row_index[:, b, :, 1], clamped[:, b, :]))
                    dve.wait_ge(thr_done, b + 1)
                    link(V.tensor_copy(thresholds[:, b:b + 1], thr_ps[:]))

            @block.tensor
            def _(pe):
                for b in range(B):
                    if b:
                        pe.wait_ge(list_copied, b)
                    for i in range(NT):
                        t = b * NT + i
                        pe.wait_ge(hot_ready, t + 1)
                        if i == 0 and b == 0:
                            pe.wait_ge(chain, B)
                        for h in range(2):
                            nc.tensor.matmul(list_ps[:, h, 0:2], hot[:, t % 4, P * h:P * h + P], pairs[:, t, :],
                                             start=i == 0, stop=i == NT - 1)
                        last = nc.tensor.matmul(row_ps[:], index_cols[:, i, :], hot[:, t % 4, :], start=i == 0,
                                                stop=i == NT - 1)
                        last.then_inc(hot_used, 1)
                        if i == NT - 1:
                            pe.wait_ge(hot_used, t + 1)
                            pe.sem_inc(listed, 1)
                    pe.wait_ge(list_copied, b + 1)
                    nc.tensor.matmul(thr_ps[:], last_row[:], picked[:, b, 1, 1:2], start=True, stop=True
                                     ).then_inc(thr_done, 1)

        for s in every:
            nc.sync.sem_clear(s)
    nc.all_engine_barrier()


def newton_rsqrt(nc, link, r, std, v, tmp):
    V = nc.vector
    link(V.reciprocal(r, std))
    link(V.tensor_tensor(tmp, r, r, ALU.mult))
    link(V.tensor_tensor(tmp, tmp, v, ALU.mult))
    link(V.tensor_scalar(tmp, tmp, -0.5, 1.5, ALU.mult, ALU.add))
    link(V.tensor_tensor(r, r, tmp, ALU.mult))


def picked_stage(chip, xn_dram, positions, mask, row_index, picked_row, picked, thresholds, inverse, ln1, ln2, w, w_ffn,
                 out_dram, HEADS):
    nc, B, D, KD = chip.nc, chip.B, chip.D, chip.KD
    G = 2 * B
    hd = D // HEADS
    HALF = hd // 2
    PAD = 32
    HG = P // PAD
    NH = HEADS // HG
    M = mask.shape[1]
    MT = M // P
    F = w_ffn["w1"][0].shape[2]
    FM = F // P
    TWO_PI = 6.283185307179586
    C1 = 6.28125
    C2 = round((TWO_PI - C1) * 2 ** 20) / 2 ** 20
    C3 = TWO_PI - C1 - C2
    PI_BELOW = 3.1415925

    with ExitStack() as outer:
        osb = lambda n, s, d=FP32: outer.enter_context(nc.sbuf_tensor(f"p_{n}", s, d))
        xs = osb("xs", [P, G, D])
        heads_T = {n: osb(f"{n}T", [P, G, NH, P]) for n in "qk"}
        vals = osb("vals", [P, G, D])
        msel = osb("msel", [P, G, 2 * P])
        o_all = osb("o_all", [P, G, D])
        small = lambda n: osb(n, [P, G])
        ss, vv, std, rr, tmp = (small(n) for n in ("ss", "vv", "std", "rr", "tmp"))

        with ExitStack() as st:
            sb = lambda n, s, d=FP32: st.enter_context(nc.sbuf_tensor(f"p_{n}", s, d))
            pb = lambda n, s: st.enter_context(nc.psum_tensor(f"p_{n}", s, FP32))
            pos, posf = sb("pos", [P, G], I32), sb("posf", [P, G])
            rows = sb("mask_rows", [P, 2, M])
            rowsT = sb("mask_rowsT", [P, MT, P])
            col_no = sb("col_no", [P, MT])
            hot = sb("col_hot", [P, MT, 2 * P])
            inv, ang, turns_i, turns = (sb("inv", [P, HALF]), sb("ang", [P, G, HALF]), sb("turns_i", [P, G, HALF], I32),
                                        sb("turns", [P, G, HALF]))
            ang2 = sb("ang2", [P, G, HALF])
            sin, cos = sb("sin", [P, G, HALF]), sb("cos", [P, G, HALF])
            sq, hn = sb("sq", [P, D]), sb("hn", [P, G, D])
            hT = [sb(f"hT{p}", [P, KD, G * P], FR) for p in "hl"]
            padded = sb("padded", [P, 2, HEADS, PAD])
            rot = [sb(f"rot{i}", [P, HEADS, HALF]) for i in range(2)]
            Tps, qkv = pb("Tps", [P, 2, 512]), pb("qkv", [P, 2, 512])
            Hps = pb("Hps", [P, 512])
            Mps, Sps = pb("Mps", [P, 2, 512]), pb("Sps", [P, 2 * P])
            m_loaded = chip.pool_sems("p_m_loaded0", "p_m_loaded1")
            x_loaded, p_loaded = chip.pool_sems("p_x_loaded", "p_p_loaded")
            (inv_loaded, made, chain, sq_done, v_ready, std_ready, hn_ready, t_done, t_hi, t_lo,
             qkv_done, qkv_read, pad_ready, ht_done, ht_copied, ang_ready, trig_ready, hot_ready, m_done, m_copied,
             s_done, s_copied) = every = chip.sems(
                st, *[f"p_{n}" for n in (
                    "inv_loaded", "made", "chain", "sq_done", "v_ready", "std_ready",
                    "hn_ready", "t_done", "t_hi", "t_lo", "qkv_done", "qkv_read", "pad_ready", "ht_done", "ht_copied",
                    "ang_ready", "trig_ready", "hot_ready", "m_done", "m_copied", "s_done", "s_copied")])
            offset = lambda g, which: bass.IndirectOffsetOnAxis(ap=row_index[:, g // 2, g % 2, which:which + 1], axis=0)

            value_bank = lambda g: Tps[:, g % 2, D:2 * D]

            with nc.Block() as block:

                @block.sync
                def _(sp):
                    sp.dma_start(inv[:], inverse.to_broadcast([P, HALF])).then_inc(inv_loaded, 16)

                @block.gpsimd
                def _(pool):
                    g_ = nc.gpsimd
                    for g in range(G):
                        g_.indirect_dma_start(out=xs[:, g, :], out_offset=None, in_=xn_dram[:, :],
                                              in_offset=offset(g, 0)).then_inc(x_loaded, 16)
                    for g in range(G):
                        g_.indirect_dma_start(out=pos[:, g:g + 1], out_offset=None, in_=positions[:, :],
                                              in_offset=offset(g, 1)).then_inc(p_loaded, 16)
                    g_.iota(col_no[:], pattern=[[P, MT]], base=0, channel_multiplier=1,
                            allow_small_or_imprecise_dtypes=True).then_inc(made, 1)
                    g_.memset(padded[:], 0.0).then_inc(made, 1)
                    for g in range(G):
                        if g >= 2:
                            pool.wait_ge(m_done, 2 * (g - 1))
                        g_.indirect_dma_start(out=rows[:, g % 2, :], out_offset=None, in_=mask[:, :],
                                              in_offset=offset(g, 1)).then_inc(m_loaded[g % 2], 16)

                @block.scalar
                def _(act):
                    act.wait_ge(x_loaded, 16 * G)
                    for g in range(G):
                        if g:
                            act.wait_ge(sq_done, g)
                        nc.scalar.activation(sq[:], xs[:, g, :], ACT.Square, accum_out=ss[:, g:g + 1]
                                             ).then_inc(sq_done, 1)
                    act.wait_ge(v_ready, 1)
                    nc.scalar.activation(std[:], vv[:], ACT.Sqrt).then_inc(std_ready, 1)
                    for g in range(G):
                        act.wait_ge(t_done, g + 1)
                        for k in range(KD):
                            nc.scalar.activation(hT[0][:, k, P * g:P * g + P], Tps[:, g % 2, P * k:P * k + P], ACT.Copy,
                                                 scale=ln1[:, k:k + 1]).then_inc(t_hi, 1)
                    act.wait_ge(ang_ready, 1)
                    nc.scalar.activation(sin[:], ang[:], ACT.Sin).then_inc(trig_ready, 1)
                    nc.scalar.activation(cos[:], ang2[:], ACT.Sin).then_inc(trig_ready, 1)
                    n = 0
                    for g in range(G):
                        act.wait_ge(qkv_done, 3 * g + 3)
                        nc.scalar.activation(vals[:, g, :], value_bank(g), ACT.Copy
                                             ).then_inc(qkv_read, 1)
                        for i, name in enumerate("qk"):
                            n += 1
                            act.wait_ge(ht_done, n)
                            nc.scalar.activation(heads_T[name][:, g, :, :], Hps[:].rearrange("p (a q) -> p a q", a=NH),
                                                 ACT.Copy).then_inc(ht_copied, 1)

                @block.vector
                def _(dve):
                    V = nc.vector
                    links = [0]

                    def link(ins):
                        links[0] += 1
                        ins.then_inc(chain, 1)
                        dve.wait_ge(chain, links[0])

                    dve.wait_ge(sq_done, G)
                    link(V.tensor_scalar(vv[:], ss[:], 1.0 / D, 1e-6, ALU.mult, ALU.add))
                    V.tensor_copy(tmp[:], vv[:]).then_inc(v_ready, 1)
                    dve.wait_ge(std_ready, 1)
                    newton_rsqrt(nc, link, rr[:], std[:], vv[:], tmp[:])
                    for g in range(G):
                        V.tensor_scalar(hn[:, g, :], xs[:, g, :], rr[:, g:g + 1], None, ALU.mult).then_inc(hn_ready, 1)
                    dve.wait_ge(p_loaded, 16 * G)
                    dve.wait_ge(inv_loaded, 16)
                    link(V.tensor_copy(posf[:], pos[:]))
                    wide = lambda a: a.rearrange("p (g o) -> p g o", o=1).to_broadcast([P, G, HALF])
                    link(V.tensor_tensor(ang[:], wide(posf[:]),
                                         inv[:].rearrange("p (o h) -> p o h", o=1).to_broadcast([P, G, HALF]), ALU.mult))
                    flat = lambda a: a[:].rearrange("p g h -> p (g h)")
                    link(V.tensor_scalar(flat(turns_i), flat(ang), 1.0 / TWO_PI, None, ALU.mult))
                    link(V.tensor_copy(turns[:], turns_i[:]))
                    for c in (C1, C2, C3):
                        link(V.scalar_tensor_tensor(flat(ang), flat(turns), -c, flat(ang), ALU.mult, ALU.add))
                    link(V.tensor_scalar_add(flat(ang2), flat(ang), TWO_PI / 4))
                    link(V.tensor_scalar(flat(turns), flat(ang2), TWO_PI / 2, -TWO_PI, ALU.is_gt, ALU.mult))
                    link(V.tensor_tensor(flat(ang2), flat(ang2), flat(turns), ALU.add))
                    for a in (ang, ang2):
                        link(V.tensor_scalar(flat(a), flat(a), PI_BELOW, -PI_BELOW, ALU.min, ALU.max))
                    V.tensor_copy(flat(turns), flat(ang2)).then_inc(ang_ready, 1)
                    for g in range(G):
                        for k in range(KD):
                            dve.wait_ge(t_hi, KD * (g + 1))
                            cols = slice(P * g, P * g + P)
                            V.scalar_tensor_tensor(hT[1][:, k, cols], Tps[:, g % 2, P * k:P * k + P], ln1[:, k:k + 1],
                                                   hT[0][:, k, cols].bitcast(FP32), ALU.mult, ALU.subtract
                                                   ).then_inc(t_lo, 1)
                    dve.wait_ge(trig_ready, 2)
                    dve.wait_ge(made, 2)
                    n = 0
                    for g in range(G):
                        bc = lambda a: a[:, g:g + 1, :].to_broadcast([P, HEADS, HALF])
                        for i, name in enumerate("qk"):
                            dve.wait_ge(qkv_done, 3 * g + i + 1)
                            t = qkv[:, i, 0:D].rearrange("p (h c) -> p h c", h=HEADS)
                            t1, t2 = t[:, :, 0:HALF], t[:, :, HALF:hd]
                            if n >= 2:
                                dve.wait_ge(ht_done, n - 1)
                            out = padded[:, i, :, :]
                            link(V.tensor_tensor(rot[0][:], t1, bc(cos), ALU.mult))
                            link(V.tensor_tensor(rot[1][:], t2, bc(sin), ALU.mult))
                            link(V.tensor_tensor(out[:, :, 0:HALF], rot[0][:], rot[1][:], ALU.subtract))
                            link(V.tensor_tensor(rot[0][:], t2, bc(cos), ALU.mult))
                            link(V.tensor_tensor(rot[1][:], t1, bc(sin), ALU.mult))
                            V.tensor_tensor(out[:, :, HALF:hd], rot[0][:], rot[1][:], ALU.add).then_inc(pad_ready, 1)
                            n += 1
                            dve.wait_ge(pad_ready, n)
                    for b in range(B):
                        if b:
                            dve.wait_ge(s_done, 2 * b)
                        for c in range(MT):
                            ins = V.tensor_scalar(hot[:, c, :], picked_row[:, b, :], col_no[:, c:c + 1], None,
                                                  ALU.is_equal)
                        ins.then_inc(hot_ready, 1)
                        for g in (2 * b, 2 * b + 1):
                            for h in range(2):
                                dve.wait_ge(m_done, 2 * g + h + 1)
                                if g and h == 0:
                                    dve.wait_ge(s_done, g)
                                V.tensor_copy(rowsT[:, 4 * h:4 * h + 4, :].rearrange("p a q -> p (a q)"), Mps[:, h, :]
                                              ).then_inc(m_copied, 1)
                            dve.wait_ge(s_done, g + 1)
                            link(V.tensor_copy(msel[:, g, :], Sps[:]))
                            V.memset(msel[:, g, 2 * P - 1:2 * P], MASKED).then_inc(s_copied, 1)

                @block.tensor
                def _(pe):
                    for g in range(G):
                        pe.wait_ge(hn_ready, g + 1)
                        if g >= 2:
                            pe.wait_ge(t_lo, KD * (g - 1))
                        for k in range(KD):
                            last = nc.tensor.transpose(Tps[:, g % 2, P * k:P * k + P], hn[:, g, P * k:P * k + P],
                                                       chip.ident[:])
                        last.then_inc(t_done, 1)
                    pe.wait_ge(t_lo, KD * G)
                    pe.wait_ge(made, 2)
                    n = 0
                    for g in range(G):
                        for i, name in enumerate(("wq", "wk", "wv")):
                            bank = qkv[:, i, 0:D] if i < 2 else value_bank(g)
                            if g and i < 2:
                                pe.wait_ge(pad_ready, 2 * g - 1 + i)
                            if g >= 2 and i == 2:
                                pe.wait_ge(qkv_read, g - 1)
                            for k in range(KD):
                                last = three_pass(nc, bank, [p[:, k, P * g:P * g + P] for p in hT],
                                                  [p[:, k, :] for p in w[name]], k == 0, k == KD - 1)
                            last.then_inc(qkv_done, 1)
                        for i in range(2):
                            pe.wait_ge(pad_ready, n + 1)
                            if n:
                                pe.wait_ge(ht_copied, n)
                            for a in range(NH):
                                src = padded[:, i, HG * a:HG * a + HG, :].rearrange("p h c -> p (h c)")
                                last = nc.tensor.transpose(Hps[:, P * a:P * a + P], src, chip.ident[:])
                            last.then_inc(ht_done, 1)
                            n += 1
                    for g in range(G):
                        pe.wait_ge(m_loaded[g % 2], 16 * (g // 2 + 1))
                        for h in range(2):
                            if g:
                                pe.wait_ge(m_copied, 2 * g - 1 + h)
                            for c in range(4):
                                last = nc.tensor.transpose(Mps[:, h, P * c:P * c + P],
                                                           rows[:, g % 2, P * (4 * h + c):P * (4 * h + c) + P],
                                                           chip.ident[:])
                            last.then_inc(m_done, 1)
                        pe.wait_ge(m_copied, 2 * g + 2)
                        pe.wait_ge(hot_ready, g // 2 + 1)
                        if g:
                            pe.wait_ge(s_copied, g)
                        for c in range(MT):
                            last = nc.tensor.matmul(Sps[:], rowsT[:, c, :], hot[:, c, :], start=c == 0, stop=c == MT - 1)
                        last.then_inc(s_done, 1)

            for s in [*m_loaded, x_loaded, p_loaded, *every]:
                nc.sync.sem_clear(s)
        nc.all_engine_barrier()

        with ExitStack() as st:
            sb = lambda n, s, d=FP32: st.enter_context(nc.sbuf_tensor(f"p_{n}", s, d))
            pb = lambda n, s: st.enter_context(nc.psum_tensor(f"p_{n}", s, FP32))
            masked, probs = sb("masked", [P, 2, 2, 2 * P]), sb("probs", [P, 2, 2, 2 * P])
            neg_max, sums = sb("neg_max", [P, G, HEADS]), sb("sums", [P, G, HEADS])
            pT = sb("pT", [P, 2, 4, P])
            S_ps, T_ps, O_ps = pb("S_ps", [P, 2, 2, 2 * P]), pb("T_ps", [P, 2, 4, P]), pb("O_ps", [P, 2, 512])
            (qk_done, masked_ready, max_done, exp_done, pt_done, pt_copied, pv_done, o_read, chain) = every = chip.sems(
                st, *[f"p_{n}" for n in ("qk_done", "masked_ready", "max_done", "exp_done", "pt_done", "pt_copied",
                                         "pv_done", "o_read", "chain2")])
            NP = HEADS // 2
            units = [(g, h2) for g in range(G) for h2 in range(NP)]
            head = lambda h2, j: (2 * (h2 // HG) + j) * HG + h2 % HG

            with nc.Block() as block:

                @block.tensor
                def _(pe):
                    def scores(n):
                        g, h2 = units[n]
                        if n >= 2:
                            pe.wait_ge(masked_ready, n - 1)
                        for j in range(2):
                            a, r = divmod(head(h2, j), HG)
                            rows_ = slice(PAD * r, PAD * r + PAD)
                            keys = heads_T["k"][rows_, 2 * (g // 2):2 * (g // 2) + 2, a, :]
                            last = nc.tensor.matmul(S_ps[:, n % 2, j, :].rearrange("p (t k) -> p t k", t=2),
                                                    heads_T["q"][rows_, g, a, :], keys, start=True, stop=True)
                        last.then_inc(qk_done, 1)

                    def products(n):
                        g, h2 = units[n]
                        pe.wait_ge(exp_done, 2 * n + 2)
                        if n >= 2:
                            pe.wait_ge(pt_copied, n - 1)
                        for j in range(2):
                            for t in range(2):
                                last = nc.tensor.transpose(T_ps[:, n % 2, 2 * j + t, :],
                                                           probs[:, n % 2, j, P * t:P * t + P], chip.ident[:])
                        last.then_inc(pt_done, 1)

                    def values(n):
                        g, h2 = units[n]
                        pe.wait_ge(pt_copied, n + 1)
                        if h2 == 0 and g >= 2:
                            pe.wait_ge(o_read, g - 1)
                        for j in range(2):
                            h = head(h2, j)
                            for t in range(2):
                                last = nc.tensor.matmul(O_ps[:, g % 2, hd * h:hd * h + hd], pT[:, n % 2, 2 * j + t, :],
                                                        vals[:, 2 * (g // 2) + t, hd * h:hd * h + hd],
                                                        start=t == 0, stop=t == 1)
                        last.then_inc(pv_done, 1)

                    N = len(units)
                    for n in range(N + 2):
                        if n < N:
                            scores(n)
                        if 1 <= n <= N:
                            products(n - 1)
                        if n >= 2:
                            values(n - 2)

                @block.vector
                def _(dve):
                    V = nc.vector
                    links = [0]

                    def link(ins):
                        links[0] += 1
                        ins.then_inc(chain, 1)
                        dve.wait_ge(chain, links[0])

                    def finish(g):
                        dve.wait_ge(pv_done, NP * (g + 1))
                        dve.wait_ge(exp_done, 2 * NP * (g + 1))
                        link(V.reciprocal(sums[:, g, :], sums[:, g, :]))
                        V.tensor_tensor(o_all[:, g, :].rearrange("p (h c) -> p h c", h=HEADS),
                                        O_ps[:, g % 2, 0:D].rearrange("p (h c) -> p h c", h=HEADS),
                                        sums[:, g, :].rearrange("p (h o) -> p h o", o=1).to_broadcast([P, HEADS, hd]),
                                        ALU.mult).then_inc(o_read, 1)

                    for n, (g, h2) in enumerate(units):
                        dve.wait_ge(qk_done, n + 1)
                        if n >= 2:
                            dve.wait_ge(exp_done, 2 * n - 2)
                        V.tensor_tensor(masked[:, n % 2, :, :], S_ps[:, n % 2, :, :],
                                        msel[:, g:g + 1, :].to_broadcast([P, 2, 2 * P]), ALU.add
                                        ).then_inc(masked_ready, 1)
                        dve.wait_ge(masked_ready, n + 1)
                        V.tensor_reduce(neg_max[:, g, 2 * h2:2 * h2 + 2], masked[:, n % 2, :, :], AX.X, ALU.max,
                                        negate=True).then_inc(max_done, 1)
                        if h2 == 3 and g:
                            finish(g - 1)
                    finish(G - 1)

                @block.scalar
                def _(act):
                    def exponentials(n):
                        g, h2 = units[n]
                        act.wait_ge(max_done, n + 1)
                        if n >= 2:
                            act.wait_ge(pt_done, n - 1)
                        for j in range(2):
                            h = head(h2, j)
                            nc.scalar.activation(probs[:, n % 2, j, :], masked[:, n % 2, j, :], ACT.Exp,
                                                 bias=neg_max[:, g, 2 * h2 + j:2 * h2 + j + 1], accum_out=sums[:, g, h:h + 1]
                                                 ).then_inc(exp_done, 1)

                    def copies(n):
                        act.wait_ge(pt_done, n + 1)
                        if n >= 2:
                            act.wait_ge(pv_done, n - 1)
                        nc.scalar.activation(pT[:, n % 2, :, :], T_ps[:, n % 2, :, :], ACT.Copy).then_inc(pt_copied, 1)

                    for n in range(len(units) + 1):
                        if n < len(units):
                            exponentials(n)
                        if n:
                            copies(n - 1)

            for s in every:
                nc.sync.sem_clear(s)
        nc.all_engine_barrier()

        with ExitStack() as st:
            sb = lambda n, s, d=FP32: st.enter_context(nc.sbuf_tensor(f"p_{n}", s, d))
            pb = lambda n, s: st.enter_context(nc.psum_tensor(f"p_{n}", s, FP32))
            oT = [sb(f"oT{p}", [P, KD, G * P], FR) for p in "hl"]
            fT = [sb(f"fT{p}", [P, KD, G * P], FR) for p in "hl"]
            x1, hn, sq = sb("x1", [P, G, D]), sb("hn2", [P, G, D]), sb("sq2", [P, D])
            gel = sb("gel", [P, 2, G * P])
            gT = [sb(f"gT{p}", [P, FM, G * P], FR) for p in "hl"]
            delta, sel = sb("delta", [P, G, D]), sb("sel", [P, G])
            Tps, acc, up = pb("Tps2", [P, 2, 512]), pb("acc2", [P, 2, 512]), pb("up2", [P, 2, 512])
            (t_done, t_hi, t_lo, wo_done, x1_ready, sq_done, v_ready, std_ready, hn_ready, up_done, gel_done, g_hi,
             g_lo, down_done, down_read, delta_ready, chain) = every = chip.sems(
                st, *[f"p3_{n}" for n in ("t_done", "t_hi", "t_lo", "wo_done", "x1_ready", "sq_done", "v_ready",
                                          "std_ready", "hn_ready", "up_done", "gel_done", "g_hi", "g_lo", "down_done",
                                          "down_read", "delta_ready", "chain")])
            (sent,) = chip.pool_sems("p3_sent")

            with nc.Block() as block:

                @block.tensor
                def _(pe):
                    def transposed(src, g, n):
                        if n >= 2:
                            pe.wait_ge(t_lo, KD * (n - 1))
                        for k in range(KD):
                            last = nc.tensor.transpose(Tps[:, n % 2, P * k:P * k + P], src[:, g, P * k:P * k + P],
                                                       chip.ident[:])
                        last.then_inc(t_done, 1)

                    for g in range(G):
                        transposed(o_all, g, g)
                    for g in range(G):
                        pe.wait_ge(t_lo, KD * (g + 1))
                        if g >= 2:
                            pe.wait_ge(x1_ready, g - 1)
                        for k in range(KD):
                            last = three_pass(nc, acc[:, g % 2, 0:D], [p[:, k, P * g:P * g + P] for p in oT],
                                              [p[:, k, :] for p in w["wo"]], k == 0, k == KD - 1)
                        last.then_inc(wo_done, 1)
                    for g in range(G):
                        pe.wait_ge(hn_ready, g + 1)
                        transposed(hn, g, G + g)
                    pe.wait_ge(t_lo, KD * 2 * G)
                    for m in range(FM):
                        if m >= 2:
                            pe.wait_ge(gel_done, m - 1)
                        for k in range(KD):
                            last = three_pass(nc, up[:, m % 2, :], [p[:, k, P * m:P * m + P] for p in w_ffn["w1"]],
                                              [p[:, k, :] for p in fT], k == 0, k == KD - 1)
                        last.then_inc(up_done, 1)
                    for g in range(G):
                        pe.wait_ge(x1_ready, G)
                        if g >= 2:
                            pe.wait_ge(down_read, g - 1)
                        for m in range(FM):
                            if g == 0:
                                pe.wait_ge(g_lo, m + 1)
                            last = three_pass(nc, acc[:, g % 2, 0:D], [p[:, m, P * g:P * g + P] for p in gT],
                                              [p[:, m, :] for p in w_ffn["w2"]], m == 0, m == FM - 1)
                        last.then_inc(down_done, 1)

                @block.scalar
                def _(act):
                    def transposed_hi(out, n, g, scale):
                        act.wait_ge(t_done, n + 1)
                        for k in range(KD):
                            nc.scalar.activation(out[:, k, P * g:P * g + P], Tps[:, n % 2, P * k:P * k + P], ACT.Copy,
                                                 scale=scale[:, k:k + 1] if scale is not None else 1.0
                                                 ).then_inc(t_hi, 1)

                    for g in range(G):
                        transposed_hi(oT[0], g, g, None)
                    for g in range(G):
                        act.wait_ge(x1_ready, g + 1)
                        if g:
                            act.wait_ge(sq_done, g)
                        nc.scalar.activation(sq[:], x1[:, g, :], ACT.Square, accum_out=ss[:, g:g + 1]
                                             ).then_inc(sq_done, 1)
                    act.wait_ge(v_ready, 1)
                    nc.scalar.activation(std[:], vv[:], ACT.Sqrt).then_inc(std_ready, 1)
                    for g in range(G):
                        transposed_hi(fT[0], G + g, g, ln2)
                    for m in range(FM):
                        act.wait_ge(up_done, m + 1)
                        if m >= 2:
                            act.wait_ge(g_lo, m - 1)
                        nc.scalar.activation(gel[:, m % 2, :], up[:, m % 2, :], ACT.Gelu_apprx_tanh
                                             ).then_inc(gel_done, 1)
                        act.wait_ge(gel_done, m + 1)
                        nc.scalar.activation(gT[0][:, m, :], gel[:, m % 2, :], ACT.Copy).then_inc(g_hi, 1)

                @block.vector
                def _(dve):
                    V = nc.vector
                    links = [0]

                    def link(ins):
                        links[0] += 1
                        ins.then_inc(chain, 1)
                        dve.wait_ge(chain, links[0])

                    def transposed_lo(out, n, g, scale):
                        cols = slice(P * g, P * g + P)
                        for k in range(KD):
                            dve.wait_ge(t_hi, KD * (n + 1))
                            V.scalar_tensor_tensor(out[1][:, k, cols], Tps[:, n % 2, P * k:P * k + P],
                                                   scale[:, k:k + 1] if scale is not None else 1.0,
                                                   out[0][:, k, cols].bitcast(FP32), ALU.mult, ALU.subtract
                                                   ).then_inc(t_lo, 1)

                    for g in range(G):
                        transposed_lo(oT, g, g, None)
                    for g in range(G):
                        dve.wait_ge(wo_done, g + 1)
                        V.tensor_tensor(x1[:, g, :], acc[:, g % 2, 0:D], xs[:, g, :], ALU.add).then_inc(x1_ready, 1)
                    dve.wait_ge(sq_done, G)
                    link(V.tensor_scalar(vv[:], ss[:], 1.0 / D, 1e-6, ALU.mult, ALU.add))
                    V.tensor_copy(tmp[:], vv[:]).then_inc(v_ready, 1)
                    dve.wait_ge(std_ready, 1)
                    newton_rsqrt(nc, link, rr[:], std[:], vv[:], tmp[:])
                    for g in range(G):
                        V.tensor_scalar(hn[:, g, :], x1[:, g, :], rr[:, g:g + 1], None, ALU.mult).then_inc(hn_ready, 1)
                    for b in range(B):
                        link(V.tensor_scalar(sel[:, 2 * b:2 * b + 2], picked[:, b, :, 1], thresholds[:, b:b + 1], -1.0,
                                             ALU.is_gt, ALU.mult))
                    for g in range(G):
                        link(V.tensor_scalar(delta[:, g, :], xs[:, g, :], sel[:, g:g + 1], None, ALU.mult))
                    for g in range(G):
                        transposed_lo(fT, G + g, g, ln2)
                    for m in range(FM):
                        dve.wait_ge(g_hi, m + 1)
                        V.tensor_tensor(gT[1][:, m, :], gel[:, m % 2, :], gT[0][:, m, :].bitcast(FP32), ALU.subtract
                                        ).then_inc(g_lo, 1)
                    for g in range(G):
                        dve.wait_ge(down_done, g + 1)
                        V.tensor_tensor(x1[:, g, :], acc[:, g % 2, 0:D], x1[:, g, :], ALU.add).then_inc(down_read, 1)
                        dve.wait_ge(down_read, g + 1)
                        V.scalar_tensor_tensor(delta[:, g, :], x1[:, g, :], picked[:, g // 2, g % 2, 1:2],
                                               delta[:, g, :], ALU.mult, ALU.add).then_inc(delta_ready, 1)

                @block.gpsimd
                def _(pool):
                    for g in range(G):
                        pool.wait_ge(delta_ready, g + 1)
                        n = P if g % 2 == 0 else P - 1
                        nc.gpsimd.indirect_dma_start(
                            out=out_dram[:, :],
                            out_offset=bass.IndirectOffsetOnAxis(ap=row_index[0:n, g // 2, g % 2, 0:1], axis=0),
                            in_=delta[0:n, g, :], in_offset=None, compute_op=ALU.add).then_inc(sent, 16)
                    pool.wait_ge(sent, 16 * G)

            for s in [sent, *every]:
                nc.sync.sem_clear(s)
        nc.all_engine_barrier()


def load_small(chip, stack, plan, scales={}):
    nc = chip.nc
    out = {name: stack.enter_context(nc.sbuf_tensor(f"c_{name}", shape, FP32)) for name, shape, _ in plan}
    with ExitStack() as st:
        loaded, scaled = chip.sems(st, "small_loaded", "small_scaled")
        with nc.Block() as block:

            @block.sync
            def _(sp):
                for name, _, view in plan:
                    sp.dma_start(out[name][:], view).then_inc(loaded, 16)
                sp.wait_ge(loaded, 16 * len(plan))

            @block.vector
            def _(dve):
                dve.wait_ge(loaded, 16 * len(plan))
                for name, scale in scales.items():
                    nc.vector.tensor_scalar(out[name][:], out[name][:], scale, None, ALU.mult).then_inc(scaled, 1)
                dve.wait_ge(scaled, len(scales))

        nc.sync.sem_clear(loaded), nc.sync.sem_clear(scaled)
    nc.all_engine_barrier()
    return out


def fill_start(chip, stack, sorted_dram, sorted_meta, trash):
    nc = chip.nc
    TILES, D = sorted_dram.shape[0] // P, chip.D
    zeros = stack.enter_context(nc.sbuf_tensor("zeros", [P, 1, D], FP32))
    nobody = stack.enter_context(nc.sbuf_tensor("nobody", [P, TILES, 2], FP32))
    (filled,) = chip.sems(stack, "rows_filled")
    first_trash = trash.shape[0] - P
    with ExitStack() as st:
        made, zeroed = chip.sems(st, "fill_made", "fill_zeroed")
        with nc.Block() as block:

            @block.gpsimd
            def _(pool):
                nc.gpsimd.memset(nobody[:], 0.0).then_inc(zeroed, 1)
                nc.gpsimd.memset(zeros[:], 0.0).then_inc(made, 1)
                pool.wait_ge(zeroed, 1)
                nc.gpsimd.iota(nobody[:, :, 0].bitcast(I32), pattern=[[1, TILES]], base=0,
                               channel_multiplier=TILES).then_inc(made, 1)

            @block.vector
            def _(dve):
                dve.wait_ge(made, 2)
                rows = nobody[:, :, 0].bitcast(I32)
                nc.vector.tensor_single_scalar(rows, rows, P - 1, ALU.bitwise_and).then_inc(made, 1)
                dve.wait_ge(made, 3)
                nc.vector.tensor_single_scalar(rows, rows, float(first_trash), ALU.add).then_inc(made, 1)

            @block.sync
            def _(sp):
                sp.wait_ge(made, 4)
                sp.dma_start(sorted_meta.rearrange("(p t) m -> p t m", p=P), nobody[:]).then_inc(filled, 16)
                sp.dma_start(trash[first_trash:first_trash + P, :], zeros[:, 0, :]).then_inc(filled, 16)

        nc.sync.sem_clear(made), nc.sync.sem_clear(zeroed)
    nc.all_engine_barrier()
    part = lambda b: (sorted_dram.rearrange("(p t) d -> p t d", p=P)[:, bass.ds(b * (TILES // chip.B), TILES // chip.B), :],
                      zeros[:].to_broadcast([P, TILES // chip.B, D]))
    return filled, 16 * (2 + chip.B), part


def build(nc, a, out, B, S):
    N, D = a["x"].shape
    chip = Chip(nc, B, S, D)
    E = a["gate_w"].shape[1]
    HEADS = 16
    M = a["mask"].shape[1]
    TILES = 2 * N // P + E
    NA = N // P
    SCALE = float(D) ** -0.5
    HEAD_SCALE = float(D // HEADS) ** -0.5
    dram = lambda n, s: nc.dram_tensor(n, s, FP32, kind="Internal").ap()
    xn1, xn2, y1 = (dram(n, (N, D)) for n in ("xn1", "xn2", "y1"))
    y2 = dram("y2", (N + P, D))
    sorted_rows, sorted_meta = dram("sorted_rows", (TILES * P, D)), dram("sorted_meta", (TILES * P, 2))
    router_out = dram("router_out", (N,))
    wide = lambda v: v.to_broadcast([P, v.shape[1]])

    def token_buffers(st, tag):
        T = [st.enter_context(nc.sbuf_tensor(f"{tag}T_{p}", [P, chip.KD, S], FR)) for p in ("hi", "lo")]
        V = [st.enter_context(nc.sbuf_tensor(f"{tag}V_{p}", [P, chip.NT, D], FR)) for p in ("hi", "lo")]
        return T, V

    with ExitStack() as top:
        constants(chip, top)
        small = load_small(chip, top, [
            ("bq", [P, chip.KD], a["bq"]), ("bk", [P, chip.KD], a["bk"]), ("bv", [P, D], wide(a["bv"])),
            ("gate_b", [P, E], wide(a["gate_b"])), ("router_b", [P, 1], wide(a["router_b"])),
            ("ln1", [P, chip.KD], a["ln1"]), ("ln2", [P, chip.KD], a["ln2"])], {"bq": SCALE})

        with ExitStack() as layer:
            sb = lambda n, s, d=FP32: layer.enter_context(nc.sbuf_tensor(n, s, d))
            fill = fill_start(chip, layer, sorted_rows, sorted_meta, y2)
            logits, meta, slots = sb("logits", [P, NA, E]), sb("meta", [P, NA, 2, 2]), sb("slots", [P, NA, 2], I32)
            tile_expert, tile_rows = sb("tile_expert", [1, TILES], I32), sb("tile_rows", [64, TILES])
            with ExitStack() as st:
                w = split_weights(chip, st, [(n, a["a0_" + n]) for n in ("wq", "wk", "wv")] + [("gw", a["gate_w"])],
                                  {"wq": SCALE}, "l0_")
                gate_w = w.pop("gw")
                T, V = token_buffers(st, "l0_")
                with nc.Fori(0, B) as b:
                    norm_stage(chip, b, "n0", a["x"], xn1, T, V, w, gate_w, logits)
                    attention_stage(chip, b, "a0", T, V, w, {"q": small["bq"], "k": small["bk"]}, [a["x"]],
                                    small["bv"], y1, background=[(*fill[2](b), fill[0])])
            gating_stage(chip, logits, small["gate_b"], meta, slots, tile_expert, tile_rows, E, TILES)
            W1_raw, W3 = routed_buffers(chip, layer, a["rw1"], a["rw3"])
            prefetch = [[(W1_raw[:, e, :, :].bitcast(FP32), a["rw1"][e].rearrange("(k p) h -> p k h", p=P)),
                         (W3[:, e, :, :], a["rw3"][e].rearrange("(k p) d -> p k d", p=P))] for e in range(E)]
            shared_stage(chip, xn1, y1, a["sw1"], a["sb1"], a["sw2"], a["sb2"], a["sw3"], a["sb3"], slots, meta,
                         sorted_rows, sorted_meta, fill, prefetch, y2[0:N, :])
            routed_stage(chip, sorted_rows, sorted_meta, W1_raw, a["rw2"], W3, a["rb1"], a["rb2"], a["rb3"],
                         tile_expert, tile_rows, y2)

        with ExitStack() as layer:
            sb = lambda n, s, d=FP32: layer.enter_context(nc.sbuf_tensor(n, s, d))
            scores, picked = sb("router_scores", [P, NA, 2]), sb("picked", [P, B, 2, 2])
            ranking = Ranking(chip, layer, scores, small["router_b"], router_out)
            row_index, picked_row = sb("row_index", [P, B, 2, 2], I32), sb("picked_row", [P, B, 2 * P])
            thresholds = sb("thresholds", [P, B])
            with ExitStack() as st:
                w = split_weights(chip, st, [(n, a["a1_" + n]) for n in ("wq", "wk", "wv", "wo")] +
                                  [("rw", a["router_w"])], {"wq": SCALE}, "l1_")
                router_w = w.pop("rw")
                T, V = token_buffers(st, "l1_")
                with nc.Fori(0, B) as b:
                    norm_stage(chip, b, "n1", y2[0:N, :], xn2, T, V, w, router_w, scores)
                    attention_stage(chip, b, "a1", T, V, w, None, [y2[0:N, :], xn2], None, out,
                                    ranking)
            rank_stage(chip, ranking, picked, row_index, picked_row, thresholds, M - 1)
            with ExitStack() as st:
                w = split_weights(chip, st, [(n, a["f1_" + n]) for n in ("wq", "wk", "wv", "wo", "w1", "w2")],
                                  {"wq": HEAD_SCALE}, "f1_")
                picked_stage(chip, xn2, a["positions"], a["mask"], row_index, picked_row, picked, thresholds,
                             a["inverse"], small["ln1"], small["ln2"], w, w, out, HEADS)




def kernel(**inputs):
    import numpy as np
    import concourse.bacc as bacc
    from concourse.bass_utils import run_bass_kernel_spmd

    i = {name: np.asarray(v) for name, v in inputs.items()}
    B, S, D = i["L0_attn_x"].shape
    E, _, H = i["L0_ffn_rw1"].shape
    M = i["L1_ffn_attention_mask"].shape[-1]
    HALF = D // 16 // 2
    columns = lambda v: v.reshape(-1, P).T
    lay = {
        "x": i["L0_attn_x"].reshape(B * S, D),
        **{"a0_" + n.lower(): i["L0_attn_" + n].T for n in ("Wq", "Wk", "Wv")},
        "bq": columns(i["L0_attn_bq"]), "bk": columns(i["L0_attn_bk"]), "bv": i["L0_attn_bv"][None],
        "gate_w": i["L0_ffn_gate_w"], "gate_b": i["L0_ffn_gate_b"][None],
        **{n: i["L0_ffn_" + n] for n in ("rw1", "rw2", "rw3", "rb1", "rb2", "rb3", "sw1", "sw2", "sw3", "sb3")},
        **{n: i["L0_ffn_" + n].reshape(2, H // P, P).transpose(2, 0, 1) for n in ("sb1", "sb2")},
        **{"a1_" + n.lower(): i["L1_attn_" + n].T for n in ("Wq", "Wk", "Wv", "Wo")},
        "router_w": np.concatenate([i["L1_ffn_router_w"], np.zeros((D, 1), np.float32)], axis=1),
        "router_b": i["L1_ffn_router_b"][None],
        **{"f1_" + n: i["L1_ffn_" + n] for n in ("wq", "wk", "wv", "wo", "w1", "w2")},
        "ln1": columns(i["L1_ffn_ln1"]), "ln2": columns(i["L1_ffn_ln2"]),
        "mask": i["L1_ffn_attention_mask"].reshape(-1, M), "positions": i["L1_ffn_position_ids"].reshape(-1, 1),
        "inverse": (1.0 / np.float32(10000.0) ** (np.arange(0, 2 * HALF, 2, dtype=np.float32) / (2 * HALF))
                    ).astype(np.float32)[None],
    }
    nc = bacc.Bacc("TRN2", target_bir_lowering=False, num_devices=1)
    arrays, args = {}, {}
    for name, v in lay.items():
        arrays[f"in_{name}"] = np.ascontiguousarray(v)
        args[name] = nc.dram_tensor(f"in_{name}", v.shape, mybir.dt.from_np(v.dtype), kind="ExternalInput").ap()
    out = nc.dram_tensor("out", (B * S, D), FP32, kind="ExternalOutput").ap()
    build(nc, args, out, B, S)
    r = run_bass_kernel_spmd(nc, [arrays], core_ids=[0])
    return r.results[0]["out"].reshape(B, S, D)
```

```python
import concourse.bass as bass
from concourse import mybir
from contextlib import ExitStack

P = 128
FP32 = mybir.dt.float32
FR = mybir.dt.float32r
I32 = mybir.dt.int32
ACT = mybir.ActivationFunctionType
ALU = mybir.AluOpType
AX = mybir.AxisListType
MASKED = -1e30


class Chip:

    def __init__(self, nc, B, S, D):
        self.nc, self.B, self.S, self.D = nc, B, S, D
        self.NT = S // P
        self.KD = D // P
        self.NG = self.NT // 4

    def sems(self, stack, *names):
        return [stack.enter_context(self.nc.semaphore(n)) for n in names]

    def pool_sems(self, *names):
        return [self.nc.alloc_semaphore(name=n) for n in names]


def three_pass(nc, out, lhs, rhs, start, stop):
    (lh, ll), (rh, rl) = lhs, rhs
    nc.tensor.matmul(out, ll, rh, start=start, stop=False)
    nc.tensor.matmul(out, lh, rl, start=False, stop=False)
    return nc.tensor.matmul(out, lh, rh, start=False, stop=stop)


def constants(chip, stack):
    nc = chip.nc
    ident = stack.enter_context(nc.sbuf_tensor("ident", [P, P], FP32))
    ident_r = stack.enter_context(nc.sbuf_tensor("ident_r", [P, P], FR))
    causal_r = stack.enter_context(nc.sbuf_tensor("causal_r", [P, P], FR))
    with ExitStack() as st:
        causal = st.enter_context(nc.sbuf_tensor("causal", [P, P], FP32))
        filled, selected, copied = chip.sems(st, "const_filled", "const_selected", "const_copied")
        with nc.Block() as block:

            @block.gpsimd
            def _(pool):
                nc.gpsimd.memset(ident[:], 0.0).then_inc(filled, 1)
                nc.gpsimd.memset(causal[:], 0.0).then_inc(filled, 1)
                pool.wait_ge(filled, 2)
                nc.gpsimd.affine_select(out=ident[:], in_=ident[:], compare_op=ALU.not_equal, fill=1.0,
                                        base=0, pattern=[[-1, P]], channel_multiplier=1).then_inc(selected, 1)
                nc.gpsimd.affine_select(out=causal[:], in_=causal[:], compare_op=ALU.is_ge, fill=MASKED,
                                        base=0, pattern=[[-1, P]], channel_multiplier=1).then_inc(selected, 1)

            @block.vector
            def _(dve):
                dve.wait_ge(selected, 2)
                nc.vector.tensor_copy(ident_r[:], ident[:]).then_inc(copied, 1)
                nc.vector.tensor_copy(causal_r[:], causal[:]).then_inc(copied, 1)
                dve.wait_ge(copied, 2)

        nc.sync.sem_clear(filled), nc.sync.sem_clear(selected), nc.sync.sem_clear(copied)
    chip.ident, chip.ident_r, chip.causal_r = ident, ident_r, causal_r
    nc.all_engine_barrier()


class Weights:

    def __init__(self, chip, stack, named, tag):
        nc = chip.nc
        self.named, self.names = named, [name for name, _ in named]
        shapes = {name: [P, w.shape[0] // P, w.shape[1]] for name, w in named}
        self.raw = {name: stack.enter_context(nc.sbuf_tensor(f"{tag}{name}_raw", shapes[name], FP32))
                    for name in self.names}
        self.loaded = dict(zip(self.names, chip.sems(stack, *[f"{tag}{name}_loaded" for name in self.names])))
        self.loads = [(self.raw[name][:], w.rearrange("(k p) n -> p k n", p=P), self.loaded[name]) for name, w in named]
        self.tag = tag


def weight_parts(chip, stack, named, tag):
    return {name: tuple(stack.enter_context(chip.nc.sbuf_tensor(f"{tag}{name}_{part}", [P, w.shape[0] // P, w.shape[1]],
                                                                FR)) for part in ("hi", "lo")) for name, w in named}


def split_weights(chip, stack, weights, scales={}, parts=None, start=False):
    nc = chip.nc
    names, raw = weights.names, weights.raw
    parts = parts or weight_parts(chip, stack, weights.named, weights.tag)
    with ExitStack() as st:
        hi_done, lo_done = chip.sems(st, weights.tag + "w_hi_done", weights.tag + "w_lo_done")
        with nc.Block() as block:

            @block.sync
            def _(sp):
                for into, src, sem in weights.loads if start else ():
                    sp.dma_start(into, src).then_inc(sem, 16)

            @block.scalar
            def _(act):
                for name in names:
                    act.wait_ge(weights.loaded[name], 16)
                    nc.scalar.activation(parts[name][0][:], raw[name][:], ACT.Copy, scale=scales.get(name, 1.0)
                                         ).then_inc(hi_done, 1)

            @block.vector
            def _(dve):
                flat = lambda a: a.rearrange("p k n -> p (k n)")
                for n, name in enumerate(names):
                    dve.wait_ge(hi_done, n + 1)
                    nc.vector.scalar_tensor_tensor(flat(parts[name][1][:]), flat(raw[name][:]), scales.get(name, 1.0),
                                                   flat(parts[name][0][:]).bitcast(FP32), ALU.mult,
                                                   ALU.subtract).then_inc(lo_done, 1)
                dve.wait_ge(lo_done, len(names))

        for s in [*weights.loaded.values(), hi_done, lo_done]:
            nc.sync.sem_clear(s)
    nc.all_engine_barrier()
    return parts


def norm_stage(chip, b, tag, src, xn_dram, T, V, w, scores):
    nc, NT, KD, NG, D = chip.nc, chip.NT, chip.KD, chip.NG, chip.D
    E = scores.shape[2]
    AHEAD = 2
    with ExitStack() as st:
        sb = lambda n, s, d=FP32: st.enter_context(nc.sbuf_tensor(f"{tag}_{n}", s, d))
        pb = lambda n, s: st.enter_context(nc.psum_tensor(f"{tag}_{n}", s, FP32))
        X, XN = sb("x", [P, NT, D]), sb("xn", [P, NT, D])
        stats, mv = sb("stats", [P, NT, 6]), sb("mv", [P, NT, 2])
        ve, std, rstd, tmp = (sb(n, [P, NT]) for n in ("ve", "std", "rstd", "tmp"))
        Tps, Vps = pb("Tps", [P, 2, 512]), pb("Vps", [P, 2, 2, 512])
        loaded = chip.sems(st, *[f"{tag}_x_loaded{g}" for g in range(NG)])
        (var_ready, std_ready, xn_ready, t_done, t_hi, t_lo, v_done, v_hi, v_lo, stored, chain) = every = chip.sems(
            st, *[f"{tag}_{n}" for n in ("var_ready", "std_ready", "xn_ready", "t_done", "t_hi", "t_lo", "v_done",
                                         "v_hi", "v_lo", "xn_stored", "dve_chain")])
        x_view = src.rearrange("(t p) d -> p t d", p=P)
        xn_view = xn_dram.rearrange("(t p) d -> p t d", p=P)

        with nc.Block() as block:

            @block.sync
            def _(sp):
                for g in range(NG):
                    sp.dma_start(X[:, 4 * g:4 * g + 4, :], x_view[:, bass.ds(b * NT + 4 * g, 4), :]
                                 ).then_inc(loaded[g], 16)
                for g in range(NG):
                    sp.wait_ge(xn_ready, 4 * (g + 1))
                    sp.dma_start(xn_view[:, bass.ds(b * NT + 4 * g, 4), :], XN[:, 4 * g:4 * g + 4, :]
                                 ).then_inc(stored, 16)
                sp.wait_ge(stored, 16 * NG)

            @block.vector
            def _(dve):
                links = [0]

                def link(ins):
                    links[0] += 1
                    ins.then_inc(chain, 1)
                    dve.wait_ge(chain, links[0])

                def values_lo(g):
                    for h in range(2):
                        n = 2 * g + h
                        pair = slice(2 * n, 2 * n + 2)
                        dve.wait_ge(v_hi, n + 1)
                        nc.vector.tensor_tensor(V[1][:, pair, :], Vps[:, n % 2, :, 0:D], V[0][:, pair, :].bitcast(FP32),
                                                ALU.subtract)
                        nc.vector.tensor_copy(scores[:, bass.ds(b * NT + 2 * n, 2), :], Vps[:, n % 2, :, D:D + E]
                                              ).then_inc(v_lo, 1)

                def normalise(g):
                    four = slice(4 * g, 4 * g + 4)
                    dve.wait_ge(loaded[g], 16)
                    for t in range(4 * g, 4 * g + 4):
                        ins = nc.vector.bn_stats(stats[:, t, :], X[:, t, :])
                    link(ins)
                    for t in range(4 * g, 4 * g + 4):
                        ins = nc.vector.bn_aggr(mv[:, t, :], stats[:, t, :])
                    link(ins)
                    nc.vector.tensor_scalar_add(ve[:, four], mv[:, four, 1], 1e-5).then_inc(var_ready, 1)
                    dve.wait_ge(std_ready, g + 1)
                    link(nc.vector.reciprocal(rstd[:, four], std[:, four]))
                    link(nc.vector.tensor_tensor(tmp[:, four], rstd[:, four], rstd[:, four], ALU.mult))
                    link(nc.vector.tensor_tensor(tmp[:, four], tmp[:, four], ve[:, four], ALU.mult))
                    link(nc.vector.tensor_scalar(tmp[:, four], tmp[:, four], -0.5, 1.5, ALU.mult, ALU.add))
                    link(nc.vector.tensor_tensor(rstd[:, four], rstd[:, four], tmp[:, four], ALU.mult))
                    for t in range(4 * g, 4 * g + 4):
                        nc.vector.tensor_scalar(XN[:, t, :], X[:, t, :], mv[:, t, 0:1], rstd[:, t:t + 1],
                                                ALU.subtract, ALU.mult).then_inc(xn_ready, 1)

                for g in range(AHEAD):
                    normalise(g)
                for g in range(NG):
                    if g + AHEAD < NG:
                        normalise(g + AHEAD)
                    for k in range(KD):
                        n = KD * g + k
                        dve.wait_ge(t_hi, n + 1)
                        tok = slice(512 * g, 512 * g + 512)
                        nc.vector.tensor_tensor(T[1][:, k, tok], Tps[:, n % 2, :], T[0][:, k, tok].bitcast(FP32),
                                                ALU.subtract).then_inc(t_lo, 1)
                    if g:
                        values_lo(g - 1)
                values_lo(NG - 1)

            @block.scalar
            def _(act):
                def values_hi(g):
                    for h in range(2):
                        n = 2 * g + h
                        act.wait_ge(v_done, n + 1)
                        nc.scalar.activation(V[0][:, 2 * n:2 * n + 2, :], Vps[:, n % 2, :, 0:D], ACT.Copy
                                             ).then_inc(v_hi, 1)

                def root(g):
                    four = slice(4 * g, 4 * g + 4)
                    act.wait_ge(var_ready, g + 1)
                    nc.scalar.activation(std[:, four], ve[:, four], ACT.Sqrt).then_inc(std_ready, 1)

                for g in range(AHEAD):
                    root(g)
                for g in range(NG):
                    if g + AHEAD < NG:
                        root(g + AHEAD)
                    for k in range(KD):
                        n = KD * g + k
                        act.wait_ge(t_done, n + 1)
                        nc.scalar.activation(T[0][:, k, 512 * g:512 * g + 512], Tps[:, n % 2, :],
                                             ACT.Copy).then_inc(t_hi, 1)
                    if g:
                        values_hi(g - 1)
                values_hi(NG - 1)

            @block.tensor
            def _(pe):
                def values(g):
                    pe.wait_ge(t_lo, KD * (g + 1))
                    for h in range(2):
                        n = 2 * g + h
                        if n >= 2:
                            pe.wait_ge(v_lo, n - 1)
                        for j in range(2):
                            t = 2 * n + j
                            x = [[part[:, k, P * t:P * t + P] for part in T] for k in range(KD)]
                            for k in range(KD):
                                last = three_pass(nc, Vps[:, n % 2, j, 0:D + E], x[k],
                                                  [part[:, k, :] for part in w["wv"]], k == 0, k == KD - 1)
                        last.then_inc(v_done, 1)

                for g in range(NG):
                    pe.wait_ge(xn_ready, 4 * (g + 1))
                    for k in range(KD):
                        n = KD * g + k
                        if n >= 2:
                            pe.wait_ge(t_lo, n - 1)
                        for j in range(4):
                            last = nc.tensor.transpose(Tps[:, n % 2, P * j:P * j + P],
                                                       XN[:, 4 * g + j, P * k:P * k + P], chip.ident[:])
                        last.then_inc(t_done, 1)
                    if g:
                        values(g - 1)
                values(NG - 1)

        for s in [*loaded, *every]:
            nc.sync.sem_clear(s)
    nc.all_engine_barrier()


class Ranking:

    def __init__(self, chip, stack, scores, router_b, order):
        sb = lambda n, s: stack.enter_context(chip.nc.sbuf_tensor(f"k_{n}", s, FP32))
        self.scores, self.router_b, self.order = scores, router_b, order
        self.weights, self.rank = sb("weights", [P, chip.B * chip.NT]), sb("rank", [P, chip.B * chip.NT])
        self.earlier = sb("earlier", [P, P])


def attention_stage(chip, b, tag, T, V, w, biases, bases, value_bias, dst, ranking=None, background=()):
    nc, NT, KD, NG, D = chip.nc, chip.NT, chip.KD, chip.NG, chip.D
    has_o = "wo" in w
    SLOTS = 4
    TBANKS = 3
    FRONTS = 3
    SBUFS = 3
    AHEAD = 2
    LAG = 2
    COUNT_FROM = 8

    steps, of_tile = [], []
    for i in range(NT):
        groups = [("p", i, k0, min(4, i + 1 - k0)) for k0 in range(0, i + 1, 4)]
        if has_o and i >= 2:
            groups.append(("o", i - 2, 0, KD))
        if has_o and i == NT - 1:
            groups += [("o", i - 1, 0, KD)]
        of_tile.append(range(len(steps), len(steps) + len(groups)))
        steps += groups
    body_steps = len(steps)
    if has_o:
        steps.append(("o", NT - 1, 0, KD))
    last_p = {i: max(n for n, s in enumerate(steps) if s[0] == "p" and s[1] == i) for i in range(NT)}
    o_step = {s[1]: n for n, s in enumerate(steps) if s[0] == "o"}
    chunks = lambda i: i // 4 + 1
    chunks_before = lambda i: sum(chunks(j) for j in range(i))
    acc_use = {}
    for kind, i, k0, _ in steps:
        if k0 == 0:
            acc_use[(kind, i)] = len(acc_use)

    project = lambda c: [(kind, c, m) for kind in "kq" for m in range(KD)]
    score = lambda i: [("s", i, j) for j in range(chunks(i))]
    first_units = project(0) + [u for i in range(AHEAD) for u in score(i)]
    front_at = {n: [] for n in range(len(steps))}
    for i in range(NT):
        units = score(i + AHEAD) if i + AHEAD < NT else []
        c = (i + AHEAD + 1) // 4
        if (i + AHEAD + 1) % 4 == 0 and c < NG:
            units = units + project(c)
        for q, u in enumerate(units):
            front_at[of_tile[i][q * len(of_tile[i]) // len(units)]].append(u)
    every_unit = first_units + [u for n in range(len(steps)) for u in front_at[n]]
    unit_no = {u: n for n, u in enumerate(every_unit)}
    proj_no = {u: n for n, u in enumerate(u for u in every_unit if u[0] != "s")}
    exp_at = {of_tile[i - 1][0]: i for i in range(1, NT)}

    with ExitStack() as st:
        sb = lambda n, s, d=FP32: st.enter_context(nc.sbuf_tensor(f"{tag}_{n}", s, d))
        pb = lambda n, s: st.enter_context(nc.psum_tensor(f"{tag}_{n}", s, FP32))
        kT = [sb(f"kT{p}", [P, KD, chip.S], FR) for p in "hl"]
        qT = [sb(f"qT{p}", [P, 2, KD, 512], FR) for p in "hl"]
        probs = sb("probs", [P, SBUFS, chip.S])
        pT = [sb(f"pT{p}", [P, SLOTS, 512], FR) for p in "hl"]
        base = sb("base", [P, 2, 4, D])
        base2 = sb("base2", [P, 2, 4, D]) if len(bases) > 1 else None
        if has_o:
            heads = sb("o_norm", [P, 2, D])
        part_min, neg_max = sb("part_min", [P, NT, 4]), sb("neg_max", [P, NT])
        sums, rsum = sb("sums", [P, NT]), sb("rsum", [P, NT])
        front, Tps, acc = pb("front", [P, FRONTS, 512]), pb("Tps", [P, TBANKS, 512]), pb("acc", [P, 2, 512])
        base_loaded = chip.sems(st, f"{tag}_base_loaded0", f"{tag}_base_loaded1")
        (proj_done, proj_hi, front_free, acc_free, s_done, max_done, exp_done, t_done, t_hi, t_lo, pv_done, rs_ready,
         base_ready, y_stored) = every = chip.sems(
            st, *[f"{tag}_{n}" for n in (
                "proj_done", "proj_hi", "front_free", "acc_free", "scores_done", "max_done", "exp_done", "t_done",
                "t_hi", "t_lo", "pv_done", "rsum_ready", "base_ready", "y_stored")])
        if ranking:
            mine, row, counts = sb("rank_mine", [P, NT]), sb("rank_row", [P, chip.S]), sb("rank_counts", [P, NT, 5])
            marks = sb("rank_marks", [P, NT // 2, P], mybir.dt.bfloat16)
            rank_sems = chip.sems(st, *[f"{tag}_rank_{n}" for n in ("mine_ready", "stored", "row_loaded", "chain",
                                                                    "counted")])
            RANK_LINKS = 6
            mine_ready, rank_stored, row_loaded, rank_chain, counted = rank_sems
        stored_as = "o" if has_o else "p"
        view = lambda a: a.rearrange("(t p) d -> p t d", p=P)
        bank_of = lambda u: front[:, unit_no[u] % FRONTS, :]

        def projected(u, part):
            kind, c, m = u
            return qT[part][:, c % 2, m, :] if kind == "q" else kT[part][:, m, 512 * c:512 * c + 512]

        with nc.Block() as block:

            @block.sync
            def _(sp):
                for c in range(NG):
                    if c >= 2:
                        sp.wait_ge(y_stored, 16 * (c - 1))
                    tiles = bass.ds(b * NT + 4 * c, 4)
                    sp.dma_start(base[:, c % 2, :, :], view(bases[0])[:, tiles, :]).then_inc(base_loaded[c % 2], 16)
                    if base2 is not None:
                        sp.dma_start(base2[:, c % 2, :, :], view(bases[1])[:, tiles, :]
                                     ).then_inc(base_loaded[c % 2], 16)
                    if c == 0:
                        for into, src, sem in background:
                            sp.dma_start(into, src).then_inc(sem, 16)
                    if ranking and c == 1:
                        sp.wait_ge(mine_ready, 1)
                        sp.dma_start(ranking.order.rearrange("(b p t) -> p b t", p=P, t=NT)[:, bass.ds(b, 1), :],
                                     mine[:].rearrange("p (o t) -> p o t", o=1)).then_inc(rank_stored, 16)
                        sp.wait_ge(rank_stored, 16)
                        everyone = ranking.order.rearrange("(o n) -> o n", o=1)[:, bass.ds(b * chip.S, chip.S)]
                        sp.dma_start(row[:], everyone.to_broadcast([P, chip.S])).then_inc(row_loaded, 16)
                    if c:
                        sp.wait_ge(acc_free, acc_use[(stored_as, 4 * c - 1)] + 1)
                        sp.dma_start(view(dst)[:, bass.ds(b * NT + 4 * (c - 1), 4), :], base[:, (c - 1) % 2, :, :]
                                     ).then_inc(y_stored, 16)
                sp.wait_ge(acc_free, acc_use[(stored_as, NT - 1)] + 1)
                sp.dma_start(view(dst)[:, bass.ds(b * NT + 4 * (NG - 1), 4), :], base[:, (NG - 1) % 2, :, :]
                             ).then_inc(y_stored, 16)
                sp.wait_ge(y_stored, 16 * NG)

            @block.gpsimd
            def _(pool):
                g = nc.gpsimd
                links = [0]

                def link(ins):
                    links[0] += 1
                    ins.then_inc(rank_chain, 1)
                    pool.wait_ge(rank_chain, links[0])

                def add_bases(c):
                    pool.wait_ge(base_loaded[c % 2], 16 * len(bases) * (c // 2 + 1))
                    slot = base[:, c % 2, :, :]
                    if base2 is not None:
                        other = base2[:, c % 2, :, :]
                    else:
                        other = value_bias[:].rearrange("p (a d) -> p a d", a=1).to_broadcast([P, 4, D])
                    g.tensor_tensor(slot, slot, other, ALU.add).then_inc(base_ready, 1)

                def own_weights():
                    link(g.memset(ranking.earlier[:], 0.0))
                    link(g.affine_select(out=ranking.earlier[:], in_=ranking.earlier[:], compare_op=ALU.is_ge, fill=1.0,
                                         base=0, pattern=[[1, P]], channel_multiplier=-1))
                    link(g.tensor_copy(mine[:], ranking.scores[:, bass.ds(b * NT, NT), 0]))
                    link(g.tensor_scalar(mine[:], mine[:], ranking.router_b[:], None, ALU.add))
                    link(g.tensor_copy(ranking.weights[:, bass.ds(b * NT, NT)], mine[:]))
                    pool.sem_inc(mine_ready, 1)

                if ranking:
                    link(g.memset(counts[:], 0.0))
                    own_weights()
                for c in range(NG):
                    add_bases(c)

            @block.scalar
            def _(act):
                def project_hi(u):
                    kind, c, m = u
                    act.wait_ge(proj_done, proj_no[u] + 1)
                    if kind == "q" and c >= 2 and m == 0:
                        act.wait_ge(s_done, chunks_before(4 * (c - 1)))
                    if biases:
                        ins = nc.scalar.activation(projected(u, 0), bank_of(u), ACT.Identity,
                                                   bias=biases[kind][:, m:m + 1])
                    else:
                        ins = nc.scalar.activation(projected(u, 0), bank_of(u), ACT.Copy)
                    ins.then_inc(proj_hi, 1)

                def exponentials(i):
                    act.wait_ge(max_done, i + 1)
                    both = probs[:, i % SBUFS, 0:P * (i + 1)]
                    nc.scalar.activation(both, both, ACT.Exp, scale=-1.0, bias=neg_max[:, i:i + 1],
                                         accum_out=sums[:, i:i + 1]).then_inc(exp_done, 1)

                def transposed_hi(n):
                    act.wait_ge(t_done, n + 1)
                    if n >= SLOTS:
                        act.wait_ge(pv_done, n - SLOTS + 1)
                    width = P * steps[n][3]
                    nc.scalar.activation(pT[0][:, n % SLOTS, 0:width], Tps[:, n % TBANKS, 0:width],
                                         ACT.Copy).then_inc(t_hi, 1)

                for u in project(0):
                    project_hi(u)
                exponentials(0)
                for n in range(len(steps)):
                    transposed_hi(n)
                    if n in exp_at:
                        exponentials(exp_at[n])
                    for u in front_at[n]:
                        if u[0] != "s":
                            project_hi(u)

            @block.vector
            def _(dve):
                def front_read(u):
                    if u[0] != "s":
                        dve.wait_ge(proj_hi, proj_no[u] + 1)
                        hi = projected(u, 0).bitcast(FP32)
                        if biases:
                            ins = nc.vector.scalar_tensor_tensor(projected(u, 1), bank_of(u),
                                                                 biases[u[0]][:, u[2]:u[2] + 1], hi, ALU.add,
                                                                 ALU.subtract)
                        else:
                            ins = nc.vector.tensor_tensor(projected(u, 1), bank_of(u), hi, ALU.subtract)
                        ins.then_inc(front_free, 1)
                        return
                    _, i, j = u
                    dve.wait_ge(s_done, chunks_before(i) + j + 1)
                    if i >= SBUFS and j == 0:
                        dve.wait_ge(t_done, last_p[i - SBUFS] + 1)
                    width = min(512, P * (i + 1) - 512 * j)
                    one = chunks(i) == 1
                    nc.vector.tensor_scalar(probs[:, i % SBUFS, 512 * j:512 * j + width], bank_of(u)[:, 0:width],
                                            -1.0, None, ALU.mult, ALU.min,
                                            accum_out=neg_max[:, i:i + 1] if one else part_min[:, i, j:j + 1]
                                            ).then_inc(front_free, 1)
                    if j == chunks(i) - 1:
                        dve.wait_ge(front_free, unit_no[u] + 1)
                        if one:
                            dve.sem_inc(max_done, 1)
                        else:
                            nc.vector.tensor_reduce(neg_max[:, i:i + 1], part_min[:, i, 0:chunks(i)], AX.X, ALU.min
                                                    ).then_inc(max_done, 1)

                def transposed_lo(n):
                    dve.wait_ge(t_hi, n + 1)
                    width = P * steps[n][3]
                    nc.vector.tensor_tensor(pT[1][:, n % SLOTS, 0:width], Tps[:, n % TBANKS, 0:width],
                                            pT[0][:, n % SLOTS, 0:width].bitcast(FP32),
                                            ALU.subtract).then_inc(t_lo, 1)

                def finish(n):
                    kind, i = steps[n][:2]
                    if kind == "p" and n != last_p[i]:
                        return
                    bank = acc[:, acc_use[(kind, i)] % 2, 0:D]
                    slot = base[:, (i // 4) % 2, i % 4, :]
                    if kind == "p":
                        dve.wait_ge(exp_done, i + 1)
                        nc.vector.reciprocal(rsum[:, i:i + 1], sums[:, i:i + 1]).then_inc(rs_ready, 1)
                        dve.wait_ge(rs_ready, i + 1)
                    dve.wait_ge(pv_done, n + 1)
                    if kind == "p" and has_o:
                        if i >= 2:
                            dve.wait_ge(t_done, o_step[i - 2] + 1)
                        nc.vector.tensor_scalar(heads[:, i % 2, :], bank, rsum[:, i:i + 1], None,
                                                ALU.mult).then_inc(acc_free, 1)
                        return
                    dve.wait_ge(base_ready, i // 4 + 1)
                    if kind == "p":
                        ins = nc.vector.scalar_tensor_tensor(slot, bank, rsum[:, i:i + 1], slot, ALU.mult, ALU.add)
                    else:
                        ins = nc.vector.tensor_tensor(slot, bank, slot, ALU.add)
                    ins.then_inc(acc_free, 1)

                def count(i, half):
                    links = 2 * i + half
                    if i == 0 and half == 0:
                        dve.wait_ge(mine_ready, 1)
                        dve.wait_ge(row_loaded, 16)
                    else:
                        dve.wait_ge(counted, links)
                    by_token = row[:].rearrange("q (p t) -> q t p", t=NT)
                    own = mine[:, i:i + 1]
                    lo, hi = NT // 2 * half, NT // 2 * (half + 1)
                    split = min(max(i, lo), hi)
                    if split > lo:
                        ins = nc.vector.tensor_scalar(marks[:, 0:split - lo, :], by_token[:, lo:split, :], own, None,
                                                      ALU.is_ge, ALU.add, accum_out=counts[:, i, half:half + 1])
                    if split < hi:
                        ins = nc.vector.tensor_scalar(marks[:, split - lo:hi - lo, :], by_token[:, split:hi, :], own,
                                                      None, ALU.is_gt, ALU.add,
                                                      accum_out=counts[:, i, 2 + half:3 + half])
                    ins.then_inc(counted, 1)
                    if half == 1:
                        dve.wait_ge(counted, links + 1)
                        nc.vector.scalar_tensor_tensor(marks[:, 0, :], by_token[:, i, :], own, ranking.earlier[:],
                                                       ALU.is_equal, ALU.mult, accum_out=counts[:, i, 4:5]
                                                       ).then_inc(rank_chain, 1)
                        dve.wait_ge(rank_chain, RANK_LINKS + i + 1)

                for u in first_units:
                    front_read(u)
                for n in range(len(steps)):
                    if n > LAG:
                        finish(n - LAG - 1)
                    transposed_lo(n)
                    for u in front_at[n]:
                        front_read(u)
                    if ranking:
                        left = len(steps) - COUNT_FROM
                        for q in range(2 * NT):
                            if n == COUNT_FROM + q * left // (2 * NT):
                                count(q // 2, q % 2)
                for n in range(len(steps) - LAG - 1, len(steps)):
                    finish(n)
                if ranking:
                    nc.vector.tensor_reduce(ranking.rank[:, bass.ds(b * NT, NT)], counts[:], AX.X, ALU.add
                                            ).then_inc(counted, 1)

            @block.tensor
            def _(pe):
                def front_unit(u):
                    kind, c, m = u
                    if unit_no[u] >= FRONTS:
                        pe.wait_ge(front_free, unit_no[u] - FRONTS + 1)
                    if kind != "s":
                        for k in range(KD):
                            last = three_pass(nc, bank_of(u), [p[:, k, P * m:P * m + P] for p in w["w" + kind]],
                                              [p[:, k, 512 * c:512 * c + 512] for p in T], k == 0, k == KD - 1)
                        last.then_inc(proj_done, 1)
                        return
                    _, i, j = u
                    if i % 4 == 0 and j == 0:
                        pe.wait_ge(front_free, unit_no[("q", i // 4, KD - 1)] + 1)
                    rows = slice(P * (i % 4), P * (i % 4) + P)
                    cols = slice(512 * j, min(512 * j + 512, P * (i + 1)))
                    width = cols.stop - cols.start
                    diagonal = j == chunks(i) - 1
                    for k in range(KD):
                        last = three_pass(nc, bank_of(u)[:, 0:width], [p[:, (i // 4) % 2, k, rows] for p in qT],
                                          [p[:, k, cols] for p in kT], k == 0, k == KD - 1 and not diagonal)
                    if diagonal:
                        last = nc.tensor.matmul(bank_of(u)[:, width - P:width], chip.ident_r[:], chip.causal_r[:],
                                                start=False, stop=True)
                    last.then_inc(s_done, 1)

                def transposes(n):
                    kind, i, k0, count = steps[n]
                    if n >= TBANKS:
                        pe.wait_ge(t_lo, n - TBANKS + 1)
                    if kind == "p":
                        pe.wait_ge(exp_done, i + 1)
                        src = probs[:, i % SBUFS, :]
                    else:
                        pe.wait_ge(acc_free, acc_use[("p", i)] + 1)
                        src = heads[:, i % 2, :]
                    for j in range(count):
                        last = nc.tensor.transpose(Tps[:, n % TBANKS, P * j:P * j + P],
                                                   src[:, P * (k0 + j):P * (k0 + j) + P], chip.ident[:])
                    last.then_inc(t_done, 1)

                def products(n):
                    kind, i, k0, count = steps[n]
                    pe.wait_ge(t_lo, n + 1)
                    u = acc_use[(kind, i)]
                    if k0 == 0 and u >= 2:
                        pe.wait_ge(acc_free, u - 1)
                    ends = kind == "o" or n == last_p[i]
                    for j in range(count):
                        rhs = [p[:, k0 + j, :] for p in (V if kind == "p" else w["wo"])]
                        last = three_pass(nc, acc[:, u % 2, 0:D], [p[:, n % SLOTS, P * j:P * j + P] for p in pT],
                                          rhs, k0 + j == 0, ends and j == count - 1)
                    last.then_inc(pv_done, 1)

                for u in first_units:
                    front_unit(u)
                for n in range(body_steps):
                    transposes(n)
                    if n >= LAG:
                        products(n - LAG)
                    for u in front_at[n]:
                        front_unit(u)
                if has_o:
                    products(body_steps - 2)
                    products(body_steps - 1)
                    transposes(body_steps)
                    products(body_steps)
                else:
                    products(body_steps - 2)
                    products(body_steps - 1)

        for s in [*base_loaded, *(rank_sems if ranking else ()), *every]:
            nc.sync.sem_clear(s)
    nc.all_engine_barrier()


def gating_stage(chip, logits, gate_b, meta, slots, tile_expert, tile_rows, E, TILES):
    nc = chip.nc
    NA = logits.shape[1]
    with ExitStack() as st:
        sb = lambda n, s, d=FP32: st.enter_context(nc.sbuf_tensor(f"g_{n}", s, d))
        ones, before, rev = sb("ones", [P, P]), sb("before", [P, P]), sb("rev", [P, E])
        tile_no, row_no = sb("tile_no", [P, TILES]), sb("row_no", [64, 1])
        L, L2, ex, eq = (sb(n, [P, NA, E]) for n in ("L", "L2", "ex", "eq"))
        oh = [sb(f"oh{k}", [P, NA, E]) for k in range(2)]
        m = [sb(f"m{k}", [P, NA]) for k in range(2)]
        mx, total = sb("mx", [P, NA]), sb("total", [P, NA])
        picked, where = sb("picked", [P, NA, E]), sb("where", [P, NA, E])
        gsum = sb("gsum", [P, NA])
        token_no = sb("token_no", [P, NA], I32)
        counts, running = sb("counts", [P, NA, E]), sb("running", [P, NA, E])
        tiles_i, tiles_f, end_tile, start_row = (sb("tiles_i", [P, E], I32), sb("tiles_f", [P, E]),
                                                 sb("end_tile", [P, E]), sb("start_row", [P, E]))
        expert_f = sb("expert_f", [P, TILES])
        slot_f = sb("slot_f", [P, NA])
        onesE = sb("onesE", [P, max(NA, E)])
        within = st.enter_context(nc.psum_tensor("g_within", [P, NA, E], FP32))
        in_tile = st.enter_context(nc.psum_tensor("g_in_tile", [P, NA, E], FP32))
        chain, made, exp_ready, picked_ready, counted = every = chip.sems(
            st, "g_chain", "g_made", "g_exp_ready", "g_picked_ready", "g_counted")
        wide = lambda a: a.rearrange("p (t o) -> p t o", o=1).to_broadcast([P, NA, E])
        tall = lambda a: a.rearrange("p (o e) -> p o e", o=1).to_broadcast([P, NA, E])

        with nc.Block() as block:

            @block.gpsimd
            def _(pool):
                nc.gpsimd.memset(ones[:], 1.0).then_inc(made, 1)
                nc.gpsimd.memset(before[:], 1.0).then_inc(made, 1)
                nc.gpsimd.memset(onesE[:], 1.0).then_inc(made, 1)
                nc.gpsimd.iota(rev[:], pattern=[[-1, E]], base=E, channel_multiplier=0,
                               allow_small_or_imprecise_dtypes=True).then_inc(made, 1)
                nc.gpsimd.iota(tile_no[:], pattern=[[1, TILES]], base=0, channel_multiplier=0,
                               allow_small_or_imprecise_dtypes=True).then_inc(made, 1)
                nc.gpsimd.iota(row_no[:], pattern=[[0, 1]], base=0, channel_multiplier=1,
                               allow_small_or_imprecise_dtypes=True).then_inc(made, 1)
                nc.gpsimd.iota(token_no[:], pattern=[[P, NA]], base=0, channel_multiplier=1).then_inc(made, 1)
                pool.wait_ge(made, 7)
                nc.gpsimd.affine_select(out=before[:], in_=before[:], compare_op=ALU.is_gt, fill=0.0, base=0,
                                        pattern=[[1, P]], channel_multiplier=-1).then_inc(made, 1)

            @block.vector
            def _(dve):
                links = [0]

                def link(ins):
                    links[0] += 1
                    ins.then_inc(chain, 1)
                    dve.wait_ge(chain, links[0])

                tt, V = nc.vector.tensor_tensor, nc.vector
                dve.wait_ge(made, 8)
                link(tt(L[:], logits[:], tall(gate_b[:]), ALU.add))
                link(V.tensor_reduce(m[0][:], L[:], AX.X, ALU.max))
                tt(ex[:], L[:], wide(m[0][:]), ALU.subtract).then_inc(exp_ready, 1)
                src = L
                for k in range(2):
                    link(tt(eq[:], src[:], wide(m[k][:]), ALU.is_equal))
                    link(tt(eq[:], eq[:], tall(rev[:]), ALU.mult))
                    link(V.tensor_reduce(mx[:], eq[:], AX.X, ALU.max))
                    link(tt(oh[k][:], eq[:], wide(mx[:]), ALU.is_equal))
                    if k == 0:
                        flat = lambda a: a.rearrange("p t e -> p (t e)")
                        link(V.scalar_tensor_tensor(flat(L2[:]), flat(oh[0][:]), MASKED, flat(L[:]), ALU.mult, ALU.add))
                        link(V.tensor_reduce(m[1][:], L2[:], AX.X, ALU.max))
                        src = L2
                tt(picked[:], oh[0][:], oh[1][:], ALU.add).then_inc(picked_ready, 1)
                dve.wait_ge(exp_ready, 2)
                link(V.tensor_reduce(total[:], ex[:], AX.X, ALU.add))
                link(V.reciprocal(total[:], total[:]))
                for k in range(2):
                    link(tt(eq[:], ex[:], oh[k][:], ALU.mult))
                    link(V.tensor_reduce(gsum[:], eq[:], AX.X, ALU.add))
                    link(V.tensor_copy(meta[:, :, k, 0].bitcast(I32), token_no[:]))
                    link(tt(meta[:, :, k, 1], gsum[:], total[:], ALU.mult))
                dve.wait_ge(counted, 1)
                link(V.tensor_copy(counts[:], in_tile[:]))
                for e in range(E):
                    ins = V.tensor_tensor_scan(running[:, :, e], onesE[:, 0:NA], counts[:, :, e], 0.0,
                                               ALU.mult, ALU.add)
                link(ins)
                link(V.tensor_scalar_add(tiles_i[:], running[:, NA - 1, :], float(P - 1)))
                link(V.tensor_single_scalar(tiles_i[:], tiles_i[:], 7, ALU.logical_shift_right))
                link(V.tensor_copy(tiles_f[:], tiles_i[:]))
                link(V.tensor_tensor_scan(end_tile[:], onesE[:, 0:E], tiles_f[:], 0.0, ALU.mult, ALU.add))
                link(tt(start_row[:], end_tile[:], tiles_f[:], ALU.subtract))
                link(V.tensor_single_scalar(start_row[:], start_row[:], float(P), ALU.mult))
                link(tt(running[:], running[:], counts[:], ALU.subtract))
                link(tt(where[:], running[:], within[:], ALU.add))
                link(tt(where[:], where[:], tall(start_row[:]), ALU.add))
                for k in range(2):
                    link(tt(eq[:], where[:], oh[k][:], ALU.mult))
                    link(V.tensor_reduce(slot_f[:], eq[:], AX.X, ALU.add))
                    link(V.tensor_copy(slots[:, :, k], slot_f[:]))
                link(V.tensor_scalar(expert_f[:], tile_no[:], end_tile[:, 0:1], None, ALU.is_ge))
                for e in range(1, E - 1):
                    link(V.scalar_tensor_tensor(expert_f[:], tile_no[:], end_tile[:, e:e + 1], expert_f[:],
                                                ALU.is_ge, ALU.add))
                V.tensor_scalar(tile_rows[0:32, :], expert_f[0:32, :], row_no[0:32, :], None, ALU.is_equal)
                V.tensor_scalar(tile_rows[32:64, :], expert_f[32:64, :], 32.0, row_no[32:64, :], ALU.add, ALU.is_equal)
                link(V.tensor_copy(tile_expert[:], expert_f[0:1, :]))

            @block.scalar
            def _(act):
                act.wait_ge(exp_ready, 1)
                nc.scalar.activation(ex[:], ex[:], ACT.Exp).then_inc(exp_ready, 1)

            @block.tensor
            def _(pe):
                pe.wait_ge(picked_ready, 1)
                nc.tensor.matmul(within[:], before[:], picked[:], start=True, stop=True)
                nc.tensor.matmul(in_tile[:], ones[:], picked[:], start=True, stop=True).then_inc(counted, 1)

        for s in every:
            nc.sync.sem_clear(s)
    nc.all_engine_barrier()


def shared_stage(chip, xn_dram, base_dram, w1, b1, w2, b2, w3, b3, slots, meta, sorted_dram, sorted_meta, fill,
                 prefetch, dst):
    nc, D, KD = chip.nc, chip.D, chip.KD
    n_sh, _, H = w1.shape
    HM = H // P
    RAWS = 3
    U = n_sh * HM
    NC = xn_dram.shape[0] // 512
    view = lambda a: a.rearrange("(t p) d -> p t d", p=P)
    with ExitStack() as st:
        sb = lambda n, s, d=FP32: st.enter_context(nc.sbuf_tensor(f"s_{n}", s, d))
        pb = lambda n, s: st.enter_context(nc.psum_tensor(f"s_{n}", s, FP32))
        W1 = [sb(f"w1{p}", [P, n_sh, KD, H], FR) for p in "hl"]
        W2 = [sb(f"w2{p}", [P, n_sh, KD, H], FR) for p in "hl"]
        W3 = [sb(f"w3{p}", [P, n_sh, HM, D], FR) for p in "hl"]
        raw = sb("raw", [P, RAWS, KD * H])
        B1, B2, B3 = sb("b1", [P, n_sh, HM]), sb("b2", [P, n_sh, HM]), sb("b3", [P, n_sh, D])
        rows, base = sb("rows", [P, 2, 4, D]), sb("base", [P, 2, 4, D])
        T = [sb(f"T{p}", [P, 2, KD, 512], FR) for p in "hl"]
        gate, hidden = sb("gate", [P, 2, 512]), sb("hidden", [P, 2, 512])
        hT = [sb(f"hT{p}", [P, U, 512], FR) for p in "hl"]
        Tps, up, acc = pb("Tps", [P, 2, 512]), pb("up", [P, 2, 2, 512]), pb("acc", [P, 2, 512])
        raw_loaded = chip.sems(st, *[f"s_raw_loaded{r}" for r in range(RAWS)])
        rows_loaded = chip.sems(st, "s_rows_loaded0", "s_rows_loaded1")
        base_loaded = chip.sems(st, "s_base_loaded0", "s_base_loaded1")
        stored = chip.sems(st, "s_stored0", "s_stored1")
        sent = chip.pool_sems("s_sent0", "s_sent1")
        (prefetched,) = chip.sems(st, "s_prefetched")
        filled, fill_count, _ = fill
        SENDS = 4 * 2 * 2
        (biases, w_hi, w_lo, b3_ready, t_done, t_hi, t_lo, up_done, gate_done, hid_done, hid_hi, hid_lo, acc_done,
         acc_free, base_ready) = every = chip.sems(
            st, *[f"s_{n}" for n in ("biases", "w_hi", "w_lo", "b3_ready", "t_done", "t_hi", "t_lo", "up_done",
                                     "gate_done", "hid_done", "hid_hi", "hid_lo", "acc_done", "acc_free",
                                     "base_ready")])
        loads = []
        for n in range(n_sh):
            for W, w in ((W1, w1), (W2, w2), (W3, w3)):
                loads.append((W, n, w[n].rearrange("(k p) h -> p k h", p=P)))
        parts_of = lambda W, n: [p[:, n, :, :].rearrange("p k h -> p (k h)") for p in W]

        with nc.Block() as block:

            @block.sync
            def _(sp):
                for c in range(2):
                    sp.dma_start(rows[:, c, :, :], view(xn_dram)[:, 4 * c:4 * c + 4, :]).then_inc(rows_loaded[c], 16)
                for q, (W, n, src) in enumerate(loads):
                    if q >= RAWS:
                        sp.wait_ge(w_lo, q - RAWS + 1)
                    sp.dma_start(raw[:, q % RAWS, :].rearrange("p (k h) -> p k h", k=src.shape[1]), src
                                 ).then_inc(raw_loaded[q % RAWS], 16)
                    if q == 0:
                        sp.dma_start(B1[:], b1).then_inc(biases, 16)
                        sp.dma_start(B2[:], b2).then_inc(biases, 16)
                        sp.dma_start(B3[:], b3.rearrange("(o n) d -> o n d", o=1).to_broadcast([P, n_sh, D])
                                     ).then_inc(biases, 16)
                for c in range(NC):
                    r = c % 2
                    if c >= 2:
                        sp.wait_ge(t_done, KD * (c - 1))
                        sp.wait_ge(sent[r], 16 * SENDS * (c // 2))
                        sp.dma_start(rows[:, r, :, :], view(xn_dram)[:, 4 * c:4 * c + 4, :]
                                     ).then_inc(rows_loaded[r], 16)
                        sp.wait_ge(stored[r], 16 * (c // 2))
                    sp.dma_start(base[:, r, :, :], view(base_dram)[:, 4 * c:4 * c + 4, :]).then_inc(base_loaded[r], 16)
                    for tile, src in prefetch[c]:
                        sp.dma_start(tile, src).then_inc(prefetched, 16)
                sp.wait_ge(prefetched, 16 * sum(len(part) for part in prefetch))

            @block.gpsimd
            def _(pool):
                pool.wait_ge(biases, 48)
                for n in range(1, n_sh):
                    nc.gpsimd.tensor_tensor(B3[:, 0, :], B3[:, 0, :], B3[:, n, :], ALU.add).then_inc(b3_ready, 1)
                    pool.wait_ge(b3_ready, n)
                nc.gpsimd.tensor_scalar(B3[:, 0, :], B3[:, 0, :], 1.0 / n_sh, 0.0, ALU.mult, ALU.add).then_inc(b3_ready, 1)
                pool.wait_ge(b3_ready, n_sh)
                for c in range(NC):
                    pool.wait_ge(base_loaded[c % 2], 16 * (c // 2 + 1))
                    slot = base[:, c % 2, :, :]
                    nc.gpsimd.tensor_tensor(slot, slot, B3[:, 0:1, :].to_broadcast([P, 4, D]), ALU.add
                                            ).then_inc(base_ready, 1)
                    if c == 0:
                        pool.wait_ge(filled, fill_count)
                    pool.wait_ge(rows_loaded[c % 2], 16 * (c // 2 + 1))
                    for j in range(4):
                        for k in range(2):
                            t = 4 * c + j
                            place = bass.IndirectOffsetOnAxis(ap=slots[:, t, k:k + 1], axis=0)
                            nc.gpsimd.indirect_dma_start(out=sorted_dram[:, :], out_offset=place,
                                                         in_=rows[:, c % 2, j, :], in_offset=None
                                                         ).then_inc(sent[c % 2], 16)
                            nc.gpsimd.indirect_dma_start(out=sorted_meta[:, :], out_offset=place,
                                                         in_=meta[:, t, k, :], in_offset=None
                                                         ).then_inc(sent[c % 2], 16)
                for r in range(2):
                    pool.wait_ge(sent[r], 16 * SENDS * (NC // 2))

            @block.scalar
            def _(act):
                def weights_hi(q):
                    W, n, _ = loads[q]
                    act.wait_ge(raw_loaded[q % RAWS], 16 * (q // RAWS + 1))
                    nc.scalar.activation(parts_of(W, n)[0], raw[:, q % RAWS, :], ACT.Copy).then_inc(w_hi, 1)

                def tokens_hi(c):
                    for k in range(KD):
                        n = KD * c + k
                        act.wait_ge(t_done, n + 1)
                        if c >= 2 and k == 0:
                            act.wait_ge(up_done, 2 * U * (c - 1))
                        nc.scalar.activation(T[0][:, c % 2, k, :], Tps[:, n % 2, :], ACT.Copy).then_inc(t_hi, 1)

                tokens_hi(0)
                for q in range(3):
                    weights_hi(q)
                act.wait_ge(biases, 48)
                for c in range(NC):
                    for u in range(U):
                        n = c * U + u
                        e, m = divmod(u, HM)
                        act.wait_ge(up_done, 2 * n + 1)
                        if n >= 2:
                            act.wait_ge(hid_done, n - 1)
                        nc.scalar.activation(gate[:, n % 2, :], up[:, n % 2, 0, :], ACT.Silu,
                                             bias=B1[:, e, m:m + 1]).then_inc(gate_done, 1)
                        if c == 0 and u == 0:
                            for q in range(3, len(loads)):
                                weights_hi(q)
                        act.wait_ge(hid_done, n + 1)
                        if c and u == 0:
                            act.wait_ge(acc_done, 4 * c)
                        nc.scalar.activation(hT[0][:, u, :], hidden[:, n % 2, :], ACT.Copy).then_inc(hid_hi, 1)
                        if u == U // 2 and c + 1 < NC:
                            tokens_hi(c + 1)
                    if c:
                        act.wait_ge(acc_free, 4 * c)
                        act.dma_start(view(dst)[:, 4 * c - 4:4 * c, :], base[:, (c - 1) % 2, :, :]
                                      ).then_inc(stored[(c - 1) % 2], 16)
                act.wait_ge(acc_free, 4 * NC)
                act.dma_start(view(dst)[:, 4 * NC - 4:4 * NC, :], base[:, (NC - 1) % 2, :, :]
                              ).then_inc(stored[(NC - 1) % 2], 16)
                for r in range(2):
                    act.wait_ge(stored[r], 16 * (NC // 2))

            @block.vector
            def _(dve):
                def weights_lo(q):
                    W, n, _ = loads[q]
                    hi, lo = parts_of(W, n)
                    dve.wait_ge(w_hi, q + 1)
                    nc.vector.tensor_tensor(lo, raw[:, q % RAWS, :], hi.bitcast(FP32), ALU.subtract).then_inc(w_lo, 1)

                def tokens_lo(c):
                    for k in range(KD):
                        n = KD * c + k
                        dve.wait_ge(t_hi, n + 1)
                        nc.vector.tensor_tensor(T[1][:, c % 2, k, :], Tps[:, n % 2, :],
                                                T[0][:, c % 2, k, :].bitcast(FP32), ALU.subtract).then_inc(t_lo, 1)

                def results(c):
                    for j in range(4):
                        n = 4 * c + j
                        dve.wait_ge(acc_done, n + 1)
                        if j == 0:
                            dve.wait_ge(base_ready, c + 1)
                        slot = base[:, c % 2, j, :]
                        nc.vector.scalar_tensor_tensor(slot, acc[:, n % 2, 0:D], 1.0 / n_sh, slot, ALU.mult, ALU.add
                                                       ).then_inc(acc_free, 1)

                tokens_lo(0)
                for q in range(3):
                    weights_lo(q)
                dve.wait_ge(biases, 48)
                for c in range(NC):
                    for u in range(U):
                        n = c * U + u
                        e, m = divmod(u, HM)
                        if c == 0 and u == 1:
                            for q in range(3, len(loads)):
                                weights_lo(q)
                        dve.wait_ge(gate_done, n + 1)
                        dve.wait_ge(up_done, 2 * n + 2)
                        if n >= 2:
                            dve.wait_ge(hid_lo, n - 1)
                        nc.vector.scalar_tensor_tensor(hidden[:, n % 2, :], up[:, n % 2, 1, :], B2[:, e, m:m + 1],
                                                       gate[:, n % 2, :], ALU.add, ALU.mult).then_inc(hid_done, 1)
                        dve.wait_ge(hid_hi, n + 1)
                        nc.vector.tensor_tensor(hT[1][:, u, :], hidden[:, n % 2, :], hT[0][:, u, :].bitcast(FP32),
                                                ALU.subtract).then_inc(hid_lo, 1)
                        if u == U // 2 and c + 1 < NC:
                            tokens_lo(c + 1)
                    results(c)

            @block.tensor
            def _(pe):
                def tokens(c):
                    pe.wait_ge(rows_loaded[c % 2], 16 * (c // 2 + 1))
                    for k in range(KD):
                        n = KD * c + k
                        if n >= 2:
                            pe.wait_ge(t_lo, n - 1)
                        for j in range(4):
                            last = nc.tensor.transpose(Tps[:, n % 2, P * j:P * j + P],
                                                       rows[:, c % 2, j, P * k:P * k + P], chip.ident[:])
                        last.then_inc(t_done, 1)

                def down(c):
                    for j in range(4):
                        n = 4 * c + j
                        if n >= 2:
                            pe.wait_ge(acc_free, n - 1)
                        for u in range(U):
                            if j == 0:
                                pe.wait_ge(hid_lo, c * U + u + 1)
                            last = three_pass(nc, acc[:, n % 2, 0:D], [p[:, u, P * j:P * j + P] for p in hT],
                                              [p[:, u // HM, u % HM, :] for p in W3], u == 0, u == U - 1)
                        last.then_inc(acc_done, 1)

                tokens(0)
                for c in range(NC):
                    pe.wait_ge(t_lo, KD * (c + 1))
                    for u in range(U):
                        n = c * U + u
                        e, m = divmod(u, HM)
                        if n >= 2:
                            pe.wait_ge(hid_done, n - 1)
                        for half, W in enumerate((W1, W2)):
                            if c == 0 and m == 0:
                                pe.wait_ge(w_lo, 3 * e + half + 1)
                            for k in range(KD):
                                last = three_pass(nc, up[:, n % 2, half, :], [p[:, e, k, P * m:P * m + P] for p in W],
                                                  [p[:, c % 2, k, :] for p in T], k == 0, k == KD - 1)
                            last.then_inc(up_done, 1)
                        if u == U // 2 and c + 1 < NC:
                            tokens(c + 1)
                    if c == 0:
                        pe.wait_ge(w_lo, len(loads))
                    down(c)

        for s in [*raw_loaded, *rows_loaded, *base_loaded, *stored, *sent, prefetched, filled, *every]:
            nc.sync.sem_clear(s)
    nc.all_engine_barrier()


def routed_buffers(chip, stack, w1, w3):
    E, D, H = w1.shape
    sb = lambda n, s, d: stack.enter_context(chip.nc.sbuf_tensor(f"r_{n}", s, d))
    return sb("w1l", [P, E, D // P, H], FR), sb("w3", [P, E, H // P, D], FP32)


def routed_stage(chip, sorted_dram, sorted_meta, W1_raw, w2, W3, b1, b2, b3, tile_expert, tile_rows, dst,
                 background=()):
    nc, D, KD = chip.nc, chip.D, chip.KD
    E, _, H = w2.shape
    HM = H // P
    TILES = tile_expert.shape[1]
    WB = 2 * H + D
    with ExitStack() as st:
        sb = lambda n, s, d=FP32: st.enter_context(nc.sbuf_tensor(f"r_{n}", s, d))
        pb = lambda n, s: st.enter_context(nc.psum_tensor(f"r_{n}", s, FP32))
        W1 = [sb("w1h", [P, E, KD, H], FR), W1_raw]
        W2 = [sb(f"w2{p}", [P, E, KD, H], FR) for p in "hl"]
        b_hi = sb("b_hi", [64, WB], FR)[:]
        brows = sb("brows", [64, WB], FR)
        ones = sb("ones", [64, P])
        sel = sb("sel", [64, 2, P], FR)
        rows, out, row_meta = sb("rows", [P, 2, D]), sb("out", [P, 2, D]), sb("row_meta", [P, 2, 2])
        T = [sb(f"T{p}", [P, 2, KD, P], FR) for p in "hl"]
        gate_hidden, hT = sb("gate_hidden", [P, 4, H]), sb("hT", [P, 2, HM, P])
        gate, hidden = gate_hidden[:, 0:2, :], gate_hidden[:, 2:4, :]
        raw_b = gate_hidden[0:64, :, :].rearrange("p a h -> p (a h)")[:, 0:WB]
        up, Tps, Gps, acc = (pb("up", [P, 2, 2, H]), pb("Tps", [P, KD, P]), pb("Gps", [P, HM, P]),
                             pb("acc", [P, 2, 512]))
        rows_loaded = chip.sems(st, "r_rows_loaded0", "r_rows_loaded1")
        meta_loaded = chip.sems(st, "r_meta_loaded0", "r_meta_loaded1")
        w2_loaded = chip.sems(st, *[f"r_w2_loaded{e}" for e in range(E)])
        (added,) = chip.pool_sems("r_added")
        (b_loaded, w_hi, w_lo, b_zero, b_split, sel_ready, t_done, t_hi, t_lo, up_done, gate_done,
         hid_done, g_done, g_copied, acc_done, out_ready, handed) = every = chip.sems(
            st, *[f"r_{n}" for n in ("b_loaded", "w_hi", "w_lo", "b_zero", "b_split", "sel_ready",
                                     "t_done", "t_hi", "t_lo", "up_done", "gate_done", "hid_done", "g_done",
                                     "g_copied", "acc_done", "out_ready", "handed")])
        splits = [(W, e) for e in range(E) for W in (W1, W2)]
        flat = lambda a: a.rearrange("p k h -> p (k h)")

        def pairs(engine, body):
            for j in range(2):
                body(j, j, True, False)
            with engine.Fori(1, TILES // 2 - 1) as i:
                for j in range(2):
                    body(2 * i + j, j, False, False)
            for j in range(2):
                body(TILES - 2 + j, j, False, j == 1)

        with nc.Block() as block:

            @block.sync
            def _(sp):
                sp.wait_ge(b_zero, 2)
                for half in range(2):
                    for col, b in ((0, b1), (H, b2), (2 * H, b3)):
                        sp.dma_start(raw_b[32 * half:32 * half + E, col:col + b.shape[1]], b).then_inc(b_loaded, 16)
                for e in range(E):
                    sp.dma_start(W2[1][:, e, :, :].bitcast(FP32), w2[e].rearrange("(k p) h -> p k h", p=P)
                                 ).then_inc(w2_loaded[e], 16)
                for into, src, sem in background:
                    sp.dma_start(into, src).then_inc(sem, 16)

                def load_rows(n, j):
                    sp.dma_start(rows[:, j, :], sorted_dram[bass.ds(n * P, P), :]).then_inc(rows_loaded[j], 16)

                def body(n, j, first, last):
                    if not last:
                        if not (first and j == 0):
                            sp.wait_ge(t_done, n)
                        load_rows(n + 1, 1 - j)
                    if not first:
                        sp.wait_ge(added, 16 * (n - 1))
                    sp.dma_start(row_meta[:, j, :], sorted_meta[bass.ds(n * P, P), :]).then_inc(meta_loaded[j], 16)

                load_rows(0, 0)
                pairs(sp, body)

            @block.gpsimd
            def _(pool):
                nc.gpsimd.memset(ones[:], 1.0).then_inc(b_zero, 1)
                nc.gpsimd.memset(raw_b, 0.0).then_inc(b_zero, 1)

                def body(n, j, first, last):
                    pool.wait_ge(out_ready, n + 1)
                    if not (first and j == 0):
                        pool.wait_ge(added, 16 * n)
                    pool.sem_inc(handed, 1)
                    nc.gpsimd.indirect_dma_start(
                        out=dst[:, :], out_offset=bass.IndirectOffsetOnAxis(ap=row_meta[:, j, 0:1].bitcast(I32), axis=0),
                        in_=out[:, j, :], in_offset=None, compute_op=ALU.add).then_inc(added, 16)

                pairs(pool, body)
                pool.wait_ge(added, 16 * TILES)

            @block.scalar
            def _(act):
                act.wait_ge(b_loaded, 96)
                nc.scalar.activation(b_hi, raw_b, ACT.Copy).then_inc(b_split, 1)
                for W, e in splits:
                    if W is W2:
                        act.wait_ge(w2_loaded[e], 16)
                    nc.scalar.activation(flat(W[0][:, e, :, :]), flat(W[1][:, e, :, :]).bitcast(FP32), ACT.Copy
                                         ).then_inc(w_hi, 1)

                def tokens_hi(n, j, first):
                    act.wait_ge(t_done, n + 1)
                    if not first:
                        act.wait_ge(up_done, 2 * n - 2)
                    nc.scalar.activation(T[0][:, j, :, :], Tps[:], ACT.Copy).then_inc(t_hi, 1)

                def body(n, j, first, last):
                    act.wait_ge(up_done, 2 * n + 1)
                    if not first:
                        act.wait_ge(hid_done, n - 1)
                    nc.scalar.activation(gate[:, j, :], up[:, j, 0, :], ACT.Silu).then_inc(gate_done, 1)
                    if not (first and j == 0):
                        copied(n - 1, 1 - j, first)
                    if not last:
                        tokens_hi(n + 1, 1 - j, first and j == 0)

                def copied(n, j, first):
                    act.wait_ge(g_done, n + 1)
                    if not first:
                        act.wait_ge(acc_done, n - 1)
                    nc.scalar.activation(hT[:, j, :, :], Gps[:], ACT.Copy).then_inc(g_copied, 1)

                tokens_hi(0, 0, True)
                pairs(act, body)
                copied(TILES - 1, 1, False)

            @block.vector
            def _(dve):
                dve.wait_ge(b_split, 1)
                nc.vector.tensor_copy(brows[0:32, :], b_hi[0:32, :].bitcast(FP32)).then_inc(b_split, 1)
                nc.vector.tensor_tensor(brows[32:64, :], raw_b[32:64, :], b_hi[32:64, :].bitcast(FP32),
                                        ALU.subtract).then_inc(b_split, 1)
                for q, (W, e) in enumerate(splits):
                    dve.wait_ge(w_hi, q + 1)
                    hi, lo = (flat(part[:, e, :, :]) for part in W)
                    nc.vector.tensor_tensor(lo, lo.bitcast(FP32), hi.bitcast(FP32), ALU.subtract).then_inc(w_lo, 1)

                def select(n, j, first):
                    if not first:
                        dve.wait_ge(up_done, 2 * n - 2)
                    nc.vector.tensor_scalar(sel[:, j, :], ones[:], tile_rows[:, bass.ds(n, 1)], None, ALU.mult
                                            ).then_inc(sel_ready, 1)

                def tokens_lo(n, j):
                    dve.wait_ge(t_hi, n + 1)
                    nc.vector.tensor_tensor(T[1][:, j, :, :], Tps[:], T[0][:, j, :, :].bitcast(FP32), ALU.subtract
                                            ).then_inc(t_lo, 1)

                def output(n, j, first):
                    dve.wait_ge(acc_done, n + 1)
                    if not first:
                        dve.wait_ge(added, 16 * (n - 1))
                    dve.wait_ge(meta_loaded[j], 16 if first else 8 * (n - j) + 16)
                    nc.vector.tensor_scalar(out[:, j, :], acc[:, j, 0:D], row_meta[:, j, 1:2], None, ALU.mult
                                            ).then_inc(out_ready, 1)

                def body(n, j, first, last):
                    if not last:
                        select(n + 1, 1 - j, first and j == 0)
                        tokens_lo(n + 1, 1 - j)
                    dve.wait_ge(gate_done, n + 1)
                    dve.wait_ge(up_done, 2 * n + 2)
                    if not first:
                        dve.wait_ge(g_done, n - 1)
                    nc.vector.tensor_tensor(hidden[:, j, :], up[:, j, 1, :], gate[:, j, :], ALU.mult
                                            ).then_inc(hid_done, 1)
                    if not (first and j == 0):
                        output(n - 1, 1 - j, first)

                dve.wait_ge(b_zero, 2)
                select(0, 0, True)
                tokens_lo(0, 0)
                pairs(dve, body)
                output(TILES - 1, 1, False)

            @block.tensor
            def _(pe):
                def tokens(n, j, loaded):
                    pe.wait_ge(rows_loaded[j], loaded)
                    for k in range(KD):
                        last = nc.tensor.transpose(Tps[:, k, :], rows[:, j, P * k:P * k + P], chip.ident[:])
                    last.then_inc(t_done, 1)

                def turned(n, j, first):
                    pe.wait_ge(hid_done, n + 1)
                    if not (first and j == 0):
                        pe.wait_ge(g_copied, n)
                    for k in range(HM):
                        last = nc.tensor.transpose(Gps[:, k, :], hidden[:, j, P * k:P * k + P], chip.ident[:])
                    last.then_inc(g_done, 1)

                def down(n, j, first):
                    expert = expert_of(n)
                    pe.wait_ge(g_copied, n + 1)
                    for k in range(HM):
                        last = nc.tensor.matmul(acc[:, j, 0:D], hT[:, j, k, :], W3[:, bass.ds(expert, 1), k, :],
                                                start=False, stop=k == HM - 1)
                    last.then_inc(acc_done, 1)

                def expert_of(n):
                    return nc.tensor.value_load(tile_expert[0:1, bass.ds(n, 1)], min_val=0, max_val=E - 1)

                def body(n, j, first, last):
                    expert = expert_of(n)
                    pe.wait_ge(t_lo, n + 1)
                    pe.wait_ge(sel_ready, n + 1)
                    if not first:
                        pe.wait_ge(hid_done, n - 1)
                    for half, W in enumerate((W1, W2)):
                        bank = up[:, j, half, :]
                        nc.tensor.matmul(bank, sel[:, j, :], brows[:, half * H:half * H + H], start=True, stop=False)
                        for k in range(KD):
                            last_up = three_pass(nc, bank, [p[:, j, k, :] for p in T],
                                                 [p[:, bass.ds(expert, 1), k, :] for p in W], False, k == KD - 1)
                        if half == 0:
                            last_up.then_inc(up_done, 1)
                            if not (first and j == 0):
                                turned(n - 1, 1 - j, first)
                            if not last:
                                tokens(n + 1, 1 - j, 8 * (n + 1 - (1 - j)) + 16)
                            if not first:
                                pe.wait_ge(out_ready, n - 1)
                            nc.tensor.matmul(acc[:, j, 0:D], sel[:, j, :], brows[:, 2 * H:WB], start=True, stop=False)
                    last_up.then_inc(up_done, 1)
                    if not (first and j == 0):
                        down(n - 1, 1 - j, first)

                pe.wait_ge(w_lo, len(splits))
                pe.wait_ge(b_split, 3)
                tokens(0, 0, 16)
                pairs(pe, body)
                turned(TILES - 1, 1, False)
                down(TILES - 1, 1, False)

        for s in [*w2_loaded, *rows_loaded, *meta_loaded, added, *every]:
            nc.sync.sem_clear(s)
    nc.all_engine_barrier()


def rank_stage(chip, ranking, picked, row_index, picked_row, thresholds, limit, background=()):
    nc, NT, B, S = chip.nc, chip.NT, chip.B, chip.S
    NA = B * NT
    K = 2 * P
    RING = 4
    with ExitStack() as st:
        sb = lambda n, s, d=FP32: st.enter_context(nc.sbuf_tensor(f"k_{n}", s, d))
        index, rank_no = sb("index", [P, NA]), sb("rank_no", [P, K])
        index_r, w_hi, w_lo = (sb(n, [P, NA], FR) for n in ("index_r", "w_hi", "w_lo"))
        hot = sb("hot", [P, RING, K], FR)
        both = sb("both", [P, 2, 2, P])
        clamped = sb("clamped", [P, B, 2])
        rows_ps = st.enter_context(nc.psum_tensor("k_rows_ps", [P, B, 2, 512], FP32))
        made, chain, hot_ready, hot_used = every = chip.sems(
            st, *[f"k_{n}" for n in ("made", "chain", "hot_ready", "hot_used")])

        with nc.Block() as block:

            @block.sync
            def _(sp):
                for into, src, sem in background:
                    sp.dma_start(into, src).then_inc(sem, 16)

            @block.gpsimd
            def _(pool):
                g = nc.gpsimd
                g.iota(rank_no[:], pattern=[[1, K]], base=0, channel_multiplier=0,
                       allow_small_or_imprecise_dtypes=True).then_inc(made, 1)
                g.iota(index[:], pattern=[[0, B], [P, NT]], base=0, channel_multiplier=1,
                       allow_small_or_imprecise_dtypes=True).then_inc(made, 1)

            @block.vector
            def _(dve):
                V = nc.vector
                links = [0]

                def link(ins):
                    links[0] += 1
                    ins.then_inc(chain, 1)
                    dve.wait_ge(chain, links[0])

                dve.wait_ge(made, 2)
                link(V.tensor_copy(index_r[:], index[:]))
                link(V.tensor_copy(w_hi[:], ranking.weights[:]))
                link(V.tensor_tensor(w_lo[:], ranking.weights[:], w_hi[:].bitcast(FP32), ALU.subtract))
                for t in range(NA):
                    if t >= RING:
                        dve.wait_ge(hot_used, t - RING + 1)
                    V.tensor_scalar(hot[:, t % RING, :], rank_no[:], ranking.rank[:, t:t + 1], None, ALU.is_equal
                                    ).then_inc(hot_ready, 1)
                for b in range(B):
                    dve.wait_ge(hot_used, NT * (b + 1))
                    index_row, weight_row = rows_ps[:, b, 0, 0:K], rows_ps[:, b, 1, 0:K]
                    V.tensor_scalar_min(picked_row[:, b, :], index_row, float(limit))
                    V.tensor_copy(thresholds[:, b:b + 1], weight_row[:, K - 1:K])
                    for which, values in enumerate((index_row, weight_row)):
                        ins = V.tensor_tensor(both[:, :, which, :], values.rearrange("p (h j) -> p h j", h=2),
                                              chip.ident[:].rearrange("p (o j) -> p o j", o=1).to_broadcast([P, 2, P]),
                                              ALU.mult)
                    link(ins)
                    link(V.tensor_reduce(picked[:, b, :, :], both[:], AX.X, ALU.add))
                    link(V.tensor_scalar_add(row_index[:, b, :, 0], picked[:, b, :, 0], float(b * S)))
                    link(V.tensor_scalar(clamped[:, b, :], picked[:, b, :, 0], float(limit), float(b * (limit + 1)),
                                         ALU.min, ALU.add))
                    link(V.tensor_copy(row_index[:, b, :, 1], clamped[:, b, :]))

            @block.tensor
            def _(pe):
                pe.wait_ge(chain, 3)
                same = lambda column: column.to_broadcast([P, P])
                for t in range(NA):
                    b, i = divmod(t, NT)
                    pe.wait_ge(hot_ready, t + 1)
                    moving = hot[:, t % RING, :]
                    nc.tensor.matmul(rows_ps[:, b, 0, 0:K], same(index_r[:, t:t + 1]), moving, start=i == 0,
                                     stop=i == NT - 1)
                    nc.tensor.matmul(rows_ps[:, b, 1, 0:K], same(w_lo[:, t:t + 1]), moving, start=i == 0, stop=False)
                    nc.tensor.matmul(rows_ps[:, b, 1, 0:K], same(w_hi[:, t:t + 1]), moving, start=False,
                                     stop=i == NT - 1).then_inc(hot_used, 1)

        for s in every:
            nc.sync.sem_clear(s)
    nc.all_engine_barrier()


def newton_rsqrt(nc, link, r, std, v, tmp):
    V = nc.vector
    link(V.reciprocal(r, std))
    link(V.tensor_tensor(tmp, r, r, ALU.mult))
    link(V.tensor_tensor(tmp, tmp, v, ALU.mult))
    link(V.tensor_scalar(tmp, tmp, -0.5, 1.5, ALU.mult, ALU.add))
    link(V.tensor_tensor(r, r, tmp, ALU.mult))


def picked_stage(chip, xn_dram, positions, mask, row_index, picked_row, picked, thresholds, inverse, ln1, ln2, w, w_ffn,
                 out_dram, HEADS):
    nc, B, D, KD = chip.nc, chip.B, chip.D, chip.KD
    G = 2 * B
    hd = D // HEADS
    HALF = hd // 2
    PAD = 32
    HG = P // PAD
    NH = HEADS // HG
    M = mask.shape[1]
    MT = M // P
    F = w_ffn["w1"][0].shape[2]
    FM = F // P
    TWO_PI = 6.283185307179586
    C1 = 6.28125
    C2 = round((TWO_PI - C1) * 2 ** 20) / 2 ** 20
    C3 = TWO_PI - C1 - C2
    PI_BELOW = 3.1415925
    LATE = 5

    with ExitStack() as outer:
        osb = lambda n, s, d=FP32: outer.enter_context(nc.sbuf_tensor(f"p_{n}", s, d))
        xs = osb("xs", [P, G, D])
        heads_T = {n: osb(f"{n}T", [P, G, NH, P]) for n in "qk"}
        vals = osb("vals", [P, G, D])
        msel = osb("msel", [P, G, 2 * P])
        oT = [osb(f"oT{p}", [P, NH, G * P], FR) for p in "hl"]
        small = lambda n: osb(n, [P, G])
        ss, vv, std, rr, tmp = (small(n) for n in ("ss", "vv", "std", "rr", "tmp"))

        with ExitStack() as st:
            sb = lambda n, s, d=FP32: st.enter_context(nc.sbuf_tensor(f"p_{n}", s, d))
            pb = lambda n, s: st.enter_context(nc.psum_tensor(f"p_{n}", s, FP32))
            pos, posf = sb("pos", [P, G], I32), sb("posf", [P, G])
            rows = sb("mask_rows", [P, 2, M])
            rowsT = sb("mask_rowsT", [P, MT, P])
            col_no = sb("col_no", [P, MT])
            hot = sb("col_hot", [P, MT, 2 * P])
            inv, ang, turns_i, turns = (sb("inv", [P, HALF]), sb("ang", [P, G, HALF]), sb("turns_i", [P, G, HALF], I32),
                                        sb("turns", [P, G, HALF]))
            ang2 = sb("ang2", [P, G, HALF])
            sin, cos = sb("sin", [P, G, HALF]), sb("cos", [P, G, HALF])
            sq, hn = sb("sq", [P, D]), sb("hn", [P, G, D])
            hT = [sb(f"hT{p}", [P, KD, G * P], FR) for p in "hl"]
            padded = sb("padded", [P, 2, HEADS, PAD])
            rot = [sb(f"rot{i}", [P, HEADS, HALF]) for i in range(2)]
            Tps, qkv = pb("Tps", [P, 2, 512]), pb("qkv", [P, 2, 512])
            Hps = pb("Hps", [P, 512])
            Mps, Sps = pb("Mps", [P, 2, 512]), pb("Sps", [P, 2 * P])
            m_loaded = chip.pool_sems("p_m_loaded0", "p_m_loaded1")
            x_loaded, p_loaded = chip.pool_sems("p_x_loaded", "p_p_loaded")
            (inv_loaded, made, chain, sq_done, v_ready, std_ready, hn_ready, t_done, t_hi, t_lo,
             qkv_done, qkv_read, pad_ready, ht_done, ht_copied, ang_ready, trig_ready, hot_ready, m_done, m_copied,
             s_done, s_copied) = every = chip.sems(
                st, *[f"p_{n}" for n in (
                    "inv_loaded", "made", "chain", "sq_done", "v_ready", "std_ready",
                    "hn_ready", "t_done", "t_hi", "t_lo", "qkv_done", "qkv_read", "pad_ready", "ht_done", "ht_copied",
                    "ang_ready", "trig_ready", "hot_ready", "m_done", "m_copied", "s_done", "s_copied")])
            offset = lambda g, which: bass.IndirectOffsetOnAxis(ap=row_index[:, g // 2, g % 2, which:which + 1], axis=0)

            value_bank = lambda g: Tps[:, g % 2, D:2 * D]

            with nc.Block() as block:

                @block.sync
                def _(sp):
                    sp.dma_start(inv[:], inverse.to_broadcast([P, HALF])).then_inc(inv_loaded, 16)

                @block.gpsimd
                def _(pool):
                    g_ = nc.gpsimd
                    for g in range(G):
                        g_.indirect_dma_start(out=xs[:, g, :], out_offset=None, in_=xn_dram[:, :],
                                              in_offset=offset(g, 0)).then_inc(x_loaded, 16)
                    for g in range(G):
                        g_.indirect_dma_start(out=pos[:, g:g + 1], out_offset=None, in_=positions[:, :],
                                              in_offset=offset(g, 1)).then_inc(p_loaded, 16)
                    g_.iota(col_no[:], pattern=[[P, MT]], base=0, channel_multiplier=1,
                            allow_small_or_imprecise_dtypes=True).then_inc(made, 1)
                    g_.memset(padded[:], 0.0).then_inc(made, 1)
                    for g in range(G):
                        if g >= 2:
                            pool.wait_ge(m_done, 2 * (g - 1))
                        g_.indirect_dma_start(out=rows[:, g % 2, :], out_offset=None, in_=mask[:, :],
                                              in_offset=offset(g, 1)).then_inc(m_loaded[g % 2], 16)

                @block.scalar
                def _(act):
                    act.wait_ge(x_loaded, 16 * G)
                    for g in range(G):
                        if g:
                            act.wait_ge(sq_done, g)
                        nc.scalar.activation(sq[:], xs[:, g, :], ACT.Square, accum_out=ss[:, g:g + 1]
                                             ).then_inc(sq_done, 1)
                    act.wait_ge(v_ready, 1)
                    nc.scalar.activation(std[:], vv[:], ACT.Sqrt).then_inc(std_ready, 1)
                    for g in range(G):
                        act.wait_ge(t_done, g + 1)
                        for k in range(KD):
                            nc.scalar.activation(hT[0][:, k, P * g:P * g + P], Tps[:, g % 2, P * k:P * k + P], ACT.Copy,
                                                 scale=ln1[:, k:k + 1]).then_inc(t_hi, 1)
                    act.wait_ge(ang_ready, 1)
                    nc.scalar.activation(sin[:], ang[:], ACT.Sin).then_inc(trig_ready, 1)
                    nc.scalar.activation(cos[:], ang2[:], ACT.Sin).then_inc(trig_ready, 1)
                    n = 0
                    for g in range(G):
                        act.wait_ge(qkv_done, 3 * g + 3)
                        nc.scalar.activation(vals[:, g, :], value_bank(g), ACT.Copy
                                             ).then_inc(qkv_read, 1)
                        for i, name in enumerate("qk"):
                            n += 1
                            act.wait_ge(ht_done, n)
                            nc.scalar.activation(heads_T[name][:, g, :, :], Hps[:].rearrange("p (a q) -> p a q", a=NH),
                                                 ACT.Copy).then_inc(ht_copied, 1)

                @block.vector
                def _(dve):
                    V = nc.vector
                    links = [0]

                    def link(ins):
                        links[0] += 1
                        ins.then_inc(chain, 1)
                        dve.wait_ge(chain, links[0])

                    dve.wait_ge(sq_done, G)
                    link(V.tensor_scalar(vv[:], ss[:], 1.0 / D, 1e-6, ALU.mult, ALU.add))
                    V.tensor_copy(tmp[:], vv[:]).then_inc(v_ready, 1)
                    dve.wait_ge(std_ready, 1)
                    newton_rsqrt(nc, link, rr[:], std[:], vv[:], tmp[:])
                    for g in range(G):
                        V.tensor_scalar(hn[:, g, :], xs[:, g, :], rr[:, g:g + 1], None, ALU.mult).then_inc(hn_ready, 1)
                    dve.wait_ge(p_loaded, 16 * G)
                    dve.wait_ge(inv_loaded, 16)
                    link(V.tensor_copy(posf[:], pos[:]))
                    wide = lambda a: a.rearrange("p (g o) -> p g o", o=1).to_broadcast([P, G, HALF])
                    link(V.tensor_tensor(ang[:], wide(posf[:]),
                                         inv[:].rearrange("p (o h) -> p o h", o=1).to_broadcast([P, G, HALF]), ALU.mult))
                    flat = lambda a: a[:].rearrange("p g h -> p (g h)")
                    link(V.tensor_scalar(flat(turns_i), flat(ang), 1.0 / TWO_PI, None, ALU.mult))
                    link(V.tensor_copy(turns[:], turns_i[:]))
                    for c in (C1, C2, C3):
                        link(V.scalar_tensor_tensor(flat(ang), flat(turns), -c, flat(ang), ALU.mult, ALU.add))
                    link(V.tensor_scalar_add(flat(ang2), flat(ang), TWO_PI / 4))
                    link(V.tensor_scalar(flat(turns), flat(ang2), TWO_PI / 2, -TWO_PI, ALU.is_gt, ALU.mult))
                    link(V.tensor_tensor(flat(ang2), flat(ang2), flat(turns), ALU.add))
                    for a in (ang, ang2):
                        link(V.tensor_scalar(flat(a), flat(a), PI_BELOW, -PI_BELOW, ALU.min, ALU.max))
                    V.tensor_copy(flat(turns), flat(ang2)).then_inc(ang_ready, 1)
                    for g in range(G):
                        for k in range(KD):
                            dve.wait_ge(t_hi, KD * (g + 1))
                            cols = slice(P * g, P * g + P)
                            V.scalar_tensor_tensor(hT[1][:, k, cols], Tps[:, g % 2, P * k:P * k + P], ln1[:, k:k + 1],
                                                   hT[0][:, k, cols].bitcast(FP32), ALU.mult, ALU.subtract
                                                   ).then_inc(t_lo, 1)
                    dve.wait_ge(trig_ready, 2)
                    dve.wait_ge(made, 2)
                    n = 0
                    for g in range(G):
                        bc = lambda a: a[:, g:g + 1, :].to_broadcast([P, HEADS, HALF])
                        for i, name in enumerate("qk"):
                            dve.wait_ge(qkv_done, 3 * g + i + 1)
                            t = qkv[:, i, 0:D].rearrange("p (h c) -> p h c", h=HEADS)
                            t1, t2 = t[:, :, 0:HALF], t[:, :, HALF:hd]
                            if n >= 2:
                                dve.wait_ge(ht_done, n - 1)
                            out = padded[:, i, :, :]
                            link(V.tensor_tensor(rot[0][:], t1, bc(cos), ALU.mult))
                            link(V.tensor_tensor(rot[1][:], t2, bc(sin), ALU.mult))
                            link(V.tensor_tensor(out[:, :, 0:HALF], rot[0][:], rot[1][:], ALU.subtract))
                            link(V.tensor_tensor(rot[0][:], t2, bc(cos), ALU.mult))
                            link(V.tensor_tensor(rot[1][:], t1, bc(sin), ALU.mult))
                            V.tensor_tensor(out[:, :, HALF:hd], rot[0][:], rot[1][:], ALU.add).then_inc(pad_ready, 1)
                            n += 1
                            dve.wait_ge(pad_ready, n)
                    for b in range(B):
                        if b:
                            dve.wait_ge(s_done, 2 * b)
                        for c in range(MT):
                            ins = V.tensor_scalar(hot[:, c, :], picked_row[:, b, :], col_no[:, c:c + 1], None,
                                                  ALU.is_equal)
                        ins.then_inc(hot_ready, 1)
                        for g in (2 * b, 2 * b + 1):
                            for h in range(2):
                                dve.wait_ge(m_done, 2 * g + h + 1)
                                if g and h == 0:
                                    dve.wait_ge(s_done, g)
                                V.tensor_copy(rowsT[:, 4 * h:4 * h + 4, :].rearrange("p a q -> p (a q)"), Mps[:, h, :]
                                              ).then_inc(m_copied, 1)
                            dve.wait_ge(s_done, g + 1)
                            link(V.tensor_copy(msel[:, g, :], Sps[:]))
                            V.memset(msel[:, g, 2 * P - 1:2 * P], MASKED).then_inc(s_copied, 1)

                @block.tensor
                def _(pe):
                    for g in range(G):
                        pe.wait_ge(hn_ready, g + 1)
                        if g >= 2:
                            pe.wait_ge(t_lo, KD * (g - 1))
                        for k in range(KD):
                            last = nc.tensor.transpose(Tps[:, g % 2, P * k:P * k + P], hn[:, g, P * k:P * k + P],
                                                       chip.ident[:])
                        last.then_inc(t_done, 1)
                    pe.wait_ge(t_lo, KD * G)
                    pe.wait_ge(made, 2)
                    n = 0
                    for g in range(G):
                        for i, name in enumerate(("wq", "wk", "wv")):
                            bank = qkv[:, i, 0:D] if i < 2 else value_bank(g)
                            if g and i < 2:
                                pe.wait_ge(pad_ready, 2 * g - 1 + i)
                            if g >= 2 and i == 2:
                                pe.wait_ge(qkv_read, g - 1)
                            for k in range(KD):
                                last = three_pass(nc, bank, [p[:, k, P * g:P * g + P] for p in hT],
                                                  [p[:, k, :] for p in w[name]], k == 0, k == KD - 1)
                            last.then_inc(qkv_done, 1)
                        for i in range(2):
                            pe.wait_ge(pad_ready, n + 1)
                            if n:
                                pe.wait_ge(ht_copied, n)
                            for a in range(NH):
                                src = padded[:, i, HG * a:HG * a + HG, :].rearrange("p h c -> p (h c)")
                                last = nc.tensor.transpose(Hps[:, P * a:P * a + P], src, chip.ident[:])
                            last.then_inc(ht_done, 1)
                            n += 1
                    for g in range(G):
                        pe.wait_ge(m_loaded[g % 2], 16 * (g // 2 + 1))
                        for h in range(2):
                            if g:
                                pe.wait_ge(m_copied, 2 * g - 1 + h)
                            for c in range(4):
                                last = nc.tensor.transpose(Mps[:, h, P * c:P * c + P],
                                                           rows[:, g % 2, P * (4 * h + c):P * (4 * h + c) + P],
                                                           chip.ident[:])
                            last.then_inc(m_done, 1)
                        pe.wait_ge(m_copied, 2 * g + 2)
                        pe.wait_ge(hot_ready, g // 2 + 1)
                        if g:
                            pe.wait_ge(s_copied, g)
                        for c in range(MT):
                            last = nc.tensor.matmul(Sps[:], rowsT[:, c, :], hot[:, c, :], start=c == 0, stop=c == MT - 1)
                        last.then_inc(s_done, 1)

            for s in [*m_loaded, x_loaded, p_loaded, *every]:
                nc.sync.sem_clear(s)
        nc.all_engine_barrier()

        with ExitStack() as st:
            sb = lambda n, s, d=FP32: st.enter_context(nc.sbuf_tensor(f"p_{n}", s, d))
            pb = lambda n, s: st.enter_context(nc.psum_tensor(f"p_{n}", s, FP32))
            RING = 4
            N = B * HEADS
            masked, probs = sb("masked", [P, RING, 2, 2 * P]), sb("probs", [P, RING, 2, 2 * P])
            neg_max, sums = sb("neg_max", [P, N, 2]), sb("sums", [P, N, 2])
            pT = sb("pT", [P, RING, 2, 2 * P])
            nothing = sb("nothing", [P, NH, G * P])
            S_ps, T_ps = pb("S_ps", [P, RING, 2, 2 * P]), pb("T_ps", [P, 2, 2, 2 * P])
            O_ps = pb("O_ps", [P, NH, 2 * P])
            (qk_done, masked_ready, max_done, exp_done, inv_ready, norm_done, pt_done, pt_copied, pv_done, zeroed,
             padded_o, o_hi, o_lo) = every = chip.sems(
                st, *[f"p_{n}" for n in ("qk_done", "masked_ready", "max_done", "exp_done", "inv_ready", "norm_done",
                                         "pt_done", "pt_copied", "pv_done", "zeroed", "padded_o", "o_hi", "o_lo")])
            place = lambda h: (h // HG, slice(PAD * (h % HG), PAD * (h % HG) + PAD))
            head_rows = [slice(PAD * r, PAD * r + hd) for r in range(HG)]

            with nc.Block() as block:

                @block.gpsimd
                def _(pool):
                    nc.gpsimd.memset(nothing[:], 0.0).then_inc(zeroed, 1)

                @block.tensor
                def _(pe):
                    def scores(pair):
                        for j in range(2):
                            for n in pair:
                                b, h = divmod(n, HEADS)
                                a, rows_ = place(h)
                                if n >= RING and j == 0:
                                    pe.wait_ge(masked_ready, n - RING + 1)
                                last = nc.tensor.matmul(S_ps[:, n % RING, j, :].rearrange("p (t k) -> p t k", t=2),
                                                        heads_T["q"][rows_, 2 * b + j, a, :],
                                                        heads_T["k"][rows_, 2 * b:2 * b + 2, a, :], start=True,
                                                        stop=True)
                                if j == 1:
                                    last.then_inc(qk_done, 1)

                    def transposes(n):
                        pe.wait_ge(norm_done, n + 1)
                        if n >= 2:
                            pe.wait_ge(pt_copied, n - 1)
                        for t in range(2):
                            for j in range(2):
                                last = nc.tensor.transpose(T_ps[:, n % 2, t, P * j:P * j + P],
                                                           probs[:, n % RING, j, P * t:P * t + P], chip.ident[:])
                        last.then_inc(pt_done, 1)

                    def values(pair):
                        pe.wait_ge(pt_copied, pair[-1] + 1)
                        b = pair[0] // HEADS
                        if b and pair[0] % HEADS == 0:
                            pe.wait_ge(o_lo, HG * b)
                        for t in range(2):
                            for n in pair:
                                h = n % HEADS
                                last = nc.tensor.matmul(O_ps[head_rows[h % HG], h // HG, :],
                                                        vals[:, 2 * b + t, hd * h:hd * h + hd],
                                                        pT[:, n % RING, t, :], start=t == 0, stop=t == 1)
                                if t == 1:
                                    last.then_inc(pv_done, 1)

                    for m in range(0, N + 6, 2):
                        if m < N:
                            scores((m, m + 1))
                        for n in (m - 3, m - 2):
                            if 0 <= n < N:
                                transposes(n)
                        if 0 <= m - 6 < N:
                            values((m - 6, m - 5))

                @block.vector
                def _(dve):
                    V = nc.vector

                    def normalise(n):
                        dve.wait_ge(exp_done, 2 * n + 2)
                        V.reciprocal(sums[:, n, :], sums[:, n, :]).then_inc(inv_ready, 1)
                        dve.wait_ge(inv_ready, n + 1)
                        V.tensor_tensor(probs[:, n % RING, :, :], probs[:, n % RING, :, :],
                                        sums[:, n, :].rearrange("p (j o) -> p j o", o=1).to_broadcast([P, 2, 2 * P]),
                                        ALU.mult).then_inc(norm_done, 1)

                    def results_lo(b):
                        for r, rows_ in enumerate(head_rows):
                            dve.wait_ge(o_hi, HG * b + HG)
                            cols = slice(2 * P * b, 2 * P * (b + 1))
                            V.tensor_tensor(oT[1][rows_, :, cols], O_ps[rows_, :, :],
                                            oT[0][rows_, :, cols].bitcast(FP32), ALU.subtract).then_inc(o_lo, 1)

                    dve.wait_ge(zeroed, 1)
                    for part in oT:
                        V.tensor_copy(part[:], nothing[:]).then_inc(padded_o, 1)
                    for n in range(N + 1):
                        if n < N:
                            b = n // HEADS
                            dve.wait_ge(qk_done, n + 1)
                            if n >= RING:
                                dve.wait_ge(exp_done, 2 * (n - RING) + 2)
                            V.tensor_tensor(masked[:, n % RING, :, :], S_ps[:, n % RING, :, :],
                                            msel[:, 2 * b:2 * b + 2, :], ALU.add).then_inc(masked_ready, 1)
                            dve.wait_ge(masked_ready, n + 1)
                            V.tensor_reduce(neg_max[:, n, :], masked[:, n % RING, :, :], AX.X, ALU.max,
                                            negate=True).then_inc(max_done, 1)
                        if n:
                            normalise(n - 1)
                        if n >= HEADS and (n - LATE) % HEADS == 0:
                            results_lo((n - LATE) // HEADS - 1)
                    results_lo(B - 1)

                @block.scalar
                def _(act):
                    def exponentials(n):
                        act.wait_ge(max_done, n + 1)
                        if n >= RING:
                            act.wait_ge(pt_done, n - RING + 1)
                        for j in range(2):
                            nc.scalar.activation(probs[:, n % RING, j, :], masked[:, n % RING, j, :], ACT.Exp,
                                                 bias=neg_max[:, n, j:j + 1], accum_out=sums[:, n, j:j + 1]
                                                 ).then_inc(exp_done, 1)

                    def copies(n):
                        act.wait_ge(pt_done, n + 1)
                        if n >= RING:
                            act.wait_ge(pv_done, n - RING + 1)
                        nc.scalar.activation(pT[:, n % RING, :, :], T_ps[:, n % 2, :, :], ACT.Copy).then_inc(pt_copied, 1)

                    def results_hi(b):
                        act.wait_ge(pv_done, HEADS * (b + 1))
                        act.wait_ge(padded_o, 2)
                        for rows_ in head_rows:
                            nc.scalar.activation(oT[0][rows_, :, 2 * P * b:2 * P * (b + 1)], O_ps[rows_, :, :],
                                                 ACT.Copy).then_inc(o_hi, 1)

                    for n in range(N + 2):
                        if n < N:
                            exponentials(n)
                        if n >= 2:
                            copies(n - 2)
                        if n >= HEADS and (n - LATE) % HEADS == 0:
                            results_hi((n - LATE) // HEADS - 1)
                    results_hi(B - 1)

            for s in every:
                nc.sync.sem_clear(s)
        nc.all_engine_barrier()

        with ExitStack() as st:
            sb = lambda n, s, d=FP32: st.enter_context(nc.sbuf_tensor(f"p_{n}", s, d))
            pb = lambda n, s: st.enter_context(nc.psum_tensor(f"p_{n}", s, FP32))
            fT = [sb(f"fT{p}", [P, KD, G * P], FR) for p in "hl"]
            x1, hn, sq = sb("x1", [P, G, D]), sb("hn2", [P, G, D]), sb("sq2", [P, D])
            gel = sb("gel", [P, 2, G * P])
            gT = [sb(f"gT{p}", [P, FM, G * P], FR) for p in "hl"]
            delta, sel = sb("delta", [P, G, D]), sb("sel", [P, G])
            Tps, acc, up = pb("Tps2", [P, 2, 512]), pb("acc2", [P, 2, 512]), pb("up2", [P, 2, 512])
            (t_done, t_hi, t_lo, wo_done, x1_ready, sq_done, v_ready, std_ready, hn_ready, up_done, gel_done, g_hi,
             g_lo, down_done, down_read, delta_ready, chain) = every = chip.sems(
                st, *[f"p3_{n}" for n in ("t_done", "t_hi", "t_lo", "wo_done", "x1_ready", "sq_done", "v_ready",
                                          "std_ready", "hn_ready", "up_done", "gel_done", "g_hi", "g_lo", "down_done",
                                          "down_read", "delta_ready", "chain")])
            (sent,) = chip.pool_sems("p3_sent")

            with nc.Block() as block:

                @block.tensor
                def _(pe):
                    def transposed(src, g, n):
                        if n >= 2:
                            pe.wait_ge(t_lo, KD * (n - 1))
                        for k in range(KD):
                            last = nc.tensor.transpose(Tps[:, n % 2, P * k:P * k + P], src[:, g, P * k:P * k + P],
                                                       chip.ident[:])
                        last.then_inc(t_done, 1)

                    for g in range(G):
                        if g >= 2:
                            pe.wait_ge(x1_ready, g - 1)
                        for a in range(NH):
                            last = three_pass(nc, acc[:, g % 2, 0:D], [p[:, a, P * g:P * g + P] for p in oT],
                                              [p[:, a, :] for p in w["wo"]], a == 0, a == NH - 1)
                        last.then_inc(wo_done, 1)
                    for g in range(G):
                        pe.wait_ge(hn_ready, g + 1)
                        transposed(hn, g, g)
                    pe.wait_ge(t_lo, KD * G)
                    for m in range(FM):
                        if m >= 2:
                            pe.wait_ge(gel_done, m - 1)
                        for k in range(KD):
                            last = three_pass(nc, up[:, m % 2, :], [p[:, k, P * m:P * m + P] for p in w_ffn["w1"]],
                                              [p[:, k, :] for p in fT], k == 0, k == KD - 1)
                        last.then_inc(up_done, 1)
                    for g in range(G):
                        pe.wait_ge(x1_ready, G)
                        if g >= 2:
                            pe.wait_ge(down_read, g - 1)
                        for m in range(FM):
                            if g == 0:
                                pe.wait_ge(g_lo, m + 1)
                            last = three_pass(nc, acc[:, g % 2, 0:D], [p[:, m, P * g:P * g + P] for p in gT],
                                              [p[:, m, :] for p in w_ffn["w2"]], m == 0, m == FM - 1)
                        last.then_inc(down_done, 1)

                @block.scalar
                def _(act):
                    def transposed_hi(out, n, g, scale):
                        act.wait_ge(t_done, n + 1)
                        for k in range(KD):
                            nc.scalar.activation(out[:, k, P * g:P * g + P], Tps[:, n % 2, P * k:P * k + P], ACT.Copy,
                                                 scale=scale[:, k:k + 1]).then_inc(t_hi, 1)

                    for g in range(G):
                        act.wait_ge(x1_ready, g + 1)
                        if g:
                            act.wait_ge(sq_done, g)
                        nc.scalar.activation(sq[:], x1[:, g, :], ACT.Square, accum_out=ss[:, g:g + 1]
                                             ).then_inc(sq_done, 1)
                    act.wait_ge(v_ready, 1)
                    nc.scalar.activation(std[:], vv[:], ACT.Sqrt).then_inc(std_ready, 1)
                    for g in range(G):
                        transposed_hi(fT[0], g, g, ln2)
                    for m in range(FM):
                        act.wait_ge(up_done, m + 1)
                        if m >= 2:
                            act.wait_ge(g_lo, m - 1)
                        nc.scalar.activation(gel[:, m % 2, :], up[:, m % 2, :], ACT.Gelu_apprx_tanh
                                             ).then_inc(gel_done, 1)
                        act.wait_ge(gel_done, m + 1)
                        nc.scalar.activation(gT[0][:, m, :], gel[:, m % 2, :], ACT.Copy).then_inc(g_hi, 1)

                @block.vector
                def _(dve):
                    V = nc.vector
                    links = [0]

                    def link(ins):
                        links[0] += 1
                        ins.then_inc(chain, 1)
                        dve.wait_ge(chain, links[0])

                    def transposed_lo(out, n, g, scale):
                        cols = slice(P * g, P * g + P)
                        for k in range(KD):
                            dve.wait_ge(t_hi, KD * (n + 1))
                            V.scalar_tensor_tensor(out[1][:, k, cols], Tps[:, n % 2, P * k:P * k + P],
                                                   scale[:, k:k + 1],
                                                   out[0][:, k, cols].bitcast(FP32), ALU.mult, ALU.subtract
                                                   ).then_inc(t_lo, 1)

                    for g in range(G):
                        dve.wait_ge(wo_done, g + 1)
                        V.tensor_tensor(x1[:, g, :], acc[:, g % 2, 0:D], xs[:, g, :], ALU.add).then_inc(x1_ready, 1)
                    dve.wait_ge(sq_done, G)
                    link(V.tensor_scalar(vv[:], ss[:], 1.0 / D, 1e-6, ALU.mult, ALU.add))
                    V.tensor_copy(tmp[:], vv[:]).then_inc(v_ready, 1)
                    dve.wait_ge(std_ready, 1)
                    newton_rsqrt(nc, link, rr[:], std[:], vv[:], tmp[:])
                    for g in range(G):
                        V.tensor_scalar(hn[:, g, :], x1[:, g, :], rr[:, g:g + 1], None, ALU.mult).then_inc(hn_ready, 1)
                    for b in range(B):
                        link(V.tensor_scalar(sel[:, 2 * b:2 * b + 2], picked[:, b, :, 1], thresholds[:, b:b + 1], -1.0,
                                             ALU.is_gt, ALU.mult))
                    for g in range(G):
                        link(V.tensor_scalar(delta[:, g, :], xs[:, g, :], sel[:, g:g + 1], None, ALU.mult))
                    for g in range(G):
                        transposed_lo(fT, g, g, ln2)
                    for m in range(FM):
                        dve.wait_ge(g_hi, m + 1)
                        V.tensor_tensor(gT[1][:, m, :], gel[:, m % 2, :], gT[0][:, m, :].bitcast(FP32), ALU.subtract
                                        ).then_inc(g_lo, 1)
                    for g in range(G):
                        dve.wait_ge(down_done, g + 1)
                        V.tensor_tensor(x1[:, g, :], acc[:, g % 2, 0:D], x1[:, g, :], ALU.add).then_inc(down_read, 1)
                        dve.wait_ge(down_read, g + 1)
                        V.scalar_tensor_tensor(delta[:, g, :], x1[:, g, :], picked[:, g // 2, g % 2, 1:2],
                                               delta[:, g, :], ALU.mult, ALU.add).then_inc(delta_ready, 1)

                @block.gpsimd
                def _(pool):
                    for g in range(G):
                        pool.wait_ge(delta_ready, g + 1)
                        n = P if g % 2 == 0 else P - 1
                        nc.gpsimd.indirect_dma_start(
                            out=out_dram[:, :],
                            out_offset=bass.IndirectOffsetOnAxis(ap=row_index[0:n, g // 2, g % 2, 0:1], axis=0),
                            in_=delta[0:n, g, :], in_offset=None, compute_op=ALU.add).then_inc(sent, 16)
                    pool.wait_ge(sent, 16 * G)

            for s in [sent, *every]:
                nc.sync.sem_clear(s)
        nc.all_engine_barrier()


def load_small(chip, out, plan, scales={}, background=()):
    nc = chip.nc
    with ExitStack() as st:
        loaded, scaled = chip.sems(st, "small_loaded", "small_scaled")
        with nc.Block() as block:

            @block.sync
            def _(sp):
                for name, _, view in plan:
                    sp.dma_start(out[name][:], view).then_inc(loaded, 16)
                for into, src, sem in background:
                    sp.dma_start(into, src).then_inc(sem, 16)
                sp.wait_ge(loaded, 16 * len(plan))

            @block.vector
            def _(dve):
                dve.wait_ge(loaded, 16 * len(plan))
                for name, scale in scales.items():
                    nc.vector.tensor_scalar(out[name][:], out[name][:], scale, None, ALU.mult).then_inc(scaled, 1)
                dve.wait_ge(scaled, len(scales))

        nc.sync.sem_clear(loaded), nc.sync.sem_clear(scaled)
    nc.all_engine_barrier()
    return out


def fill_start(chip, stack, sorted_dram, sorted_meta, trash):
    nc = chip.nc
    TILES, D = sorted_dram.shape[0] // P, chip.D
    zeros = stack.enter_context(nc.sbuf_tensor("zeros", [P, 1, D], FP32))
    nobody = stack.enter_context(nc.sbuf_tensor("nobody", [P, TILES, 2], FP32))
    (filled,) = chip.sems(stack, "rows_filled")
    first_trash = trash.shape[0] - P
    with ExitStack() as st:
        made, zeroed = chip.sems(st, "fill_made", "fill_zeroed")
        with nc.Block() as block:

            @block.gpsimd
            def _(pool):
                nc.gpsimd.memset(nobody[:], 0.0).then_inc(zeroed, 1)
                nc.gpsimd.memset(zeros[:], 0.0).then_inc(made, 1)
                pool.wait_ge(zeroed, 1)
                nc.gpsimd.iota(nobody[:, :, 0].bitcast(I32), pattern=[[1, TILES]], base=0,
                               channel_multiplier=TILES).then_inc(made, 1)

            @block.vector
            def _(dve):
                dve.wait_ge(made, 2)
                rows = nobody[:, :, 0].bitcast(I32)
                nc.vector.tensor_single_scalar(rows, rows, P - 1, ALU.bitwise_and).then_inc(made, 1)
                dve.wait_ge(made, 3)
                nc.vector.tensor_single_scalar(rows, rows, float(first_trash), ALU.add).then_inc(made, 1)

            @block.sync
            def _(sp):
                sp.wait_ge(made, 4)
                sp.dma_start(sorted_meta.rearrange("(p t) m -> p t m", p=P), nobody[:]).then_inc(filled, 16)
                sp.dma_start(trash[first_trash:first_trash + P, :], zeros[:, 0, :]).then_inc(filled, 16)

        nc.sync.sem_clear(made), nc.sync.sem_clear(zeroed)
    nc.all_engine_barrier()
    part = lambda b: (sorted_dram.rearrange("(p t) d -> p t d", p=P)[:, bass.ds(b * (TILES // chip.B), TILES // chip.B), :],
                      zeros[:].to_broadcast([P, TILES // chip.B, D]))
    return filled, 16 * (2 + chip.B), part


def build(nc, a, out, B, S):
    N, D = a["x"].shape
    chip = Chip(nc, B, S, D)
    E = a["gate_b"].shape[1]
    HEADS = 16
    M = a["mask"].shape[1]
    TILES = 2 * N // P + E
    NA = N // P
    SCALE = float(D) ** -0.5
    HEAD_SCALE = float(D // HEADS) ** -0.5
    dram = lambda n, s: nc.dram_tensor(n, s, FP32, kind="Internal").ap()
    xn1, xn2, y1 = (dram(n, (N, D)) for n in ("xn1", "xn2", "y1"))
    y2 = dram("y2", (N + P, D))
    sorted_rows, sorted_meta = dram("sorted_rows", (TILES * P, D)), dram("sorted_meta", (TILES * P, 2))
    router_out = dram("router_out", (N,))
    wide = lambda v: v.to_broadcast([P, v.shape[1]])

    def token_buffers(st, tag):
        T = [st.enter_context(nc.sbuf_tensor(f"{tag}T_{p}", [P, chip.KD, S], FR)) for p in ("hi", "lo")]
        V = [st.enter_context(nc.sbuf_tensor(f"{tag}V_{p}", [P, chip.NT, D], FR)) for p in ("hi", "lo")]
        return T, V

    with ExitStack() as top:
        constants(chip, top)

        with ExitStack() as layer:
            sb = lambda n, s, d=FP32: layer.enter_context(nc.sbuf_tensor(n, s, d))
            plan = [("bq", [P, chip.KD], a["bq"]), ("bk", [P, chip.KD], a["bk"]), ("bv", [P, D], wide(a["bv"])),
                    ("gate_b", [P, E], wide(a["gate_b"])), ("router_b", [P, 1], wide(a["router_b"])),
                    ("ln1", [P, chip.KD], a["ln1"]), ("ln2", [P, chip.KD], a["ln2"])]
            small_tiles = {name: top.enter_context(nc.sbuf_tensor(f"c_{name}", shape, FP32)) for name, shape, _ in plan}
            logits, meta, slots = sb("logits", [P, NA, E]), sb("meta", [P, NA, 2, 2]), sb("slots", [P, NA, 2], I32)
            tile_expert, tile_rows = sb("tile_expert", [1, TILES], I32), sb("tile_rows", [64, TILES])
            with ExitStack() as st:
                weights = Weights(chip, st, [(n, a["a0_" + n]) for n in ("wv", "wq", "wk")], "l0_")
                small = load_small(chip, small_tiles, plan, {"bq": SCALE}, weights.loads)
                w = split_weights(chip, st, weights, {"wq": SCALE})
                fill = fill_start(chip, st, sorted_rows, sorted_meta, y2)
                T, V = token_buffers(st, "l0_")
                with nc.Fori(0, B) as b:
                    norm_stage(chip, b, "n0", a["x"], xn1, T, V, w, logits)
                    attention_stage(chip, b, "a0", T, V, w, {"q": small["bq"], "k": small["bk"]}, [a["x"]],
                                    small["bv"], y1, background=[(*fill[2](b), fill[0])])
            gating_stage(chip, logits, small["gate_b"], meta, slots, tile_expert, tile_rows, E, TILES)
            W1_raw, W3 = routed_buffers(chip, layer, a["rw1"], a["rw3"])
            prefetch = [[(W1_raw[:, e, :, :].bitcast(FP32), a["rw1"][e].rearrange("(k p) h -> p k h", p=P)),
                         (W3[:, e, :, :], a["rw3"][e].rearrange("(k p) d -> p k d", p=P))] for e in range(E)]
            shared_stage(chip, xn1, y1, a["sw1"], a["sb1"], a["sw2"], a["sb2"], a["sw3"], a["sb3"], slots, meta,
                         sorted_rows, sorted_meta, fill, prefetch, y2[0:N, :])
            routed_stage(chip, sorted_rows, sorted_meta, W1_raw, a["rw2"], W3, a["rb1"], a["rb2"], a["rb3"],
                         tile_expert, tile_rows, y2)

        with ExitStack() as layer:
            sb = lambda n, s, d=FP32: layer.enter_context(nc.sbuf_tensor(n, s, d))
            scores, picked = sb("router_scores", [P, NA, 2]), sb("picked", [P, B, 2, 2])
            ranking = Ranking(chip, layer, scores, small["router_b"], router_out)
            row_index, picked_row = sb("row_index", [P, B, 2, 2], I32), sb("picked_row", [P, B, 2 * P])
            thresholds = sb("thresholds", [P, B])
            with ExitStack() as st:
                named = [(n, a["a1_" + n]) for n in ("wv", "wq", "wk", "wo")]
                w = weight_parts(chip, st, named, "l1_")
                with ExitStack() as raw:
                    weights = Weights(chip, raw, named, "l1_")
                    split_weights(chip, raw, weights, {"wq": SCALE}, w, start=True)
                T, V = token_buffers(st, "l1_")
                with nc.Fori(0, B) as b:
                    norm_stage(chip, b, "n1", y2[0:N, :], xn2, T, V, w, scores)
                    attention_stage(chip, b, "a1", T, V, w, None, [y2[0:N, :], xn2], None, out, ranking)
            with ExitStack() as st:
                weights = Weights(chip, st, [(n, a["f1_" + n]) for n in ("wq", "wk", "wv", "wo", "w1", "w2")],
                                  "f1_")
                rank_stage(chip, ranking, picked, row_index, picked_row, thresholds, M - 1, weights.loads)
                w = split_weights(chip, st, weights, {"wq": HEAD_SCALE})
                picked_stage(chip, xn2, a["positions"], a["mask"], row_index, picked_row, picked, thresholds,
                             a["inverse"], small["ln1"], small["ln2"], w, w, out, HEADS)




def kernel(**inputs):
    import numpy as np
    import concourse.bacc as bacc
    from concourse.bass_utils import run_bass_kernel_spmd

    i = {name: np.asarray(v) for name, v in inputs.items()}
    B, S, D = i["L0_attn_x"].shape
    E, _, H = i["L0_ffn_rw1"].shape
    M = i["L1_ffn_attention_mask"].shape[-1]
    HEADS = 16
    HALF = D // HEADS // 2
    columns = lambda v: v.reshape(-1, P).T
    lay = {
        "x": i["L0_attn_x"].reshape(B * S, D),
        **{"a0_" + n.lower(): i["L0_attn_" + n].T for n in ("Wq", "Wk")},
        "a0_wv": np.concatenate([i["L0_attn_Wv"].T, i["L0_ffn_gate_w"]], axis=1),
        "bq": columns(i["L0_attn_bq"]), "bk": columns(i["L0_attn_bk"]), "bv": i["L0_attn_bv"][None],
        "gate_b": i["L0_ffn_gate_b"][None],
        **{n: i["L0_ffn_" + n] for n in ("rw1", "rw2", "rw3", "rb1", "rb2", "rb3", "sw1", "sw2", "sw3", "sb3")},
        **{n: i["L0_ffn_" + n].reshape(2, H // P, P).transpose(2, 0, 1) for n in ("sb1", "sb2")},
        **{"a1_" + n.lower(): i["L1_attn_" + n].T for n in ("Wq", "Wk", "Wo")},
        "a1_wv": np.concatenate([i["L1_attn_Wv"].T, i["L1_ffn_router_w"], np.zeros((D, 1), np.float32)], axis=1),
        "router_b": i["L1_ffn_router_b"][None],
        **{"f1_" + n: i["L1_ffn_" + n] for n in ("wq", "wk", "wv", "w1", "w2")},
        "f1_wo": np.concatenate([i["L1_ffn_wo"].reshape(HEADS, -1, D), np.zeros((HEADS, 32 - D // HEADS, D), np.float32)],
                                axis=1).reshape(HEADS * 32, D),
        "ln1": columns(i["L1_ffn_ln1"]), "ln2": columns(i["L1_ffn_ln2"]),
        "mask": i["L1_ffn_attention_mask"].reshape(-1, M), "positions": i["L1_ffn_position_ids"].reshape(-1, 1),
        "inverse": (1.0 / np.float32(10000.0) ** (np.arange(0, 2 * HALF, 2, dtype=np.float32) / (2 * HALF))
                    ).astype(np.float32)[None],
    }
    nc = bacc.Bacc("TRN2", target_bir_lowering=False, num_devices=1)
    arrays, args = {}, {}
    for name, v in lay.items():
        arrays[f"in_{name}"] = np.ascontiguousarray(v)
        args[name] = nc.dram_tensor(f"in_{name}", v.shape, mybir.dt.from_np(v.dtype), kind="ExternalInput").ap()
    out = nc.dram_tensor("out", (B * S, D), FP32, kind="ExternalOutput").ap()
    build(nc, args, out, B, S)
    r = run_bass_kernel_spmd(nc, [arrays], core_ids=[0])
    return r.results[0]["out"].reshape(B, S, D)
```
